# Optimizing a Trainium2 kernel written in Bass

```python
import numpy as np
import jax
import jax.numpy as jnp

def _softmax(x, axis=-1):
    return jax.nn.softmax(x, axis=axis)

def _gelu(x):
    return jax.nn.gelu(x, approximate=True)

def _silu(x):
    return jax.nn.silu(x)

def _sigmoid(x):
    return jax.nn.sigmoid(x)

def _layernorm(x, axis=-1, eps=1e-05):
    m = jnp.mean(x, axis=axis, keepdims=True)
    v = jnp.var(x, axis=axis, keepdims=True)
    return (x - m) / jnp.sqrt(v + eps)

def _scatter_add(tgt, idx, src, axis=0):
    return tgt.at[idx].add(src)

def _segment_sum(src, seg, n):
    return jax.ops.segment_sum(src, seg, n)
kernel_name = 'mk_adaln_d1_jaxref_r4_543b01'

def setup_inputs(seed: int=0):
    np.random.seed(seed)
    _w = jnp.asarray

    def _L0_attn_setup():
        import jax, jax.numpy as jnp
        import numpy as np
        B, L, D, DIN, S, R, K = (2, 256, 256, 512, 16, 64, 4)
        key = jax.random.key(seed)
        ks = jax.random.split(key, 8)
        f = lambda k, sh, sc: jax.random.normal(k, sh, jnp.float32) * sc
        return {'x': f(ks[0], (B, L, D), 1.0), 'norm_w': jnp.ones((D,), jnp.float32), 'W_in': f(ks[1], (D, 2 * DIN), D ** (-0.5)), 'conv_w': f(ks[2], (DIN, 1, K), 0.5), 'conv_b': jnp.zeros((DIN,), jnp.float32), 'W_x': f(ks[3], (DIN, R + 2 * S), DIN ** (-0.5)), 'W_dt': f(ks[4], (R, DIN), R ** (-0.5)), 'b_dt': f(ks[5], (DIN,), 0.1), 'A_log': jnp.log(jnp.broadcast_to(jnp.arange(1, S + 1, dtype=jnp.float32), (DIN, S))), 'D_skip': jnp.ones((DIN,), jnp.float32), 'W_out': f(ks[6], (DIN, D), DIN ** (-0.5))}
    _L0_attn_in = _L0_attn_setup()

    def _L0_ffn_setup():
        import jax, jax.numpy as jnp
        import numpy as np
        E, K, D, F = (8, 2, 256, 1024)
        EPS = 1e-06
        B, S = (2, 256)
        key = jax.random.key(seed)
        ks = jax.random.split(key, 6)
        s_in = 1.0 / np.sqrt(D)
        s_mid = 1.0 / np.sqrt(F)
        return {'x': jax.random.normal(ks[0], (B, S, D), dtype=jnp.float32), 'Wg': jax.random.normal(ks[1], (D, E), dtype=jnp.float32) * s_in, 'gamma': jnp.ones((E, D), dtype=jnp.float32), 'beta': jnp.zeros((E, D), dtype=jnp.float32), 'W1': jax.random.normal(ks[2], (E, D, F), dtype=jnp.float32) * s_in, 'b1': jnp.zeros((E, F), dtype=jnp.float32), 'W2': jax.random.normal(ks[3], (E, F, D), dtype=jnp.float32) * s_mid, 'b2': jnp.zeros((E, D), dtype=jnp.float32)}
    _L0_ffn_in = _L0_ffn_setup()
    _L0_c = _w((lambda *s: np.random.randn(*s).astype(np.float32) * 0.05)(8, 256))
    _L0_wmod = _w((lambda *s: np.random.randn(*s).astype(np.float32) * 0.05)(256, 6 * 256) * 256 ** (-0.5))
    _d = {'L0_attn_x': _L0_attn_in['x'], 'L0_attn_norm_w': _L0_attn_in['norm_w'], 'L0_attn_W_in': _L0_attn_in['W_in'], 'L0_attn_conv_w': _L0_attn_in['conv_w'], 'L0_attn_conv_b': _L0_attn_in['conv_b'], 'L0_attn_W_x': _L0_attn_in['W_x'], 'L0_attn_W_dt': _L0_attn_in['W_dt'], 'L0_attn_b_dt': _L0_attn_in['b_dt'], 'L0_attn_A_log': _L0_attn_in['A_log'], 'L0_attn_D_skip': _L0_attn_in['D_skip'], 'L0_attn_W_out': _L0_attn_in['W_out'], 'L0_ffn_Wg': _L0_ffn_in['Wg'], 'L0_ffn_gamma': _L0_ffn_in['gamma'], 'L0_ffn_beta': _L0_ffn_in['beta'], 'L0_ffn_W1': _L0_ffn_in['W1'], 'L0_ffn_b1': _L0_ffn_in['b1'], 'L0_ffn_W2': _L0_ffn_in['W2'], 'L0_ffn_b2': _L0_ffn_in['b2'], 'L0_c': _L0_c, 'L0_wmod': _L0_wmod}
    _x0 = _d['L0_attn_x']
    _d['L0_attn_x'] = jax.random.normal(jax.random.fold_in(jax.random.key(seed), 1), (8, 512, 256), dtype=_x0.dtype)
    del _x0
    return _d

def reference(L0_attn_x, L0_attn_norm_w, L0_attn_W_in, L0_attn_conv_w, L0_attn_conv_b, L0_attn_W_x, L0_attn_W_dt, L0_attn_b_dt, L0_attn_A_log, L0_attn_D_skip, L0_attn_W_out, L0_ffn_Wg, L0_ffn_gamma, L0_ffn_beta, L0_ffn_W1, L0_ffn_b1, L0_ffn_W2, L0_ffn_b2, L0_c, L0_wmod):

    def _L0_attn_ref(x, norm_w, W_in, conv_w, conv_b, W_x, W_dt, b_dt, A_log, D_skip, W_out):
        import jax, jax.numpy as jnp
        import numpy as np
        B, L, D, DIN, S, R, K = (2, 256, 256, 512, 16, 64, 4)
        eps = 1e-05
        xn = x * jax.lax.rsqrt(jnp.mean(x * x, axis=-1, keepdims=True) + eps) * norm_w
        xz = xn @ W_in
        xi, z = jnp.split(xz, 2, axis=-1)
        xt = jnp.transpose(xi, (0, 2, 1))
        xc = jax.lax.conv_general_dilated(xt, conv_w, (1,), [(K - 1, 0)], feature_group_count=DIN)
        xc = jnp.transpose(xc, (0, 2, 1)) + conv_b
        xc = jax.nn.silu(xc)
        xd = xc @ W_x
        dt, Bm, Cm = jnp.split(xd, [R, R + S], axis=-1)
        dt = jax.nn.softplus(dt @ W_dt + b_dt)
        A = -jnp.exp(A_log)
        dA = jnp.exp(dt[..., None] * A)
        dBu = (dt * xc)[..., None] * Bm[:, :, None, :]

        def comb(c1, c2):
            a1, b1 = c1
            a2, b2 = c2
            return (a1 * a2, a2 * b1 + b2)
        _, h = jax.lax.associative_scan(comb, (dA, dBu), axis=1)
        y = jnp.einsum('blds,bls->bld', h, Cm) + D_skip * xc
        y = y * jax.nn.silu(z)
        return x + y @ W_out

    def _L0_ffn_ref(x, Wg, gamma, beta, W1, b1, W2, b2):
        import jax, jax.numpy as jnp
        import numpy as np
        E, K, D, F = (8, 2, 256, 1024)
        EPS = 1e-06
        B, S = (2, 256)
        orig_shape = x.shape
        xf = x.reshape(-1, orig_shape[-1])
        scores = xf @ Wg
        w, idx = jax.lax.top_k(scores, K)
        w = jax.nn.softmax(w, axis=-1)
        mu = jnp.mean(xf, axis=-1, keepdims=True)
        var = jnp.var(xf, axis=-1, keepdims=True)
        xhat = (xf - mu) * jax.lax.rsqrt(var + EPS)
        normed = xhat[None, :, :] * gamma[:, None, :] + beta[:, None, :]
        h = jax.nn.relu(jnp.einsum('end,edf->enf', normed, W1) + b1[:, None, :])
        out = jnp.einsum('enf,efd->end', h, W2) + b2[:, None, :] + xf[None, :, :]
        cw = jnp.sum(w[..., None] * jax.nn.one_hot(idx, E, dtype=w.dtype), axis=1)
        y = jnp.einsum('ne,end->nd', cw, out)
        return y.reshape(orig_shape)
    x = L0_attn_x
    mod = (_silu(L0_c) @ L0_wmod).reshape(L0_c.shape[0], 6, 1, -1)
    sa, ca, ga, sb, cb, gb = (mod[:, 0], mod[:, 1], mod[:, 2], mod[:, 3], mod[:, 4], mod[:, 5])
    ga = (2 * (ga >= 0) - 1) * jnp.maximum(jnp.abs(ga), 0.25)
    gb = (2 * (gb >= 0) - 1) * jnp.maximum(jnp.abs(gb), 0.25)
    h = _layernorm(x, axis=-1) * (1 + ca) + sa
    x = x + ga * _L0_attn_ref(h, L0_attn_norm_w, L0_attn_W_in, L0_attn_conv_w, L0_attn_conv_b, L0_attn_W_x, L0_attn_W_dt, L0_attn_b_dt, L0_attn_A_log, L0_attn_D_skip, L0_attn_W_out)
    h = _layernorm(x, axis=-1) * (1 + cb) + sb
    x = x + gb * _L0_ffn_ref(h, L0_ffn_Wg, L0_ffn_gamma, L0_ffn_beta, L0_ffn_W1, L0_ffn_b1, L0_ffn_W2, L0_ffn_b2)
    return x

_drawn_inputs = setup_inputs


def setup_inputs(seed=0):
    import zlib

    import numpy as np

    out = dict(_drawn_inputs(seed))
    spreads = {'L0_attn_norm_w': (1.0, 0.2),
     'L0_attn_conv_b': (0.0, 0.274),
     'L0_attn_D_skip': (1.0, 0.6),
     'L0_ffn_gamma': (1.0, 0.6),
     'L0_ffn_beta': (0.0, 0.664),
     'L0_ffn_b1': (0.0, 0.644),
     'L0_ffn_b2': (0.0, 0.464)}
    factors = {'L0_attn_b_dt': 4.999}
    for name, (base, spread) in spreads.items():
        noise = np.random.default_rng([zlib.crc32(name.encode()), seed]).standard_normal(out[name].shape)
        drawn = base * np.exp(spread * noise) if base else spread * noise
        out[name] = jnp.asarray(drawn.astype(out[name].dtype))
    for name, factor in factors.items():
        out[name] = (out[name] * factor).astype(out[name].dtype)
    return out
```

```python
import concourse.bass as bass
from concourse import mybir
from contextlib import ExitStack

F32 = mybir.dt.float32
U32 = mybir.dt.uint32
I32 = mybir.dt.int32
ALU = mybir.AluOpType
ACT = mybir.ActivationFunctionType
AX = mybir.AxisListType

NB, L, D = 8, 512, 256
DIN, NS, R, K = 512, 16, 64, 4
E, F = 8, 1024
P = 128
NTOK = NB * L
CH = DIN // P
TI = L // P
DC = D // P
FC = F // P
XD = R + 2 * NS
NT = NTOK // P
NSLOT = 2 * NTOK // P + E
UNITS = NS * CH
PAD = K - 1
LN_EPS, FFN_EPS = 1e-5, 1e-6
P_LINKS, O_LINKS = 3, 17


def adaln_kernel(nc, x, norm_w, W_in, conv_w, conv_b, W_x, W_dt, b_dt, A_log, D_skip, W_out,
                 Wg, gamma, beta, W1, b1, W2, b2, cT, wmod, out):
    def dram(name, shape):
        return nc.dram_tensor(name, shape, F32, kind="Internal").ap()

    mod_d = dram("mod_d", (NB, 6 * D))
    b_d = dram("b_d", (NB, NS, L))
    xhat_d = dram("xhat_d", (NTOK, D))
    base_d = dram("base_d", (NTOK, D))
    slotx_d = dram("slotx_d", (NSLOT * P, D))
    sloty_d = dram("sloty_d", (NSLOT * P, D))

    ctx = ExitStack()
    with ctx:
        def sb(name, shape, dt=F32, stack=ctx):
            return stack.enter_context(nc.sbuf_tensor(name, shape, dt))

        def sem(name):
            return ctx.enter_context(nc.semaphore(name))

        ident = sb("ident", [P, P])
        oh = sb("oh", [P, 2, NT, E])
        wts = sb("wts", [P, 2, NT])
        slots = sb("slots", [P, 2, NT], U32)
        tile_expert = sb("tile_expert", [P, NSLOT], I32)
        psum = ctx.enter_context(nc.psum_tensor("psum", [P, 8, 512], F32))
        T = psum[:, 0:4, :]
        Q = psum[:, 4:8, :]

        stage_a(nc, ctx, sem, ident, oh, wts, T, Q, mod_d, b_d, xhat_d, base_d, slotx_d,
                x, norm_w, W_in, conv_w, conv_b, W_x, W_dt, b_dt, A_log, D_skip, W_out, Wg, cT, wmod)
        with ExitStack() as held:
            w1_sb = sb("w1_sb", [P, E * DC, F], stack=held)
            w2_sb = sb("w2_sb", [P, E * FC, D], stack=held)
            b1_sb = sb("b1_sb", [P, E, F], stack=held)
            b2_sb = sb("b2_sb", [P, E, D], stack=held)
            gam = sb("gam", [P, E * DC], stack=held)
            bet = sb("bet", [P, E * DC], stack=held)
            weights_in = sem("weights_in")
            stage_b(nc, sem, ident, oh, slots, tile_expert, psum, xhat_d, slotx_d,
                    w1_sb, w2_sb, b1_sb, b2_sb, gam, bet, W1, W2, b1, b2, gamma, beta, weights_in)
            stage_c(nc, sem, ident, tile_expert, psum, slotx_d, sloty_d, w1_sb, w2_sb, b1_sb, b2_sb, gam, bet)
        stage_d(nc, sem, slots, wts, mod_d, base_d, sloty_d, out)


def stage_a(nc, ctx, sem, ident, oh, wts, T, Q, mod_d, b_d, xhat_d, base_d, slotx_d,
            x, norm_w, W_in, conv_w, conv_b, W_x, W_dt, b_dt, A_log, D_skip, W_out, Wg, cT, wmod):
    with ExitStack() as own:
        def sb(name, shape, dt=F32):
            return own.enter_context(nc.sbuf_tensor(name, shape, dt))

        win = sb("win", [P, DC, 2 * DIN])
        wx = sb("wx", [P, CH, XD])
        wdt = sb("wdt", [R, DIN])
        wout = sb("wout", [P, CH, D])
        wg = sb("wg", [P, DC, E])
        nw = sb("nw", [P, DC])
        cw = sb("cw", [P, CH, K])
        cb = sb("cb", [P, CH])
        bdt = sb("bdt", [P, CH])
        dsk = sb("dsk", [P, CH])
        aneg = sb("aneg", [P, CH, NS])
        iota8 = sb("iota8", [P, E])
        mhalf = sb("mhalf", [P, TI])
        xin = sb("xin", [P, 2, TI, D])
        hmod = sb("hmod", [P, 2, TI, D])
        modp = sb("modp", [P, 2, D])
        modo = sb("modo", [P, 4, D])
        xn = sb("xn", [P, TI, D])
        xnT = sb("xnT", [P, DC, L])
        xipad = sb("xipad", [P, CH, PAD + L])
        xc = sb("xc", [P, 2, CH, L])
        sz = sb("sz", [P, 2, CH, L])
        xd = sb("xd", [XD, L])
        ct = sb("ct", [P, 2, TI, NS])
        dt = sb("dt", [P, 2, CH, L])
        u = sb("u", [P, 2, CH, L])
        brep = sb("brep", [P, 4, L])
        dA = sb("dA", [P, 4, L])
        dBu = sb("dBu", [P, 4, L])
        hs = sb("hs", [P, 2, CH, L])
        y = sb("y", [P, TI, DIN])
        gT = sb("gT", [P, CH, L])
        xfT = gT
        x1 = sb("x1", [P, TI, D])
        xf = sb("xf", [P, TI, D])
        xh = sb("xh", [P, TI, D])
        bs = sb("bs", [P, TI, 6])
        mv = sb("mv", [P, 3, TI, 2])
        rs = sb("rs", [P, 4, TI])
        tmp = sb("tmp", [P, 4, TI])
        ssq = sb("ssq", [P, TI])
        sc = sb("sc", [P, TI, E])
        top = sb("top", [P, TI, 8])
        tix = sb("tix", [P, TI, 8], U32)
        tif = sb("tif", [P, TI, 2])
        vd = sb("vd", [P, 4, TI])
        spare = sb("spare", [P, 1])
        eps = sb("eps", [P, 2, TI])
        cts = xn[:, 0, 0:DC * NB].rearrange("p (k b) -> p k b", k=DC)
        wmod_sb = hs[:, :, :, :].rearrange("p a c l -> p (a c l)")[:, 0:DC * 6 * D].rearrange("p (k n) -> p k n", k=DC)
        m8 = y[0:NB, :, :].rearrange("p a b -> p (a b)")[:, 0:6 * D]
        m8n = gT[0:NB, 0, 0:2 * D].rearrange("p (a d) -> p a d", a=2)
        zrow = dt[:, 0, :, :].rearrange("p c l -> p (c l)")

        s_w = sem("weights_loaded")
        s_ct = sem("c_loaded")
        s_id = sem("ident_steps")
        s_csilu = sem("c_silu")
        s_modps = sem("mod_ps")
        s_m8 = sem("mod_rows_copied")
        s_modr = sem("mod_rows_ready")
        s_modst = sem("mod_stored")
        s_const = sem("constants_ready")
        s_aexp = sem("a_exp")
        s_zero = sem("slot_rows_zeroed")
        s_pload = sem("x_and_modp_loaded")
        s_oload = sem("modo_loaded")
        s_ln1 = sem("ln1_stats")
        s_ln1r = sem("ln1_rstd")
        s_h = sem("h_ready")
        s_sq = sem("square_sums")
        s_rms = sem("rms_rstd")
        s_xn = sem("xn_ready")
        s_xntp = sem("xnT_ps")
        s_xnt = sem("xnT_ready")
        s_xip = sem("xi_ps")
        s_xi = sem("xi_ready")
        s_zp = sem("z_ps")
        s_z = sem("z_ready")
        s_tap = sem("conv_taps")
        s_xc = sem("xc_ready")
        s_xdp = sem("xd_ps")
        s_xd = sem("xd_ready")
        s_bst = sem("b_stored")
        s_cp = sem("c_ps")
        s_c = sem("c_ready")
        s_dtp = sem("dt_ps")
        s_sp = sem("softplus_parts")
        s_dt = sem("dt_ready")
        s_u = sem("u_ready")
        s_br = [sem(f"brep_loaded{i}") for i in range(4)]
        s_dA = sem("dA_ready")
        s_dBu = sem("dBu_ready")
        s_scan = sem("scanned")
        s_tr = sem("states_transposed")
        s_y = sem("y_added")
        s_yT = sem("yT_ps")
        s_g = sem("skip_added")
        s_gate = sem("gated")
        s_op = sem("out_ps")
        s_x1 = sem("x1_ready")
        s_ln2r = sem("ln2_rstd")
        s_xf = sem("xf_ready")
        s_ln3r = sem("ln3_rstd")
        s_xh = sem("xhat_ready")
        s_xhst = sem("xhat_stored")
        s_xftp = sem("xfT_ps")
        s_xft = sem("xfT_ready")
        s_scp = sem("scores_ps")
        s_vd = sem("top_difference")
        s_ve = sem("top_exp")
        s_base = sem("base_ready")
        s_bast = sem("base_stored")
        s_act = sem("act_links")

        def after(eng, s, value):
            if not (isinstance(value, int) and value <= 0):
                eng.wait_ge(s, value)

        def immediate(eng):
            eng.wait_ge(s_id, 2)

        def sequences(eng, prologue, body, epilogue):
            prologue()
            body(0, 0, False, True)
            with eng.Fori(0, (NB - 2) // 2) as turn:
                body(2 * turn + 1, 1, True, True)
                body(2 * turn + 2, 0, True, True)
            body(NB - 1, 1, True, False)
            epilogue()

        block = own.enter_context(nc.Block())

        @block.sync
        def _(sp):
            sp.dma_start(cts, cT.rearrange("(k p) b -> p k b", p=P)).then_inc(s_ct, 16)
            sp.dma_start(wmod_sb, wmod.rearrange("(k p) n -> p k n", p=P)).then_inc(s_ct, 16)
            for dst, src in ((win[:, :, :], W_in.rearrange("(k p) n -> p k n", p=P)),
                             (wx[:, :, :], W_x.rearrange("(k p) n -> p k n", p=P)),
                             (wdt[:, :], W_dt), (wout[:, :, :], W_out.rearrange("(k p) n -> p k n", p=P)),
                             (wg[:, :, :], Wg.rearrange("(k p) n -> p k n", p=P)),
                             (nw[:, :], norm_w), (cw[:, :, :], conv_w), (cb[:, :], conv_b),
                             (bdt[:, :], b_dt), (dsk[:, :], D_skip), (aneg[:, :, :], A_log)):
                sp.dma_start(dst, src).then_inc(s_w, 16)
            sp.wait_ge(s_const, 1)
            zsrc = zrow.rearrange("p (a d) -> p a d", d=D)
            per = CH * L // D
            for k in range(NSLOT // per):
                sp.dma_start(slotx_d[k * per * P:(k + 1) * per * P, :].rearrange("(p a) d -> p a d", p=P),
                             zsrc).then_inc(s_zero, 16)
            sp.wait_ge(s_modr, 1)
            sp.dma_start(mod_d, m8).then_inc(s_modst, 16)
            sp.wait_ge(s_modst, 16)
            sp.wait_ge(s_zero, 16 * (NSLOT // per))

            def mod_rows(n, first, count, dst):
                rows = mod_d[bass.ds(n, 1), first * D:(first + count) * D]
                return dict(out=dst.rearrange("p m d -> p (m d)"), in_=rows.to_broadcast([P, count * D]))

            def load(n, p):
                immediate(sp)
                after(sp, s_x1, n - 1)
                sp.dma_start(xin[:, p, :, :], x[bass.ds(n * L, L), :].rearrange("(i p) d -> p i d", p=P)).then_inc(s_pload, 16)
                sp.dma_start(**mod_rows(n, 0, 2, modp[:, :, :])).then_inc(s_pload, 16)

            def load_o(n):
                immediate(sp)
                after(sp, s_base, n)
                sp.dma_start(**mod_rows(n, 2, 4, modo[:, :, :])).then_inc(s_oload, 16)

            def store_b(n):
                immediate(sp)
                sp.wait_ge(s_xd, n + 1)
                sp.dma_start(b_d[bass.ds(n, 1), :, :].rearrange("a s l -> (a s) l"), xd[R:R + NS, :]).then_inc(s_bst, 16)

            def load_brep(n, s):
                immediate(sp)
                if s == 0:
                    sp.wait_ge(s_bst, 16 * (n + 1))
                after(sp, s_dBu, n * UNITS + 4 * (s - 3))
                sp.dma_start(brep[:, s % 4, :], b_d[bass.ds(n, 1), s, :].to_broadcast([P, L])).then_inc(s_br[s % 4], 16)

            def store_xhat(n):
                immediate(sp)
                sp.wait_ge(s_xh, n + 1)
                sp.dma_start(xhat_d[bass.ds(n * L, L), :].rearrange("(i p) d -> p i d", p=P), xh[:, :, :]).then_inc(s_xhst, 16)

            def store_base(n):
                immediate(sp)
                sp.wait_ge(s_base, n + 1)
                sp.dma_start(base_d[bass.ds(n * L, L), :].rearrange("(i p) d -> p i d", p=P), x1[:, :, :]).then_inc(s_bast, 16)

            def prologue():
                load(0, 0)
                store_b(0)

            def body(n, p, has_o, has_p):
                for s in range(NS):
                    load_brep(n, s)
                    if has_o and s == 1:
                        load_o(n - 1)
                    if has_p and s == 5:
                        load(n + 1, 1 - p)
                    if has_o and s == 9:
                        store_xhat(n - 1)
                    if has_o and s == 12:
                        store_base(n - 1)
                if has_p:
                    store_b(n + 1)

            def epilogue():
                load_o(NB - 1)
                store_xhat(NB - 1)
                store_base(NB - 1)
                sp.wait_ge(s_xhst, 16 * NB)
                sp.wait_ge(s_bast, 16 * NB)

            sequences(sp, prologue, body, epilogue)

        @block.gpsimd
        def _(pool):
            pool.memset(zrow, 0.0)
            pool.memset(mhalf[:, :], -0.5)
            pool.memset(eps[:, 0, :], LN_EPS)
            pool.memset(eps[:, 1, :], FFN_EPS)
            pool.iota(iota8[:, :], [[1, E]], base=0, channel_multiplier=0, allow_small_or_imprecise_dtypes=True)
            pool.memset(xipad[:, :, 0:PAD], 0.0).then_inc(s_const, 1)
            pool.memset(ident[:, :], 0.0).then_inc(s_id, 1)
            pool.wait_ge(s_id, 1)
            pool.affine_select(out=ident[:, :], in_=ident[:, :], compare_op=ALU.not_equal, fill=1.0, base=0,
                               pattern=[[-1, P]], channel_multiplier=1).then_inc(s_id, 1)

            def ln1(n):
                pool.wait_ge(s_ln1, n + 1)
                rstd_p(n, 0, mv[:, 0, :, 1], eps[:, 0, :], s_ln1r)

            def rms(n):
                pool.wait_ge(s_sq, n + 1)
                rstd_p(n, 3, ssq[:, :], eps[:, 0, :], s_rms)

            pl, ol = sem("pool_links_p"), sem("pool_links_o")

            def rstd_on(s, count, which, src, add, ready):
                nc.gpsimd.tensor_tensor(tmp[:, which, :], src, add, ALU.add).then_inc(s, 1)
                pool.wait_ge(s, count)
                nc.gpsimd.tensor_tensor(rs[:, which, :], tmp[:, which, :], mhalf[:, :], ALU.pow).then_inc(ready, 1)

            def rstd_p(n, which, src, add, ready):
                rstd_on(pl, 2 * n + (1 if which == 0 else 2), which, src, add, ready)

            def gate(n, p):
                for c in range(CH):
                    pool.wait_ge(s_g, n * CH + c + 1)
                    nc.gpsimd.tensor_tensor(gT[:, c, :], gT[:, c, :], sz[:, p, c, :], ALU.mult).then_inc(s_gate, 1)

            def ln2(n):
                pool.wait_ge(s_x1, n + 1)
                rstd_on(ol, 2 * n + 1, 1, mv[:, 1, :, 1], eps[:, 0, :], s_ln2r)

            def ln3(n):
                pool.wait_ge(s_xf, n + 1)
                rstd_on(ol, 2 * n + 2, 2, mv[:, 2, :, 1], eps[:, 1, :], s_ln3r)

            def inputs(n, p, s):
                pool.wait_ge(s_br[s % 4], 16 * (n * (NS // 4) + s // 4 + 1))
                for c in range(CH):
                    i = s * CH + c
                    if s == 0:
                        pool.wait_ge(s_u, n * CH + c + 1)
                    after(pool, s_scan, n * UNITS + i - 3)
                    nc.gpsimd.tensor_tensor(dBu[:, i % 4, :], u[:, p, c, :], brep[:, s % 4, :], ALU.mult).then_inc(s_dBu, 1)

            def prologue():
                ln1(0)
                rms(0)

            def body(n, p, has_o, has_p):
                for s in range(NS):
                    inputs(n, p, s)
                    if has_o and s == 1:
                        gate(n - 1, 1 - p)
                    if has_o and s == 4:
                        ln2(n - 1)
                    if has_o and s == 6:
                        ln3(n - 1)
                    if has_p and s == 7:
                        ln1(n + 1)
                    if has_p and s == 8:
                        rms(n + 1)

            def epilogue():
                gate(NB - 1, 1)
                ln2(NB - 1)
                ln3(NB - 1)

            sequences(pool, prologue, body, epilogue)

        @block.scalar
        def _(act):
            act.wait_ge(s_ct, 32)
            nc.scalar.activation(cts, cts, ACT.Silu).then_inc(s_csilu, 1)
            for j in range(3):
                act.wait_ge(s_modps, j + 1)
                nc.scalar.activation(m8[:, j * 512:(j + 1) * 512], Q[0:NB, j, :], ACT.Copy).then_inc(s_m8, 1)
            act.wait_ge(s_w, 16 * 11)
            nc.scalar.activation(aneg[:, :, :], aneg[:, :, :], ACT.Exp).then_inc(s_aexp, 1)
            act.wait_ge(s_aexp, 1)
            nc.scalar.activation(aneg[:, :, :], aneg[:, :, :], ACT.Copy, scale=-1.0).then_inc(s_aexp, 1)
            act.wait_ge(s_aexp, 2)

            def squares(n, p):
                act.wait_ge(s_h, n + 1)
                for i in range(TI):
                    last = nc.scalar.activation(xn[:, i, :], hmod[:, p, i, :], ACT.Square, scale=float(D) ** -0.5, accum_out=ssq[:, i:i + 1])
                last.then_inc(s_sq, 1)

            def norm(n, p):
                act.wait_ge(s_rms, n + 1)
                for i in range(TI):
                    last = nc.scalar.activation(xn[:, i, :], hmod[:, p, i, :], ACT.Copy, scale=rs[:, 3, i:i + 1])
                last.then_inc(s_xn, 1)

            def norm_t(n):
                act.wait_ge(s_xntp, n + 1)
                for c in range(DC):
                    last = nc.scalar.activation(xnT[:, c, :], Q[:, c, :], ACT.Copy, scale=nw[:, c:c + 1])
                last.then_inc(s_xnt, 1)

            def conv_in(n, chunks):
                for c in chunks:
                    act.wait_ge(s_xip, n * CH + c + 1)
                    nc.scalar.activation(xipad[:, c, PAD:], Q[:, c, :], ACT.Copy).then_inc(s_xi, 1)

            def silus(n, p):
                for c in range(CH):
                    act.wait_ge(s_zp, n * CH + c + 1)
                    nc.scalar.activation(sz[:, p, c, :], Q[:, c, :], ACT.Silu).then_inc(s_z, 1)
                for c in range(CH):
                    act.wait_ge(s_tap, n * CH * K + CH * (K - 1) + c + 1)
                    nc.scalar.activation(xc[:, p, c, :], xc[:, p, c, :], ACT.Silu).then_inc(s_xc, 1)

            def xd_copy(n):
                act.wait_ge(s_xdp, n + 1)
                after(act, s_bst, 16 * n)
                nc.scalar.activation(xd[:, :], Q[0:XD, 0, :], ACT.Copy).then_inc(s_xd, 1)

            def c_copy(n, p):
                act.wait_ge(s_cp, n + 1)
                nc.scalar.activation(ct[:, p, :, :], Q[:, 1, 0:TI * XD].rearrange("p (i n) -> p i n", i=TI)[:, :, R + NS:XD],
                                     ACT.Copy).then_inc(s_c, 1)

            def softplus(n, p):
                for c in range(CH):
                    q = Q[:, (c + 2) % 4, :]
                    act.wait_ge(s_dtp, n * CH + c + 1)
                    nc.scalar.activation(u[:, p, c, :], q, ACT.Abs, bias=bdt[:, c:c + 1]).then_inc(s_act, 1)
                    nc.scalar.activation(dt[:, p, c, :], q, ACT.Relu, bias=bdt[:, c:c + 1])
                for c in range(CH):
                    act.wait_ge(s_act, n * 2 * CH + c + 1)
                    nc.scalar.activation(u[:, p, c, :], u[:, p, c, :], ACT.Exp, scale=-1.0).then_inc(s_act, 1)
                for c in range(CH):
                    act.wait_ge(s_act, n * 2 * CH + CH + c + 1)
                    nc.scalar.activation(u[:, p, c, :], u[:, p, c, :], ACT.Ln, bias=1.0).then_inc(s_sp, 1)

            def decays(n, p, s):
                for c in range(CH):
                    i = s * CH + c
                    if s == 0:
                        act.wait_ge(s_dt, n * CH + c + 1)
                    after(act, s_scan, n * UNITS + i - 3)
                    nc.scalar.activation(dA[:, i % 4, :], dt[:, p, c, :], ACT.Exp,
                                         scale=aneg[:, c, s:s + 1]).then_inc(s_dA, 1)

            def scores_in(n):
                act.wait_ge(s_xftp, n + 1)
                for c in range(DC):
                    last = nc.scalar.activation(xfT[:, c, :], Q[:, 2 + c, :], ACT.Copy)
                last.then_inc(s_xft, 1)

            def top_exp(n):
                act.wait_ge(s_vd, n + 1)
                nc.scalar.activation(vd[:, 1, :], vd[:, 0, :], ACT.Exp).then_inc(s_ve, 1)

            def prologue():
                squares(0, 0)
                norm(0, 0)
                norm_t(0)
                conv_in(0, range(CH))
                silus(0, 0)
                xd_copy(0)
                c_copy(0, 0)
                softplus(0, 0)

            def body(n, p, has_o, has_p):
                for s in range(NS):
                    decays(n, p, s)
                    if has_o and s == 7:
                        scores_in(n - 1)
                    if has_p and s == 8:
                        squares(n + 1, 1 - p)
                    if has_o and s == 9:
                        top_exp(n - 1)
                    if has_p and s == 9:
                        norm(n + 1, 1 - p)
                    if has_p and s == 10:
                        norm_t(n + 1)
                    if has_p and s == 11:
                        conv_in(n + 1, (0, 1))
                    if has_p and s == 12:
                        conv_in(n + 1, (2, 3))
                    if has_p and s == 15:
                        silus(n + 1, 1 - p)
                        xd_copy(n + 1)
                        c_copy(n + 1, 1 - p)
                        softplus(n + 1, 1 - p)

            def epilogue():
                scores_in(NB - 1)
                top_exp(NB - 1)

            sequences(act, prologue, body, epilogue)

        @block.tensor
        def _(pe):
            pe.wait_ge(s_csilu, 1)
            for j in range(3):
                for k in range(DC):
                    last = nc.tensor.matmul(Q[0:NB, j, :], cts[:, k, :], wmod_sb[:, k, j * 512:(j + 1) * 512],
                                            start=(k == 0), stop=(k == DC - 1))
                last.then_inc(s_modps, 1)
            pe.wait_ge(s_id, 2)
            pe.wait_ge(s_w, 16 * 11)
            pe.wait_ge(s_m8, 3)

            def norm_t(n):
                pe.wait_ge(s_xn, n + 1)
                after(pe, s_vd, n - 1)
                for c in range(DC):
                    for i in range(TI):
                        last = nc.tensor.transpose(Q[:, c, i * P:(i + 1) * P], xn[:, i, c * P:(c + 1) * P], ident[:, :])
                last.then_inc(s_xntp, 1)

            def in_proj_x(n, chunks):
                pe.wait_ge(s_xnt, n + 1)
                for c in chunks:
                    for k in range(DC):
                        last = nc.tensor.matmul(Q[:, c, :], win[:, k, c * P:(c + 1) * P], xnT[:, k, :],
                                                start=(k == 0), stop=(k == DC - 1))
                    last.then_inc(s_xip, 1)

            def in_proj_z(n, chunks):
                for c in chunks:
                    pe.wait_ge(s_xi, n * CH + c + 1)
                    for k in range(DC):
                        last = nc.tensor.matmul(Q[:, c, :], win[:, k, DIN + c * P:DIN + (c + 1) * P], xnT[:, k, :],
                                                start=(k == 0), stop=(k == DC - 1))
                    last.then_inc(s_zp, 1)

            def x_proj(n, p):
                pe.wait_ge(s_z, n * CH + CH)
                for c in range(CH):
                    pe.wait_ge(s_xc, n * CH + c + 1)
                    last = nc.tensor.matmul(Q[0:XD, 0, :], wx[:, c, :], xc[:, p, c, :],
                                            start=(c == 0), stop=(c == CH - 1))
                last.then_inc(s_xdp, 1)
                pe.wait_ge(s_xd, n + 1)
                for i in range(TI):
                    last = nc.tensor.transpose(Q[:, 1, i * XD:(i + 1) * XD], xd[:, i * P:(i + 1) * P], ident[0:XD, 0:XD])
                last.then_inc(s_cp, 1)
                for c in range(CH):
                    if c == 3:
                        pe.wait_ge(s_c, n + 1)
                    nc.tensor.matmul(Q[:, (c + 2) % 4, :], wdt[:, c * P:(c + 1) * P], xd[0:R, :],
                                     start=True, stop=True).then_inc(s_dtp, 1)

            def states(n, s):
                pe.wait_ge(s_scan, n * UNITS + CH * (s + 1))
                for i in range(TI):
                    after(pe, s_y, n * UNITS + TI * (s - 1) + i + 1)
                    for c in range(CH):
                        last = nc.tensor.transpose(T[:, i, c * P:(c + 1) * P], hs[:, s % 2, c, i * P:(i + 1) * P], ident[:, :])
                    last.then_inc(s_tr, 1)

            def y_t(n, projected):
                pe.wait_ge(s_y, (n + 1) * UNITS)
                pe.wait_ge(s_sp, projected * CH)
                for c in range(CH):
                    for i in range(TI):
                        last = nc.tensor.transpose(Q[:, c, i * P:(i + 1) * P], y[:, i, c * P:(c + 1) * P], ident[:, :])
                    last.then_inc(s_yT, 1)

            def out_proj(n):
                pe.wait_ge(s_gate, (n + 1) * CH)
                for i in range(TI):
                    for c in range(CH):
                        last = nc.tensor.matmul(Q[:, i // 2, (i % 2) * D:(i % 2 + 1) * D], gT[:, c, i * P:(i + 1) * P],
                                                wout[:, c, :], start=(c == 0), stop=(c == CH - 1))
                last.then_inc(s_op, 1)

            def xf_t(n):
                pe.wait_ge(s_xf, n + 1)
                for c in range(DC):
                    for i in range(TI):
                        last = nc.tensor.transpose(Q[:, 2 + c, i * P:(i + 1) * P], xf[:, i, c * P:(c + 1) * P], ident[:, :])
                last.then_inc(s_xftp, 1)

            def scores(n):
                pe.wait_ge(s_xft, n + 1)
                for i in range(TI):
                    for c in range(DC):
                        last = nc.tensor.matmul(Q[:, 0, i * E:(i + 1) * E], xfT[:, c, i * P:(i + 1) * P], wg[:, c, :],
                                                start=(c == 0), stop=(c == DC - 1))
                last.then_inc(s_scp, 1)

            def prologue():
                norm_t(0)
                in_proj_x(0, range(CH))
                in_proj_z(0, range(CH))
                x_proj(0, 0)

            def body(n, p, has_o, has_p):
                if has_o:
                    y_t(n - 1, n + 1)
                for s in range(NS):
                    states(n, s)
                    if has_o and s == 2:
                        out_proj(n - 1)
                    if has_o and s == 6:
                        xf_t(n - 1)
                    if has_o and s == 7:
                        scores(n - 1)
                    if has_p and s == 9:
                        norm_t(n + 1)
                    if has_p and s in (10, 11):
                        in_proj_x(n + 1, (0, 1) if s == 10 else (2, 3))
                    if has_p and s in (12, 13):
                        in_proj_z(n + 1, (0, 1) if s == 12 else (2, 3))
                    if has_p and s == 15:
                        x_proj(n + 1, 1 - p)

            def epilogue():
                y_t(NB - 1, NB)
                out_proj(NB - 1)
                xf_t(NB - 1)
                scores(NB - 1)

            sequences(pe, prologue, body, epilogue)

        @block.vector
        def _(dve):
            own_p, own_o = sem("dve_links_p"), sem("dve_links_o")
            count = {"p": 0, "o": 0}

            def link(ins, kind, n):
                s, per = (own_p, P_LINKS) if kind == "p" else (own_o, O_LINKS)
                ins.then_inc(s, 1)
                count[kind] += 1
                dve.wait_ge(s, n * per + count[kind])

            def counted(p_links, o_links):
                assert count == {"p": p_links, "o": o_links}, count
                count["p"] = count["o"] = 0

            dve.wait_ge(s_m8, 3)
            m6 = m8.rearrange("p (m d) -> p m d", m=6)
            setup = sem("dve_setup")
            steps = [0]

            def then(ins):
                steps[0] += 1
                ins.then_inc(setup, 1)
                dve.wait_ge(setup, steps[0])

            for m in (1, 4):
                then(nc.vector.tensor_scalar(m6[:, m, :], m6[:, m, :], 1.0, None, ALU.add))
            for m in (2, 5):
                a, b = m8n[:, 0, :], m8n[:, 1, :]
                then(nc.vector.tensor_scalar(a, m6[:, m, :], -1.0, None, ALU.mult))
                then(nc.vector.tensor_tensor(a, a, m6[:, m, :], ALU.max))
                then(nc.vector.tensor_scalar(b, m6[:, m, :], 0.0, 2.0, ALU.is_ge, ALU.mult))
                then(nc.vector.tensor_scalar(b, b, -1.0, None, ALU.add))
                then(nc.vector.tensor_scalar(a, a, 0.25, None, ALU.max))
                then(nc.vector.tensor_tensor(m6[:, m, :], a, b, ALU.mult))
            nc.vector.tensor_copy(tif[0:1, 0, 0:1], m6[0:1, 0, 0:1]).then_inc(s_modr, 1)
            dve.wait_ge(s_const, 1)
            dve.wait_ge(s_w, 16 * 11)
            dve.wait_ge(s_modst, 16)
            dve.wait_ge(s_zero, 16 * (NSLOT // (CH * L // D)))

            def carrier():
                nc.vector.memset(spare[:, :], 0.0)

            def stats(kind, n, src, which, ready):
                for i in range(TI):
                    last = nc.vector.bn_stats(bs[:, i, :], src[:, i, :])
                link(last, kind, n)
                carrier()
                for i in range(TI):
                    last = nc.vector.bn_aggr(mv[:, which, i, :], bs[:, i, :])
                if ready is not None:
                    last.then_inc(ready, 1)
                return last

            def normalise(dst, src, which):
                for i in range(TI):
                    last = nc.vector.tensor_scalar(dst[:, i, :], src[:, i, :], mv[:, which, i, 0:1], rs[:, which, i:i + 1],
                                                   ALU.subtract, ALU.mult)
                return last

            def rows(m):
                return m.unsqueeze(1).to_broadcast([P, TI, D])

            def p_stats(n, p):
                dve.wait_ge(s_pload, 32 * (n + 1))
                stats("p", n, xin[:, p], 0, s_ln1)

            def p_mod(n, p):
                h = hmod[:, p, :, :]
                dve.wait_ge(s_ln1r, n + 1)
                link(normalise(h, xin[:, p], 0), "p", n)
                link(nc.vector.tensor_tensor(h, h, rows(modp[:, 1, :]), ALU.mult), "p", n)
                nc.vector.tensor_tensor(h, h, rows(modp[:, 0, :]), ALU.add).then_inc(s_h, 1)

            def conv(n, p, taps):
                for k in taps:
                    for c in range(CH):
                        src = xipad[:, c, k:k + L]
                        dst = xc[:, p, c, :]
                        if k == 0:
                            dve.wait_ge(s_xi, n * CH + c + 1)
                            ins = nc.vector.tensor_scalar(dst, src, cw[:, c, 0:1], cb[:, c:c + 1], ALU.mult, ALU.add)
                        else:
                            dve.wait_ge(s_tap, n * CH * K + CH * (k - 1) + c + 1)
                            ins = nc.vector.scalar_tensor_tensor(dst, src, cw[:, c, k:k + 1], dst, ALU.mult, ALU.add)
                        ins.then_inc(s_tap, 1)

            def dt_u(n, p):
                for c in range(CH):
                    dve.wait_ge(s_sp, n * CH + c + 1)
                    nc.vector.tensor_tensor(dt[:, p, c, :], dt[:, p, c, :], u[:, p, c, :], ALU.add).then_inc(s_dt, 1)
                for c in range(CH):
                    dve.wait_ge(s_dt, n * CH + c + 1)
                    nc.vector.tensor_tensor(u[:, p, c, :], dt[:, p, c, :], xc[:, p, c, :], ALU.mult).then_inc(s_u, 1)

            def scans(n, s):
                if s >= 2:
                    dve.wait_ge(s_tr, n * UNITS + TI * (s - 1))
                for c in range(CH):
                    i = s * CH + c
                    dve.wait_ge(s_dA, n * UNITS + i + 1)
                    dve.wait_ge(s_dBu, n * UNITS + i + 1)
                    nc.vector.tensor_tensor_scan(hs[:, s % 2, c, :], dA[:, i % 4, :], dBu[:, i % 4, :], 0.0,
                                                 ALU.mult, ALU.add).then_inc(s_scan, 1)

            def add_y(n, p, s):
                for i in range(TI):
                    dve.wait_ge(s_tr, n * UNITS + TI * s + i + 1)
                    c_s = ct[:, p, i, s:s + 1]
                    if s == 0:
                        after(dve, s_yT, n * CH)
                        ins = nc.vector.tensor_scalar(y[:, i, :], T[:, i, :], c_s, None, ALU.mult)
                    else:
                        dve.wait_ge(s_y, n * UNITS + TI * (s - 1) + i + 1)
                        ins = nc.vector.scalar_tensor_tensor(y[:, i, :], T[:, i, :], c_s, y[:, i, :], ALU.mult, ALU.add)
                    ins.then_inc(s_y, 1)

            def o_skip(n, p):
                for c in range(CH):
                    dve.wait_ge(s_yT, n * CH + c + 1)
                    nc.vector.scalar_tensor_tensor(gT[:, c, :], xc[:, p, c, :], dsk[:, c:c + 1], Q[:, c, :],
                                                   ALU.mult, ALU.add).then_inc(s_g, 1)

            def o_resid(n, p):
                dve.wait_ge(s_op, n + 1)
                dve.wait_ge(s_oload, 16 * (n + 1))
                o = Q[:, 0:2, :].rearrange("p b (i d) -> p (b i) d", d=D)
                after(dve, s_bast, 16 * n)
                link(nc.vector.tensor_tensor(x1[:, :, :], hmod[:, p, :, :], o, ALU.add), "o", n)
                link(nc.vector.tensor_tensor(x1[:, :, :], x1[:, :, :], rows(modo[:, 0, :]), ALU.mult), "o", n)
                link(nc.vector.tensor_tensor(x1[:, :, :], x1[:, :, :], xin[:, p, :, :], ALU.add), "o", n)
                stats("o", n, x1, 1, s_x1)

            def o_mod(n):
                dve.wait_ge(s_ln2r, n + 1)
                link(normalise(xf, x1, 1), "o", n)
                link(nc.vector.tensor_tensor(xf[:, :, :], xf[:, :, :], rows(modo[:, 2, :]), ALU.mult), "o", n)
                link(nc.vector.tensor_tensor(xf[:, :, :], xf[:, :, :], rows(modo[:, 1, :]), ALU.add), "o", n)
                stats("o", n, xf, 2, s_xf)

            def o_xhat(n):
                dve.wait_ge(s_ln3r, n + 1)
                after(dve, s_xhst, 16 * n)
                normalise(xh, xf, 2).then_inc(s_xh, 1)

            def o_top(n):
                dve.wait_ge(s_scp, n + 1)
                link(nc.vector.tensor_copy(sc[:, :, :], Q[:, 0, 0:TI * E].rearrange("p (i e) -> p i e", i=TI)), "o", n)
                carrier()
                for i in range(TI):
                    last = nc.vector.max(top[:, i, :], sc[:, i, :])
                link(last, "o", n)
                carrier()
                for i in range(TI):
                    last = nc.vector.max_index(tix[:, i, :], top[:, i, :], sc[:, i, :])
                nc.vector.tensor_tensor(vd[:, 0, :], top[:, :, 1], top[:, :, 0], ALU.subtract).then_inc(s_vd, 1)
                link(last, "o", n)
                link(nc.vector.tensor_copy(tif[:, :, :], tix[:, :, 0:2]), "o", n)
                for k in range(2):
                    nc.vector.tensor_tensor(oh[:, k, bass.ds(n * TI, TI), :], iota8[:, :].unsqueeze(1).to_broadcast([P, TI, E]),
                                            tif[:, :, k].unsqueeze(2).to_broadcast([P, TI, E]), ALU.is_equal)

            def o_base(n):
                dve.wait_ge(s_ve, n + 1)
                w1, w2 = wts[:, 0, bass.ds(n * TI, TI)], wts[:, 1, bass.ds(n * TI, TI)]
                link(nc.vector.tensor_scalar(vd[:, 2, :], vd[:, 1, :], 1.0, None, ALU.add), "o", n)
                link(nc.vector.reciprocal(vd[:, 2, :], vd[:, 2, :]), "o", n)
                link(nc.vector.tensor_tensor(vd[:, 1, :], vd[:, 1, :], vd[:, 2, :], ALU.mult), "o", n)
                nc.vector.tensor_copy(w1, vd[:, 2, :])
                nc.vector.tensor_copy(w2, vd[:, 1, :])
                link(nc.vector.tensor_tensor(vd[:, 3, :], vd[:, 1, :], vd[:, 2, :], ALU.add), "o", n)
                for i in range(TI):
                    last = nc.vector.scalar_tensor_tensor(xf[:, i, :], xf[:, i, :], vd[:, 3, i:i + 1], modo[:, 3, :],
                                                          ALU.mult, ALU.mult)
                link(last, "o", n)
                nc.vector.tensor_tensor(x1[:, :, :], x1[:, :, :], xf[:, :, :], ALU.add).then_inc(s_base, 1)

            def prologue():
                p_stats(0, 0)
                p_mod(0, 0)
                conv(0, 0, range(K))
                dt_u(0, 0)
                counted(P_LINKS, 0)

            def body(n, p, has_o, has_p):
                scans(n, 0)
                for s in range(NS):
                    if s + 1 < NS:
                        scans(n, s + 1)
                    if has_o and s == 0:
                        o_skip(n - 1, 1 - p)
                    add_y(n, p, s)
                    if has_o and s == 3:
                        o_resid(n - 1, 1 - p)
                    if has_o and s == 5:
                        o_mod(n - 1)
                    if has_p and s == 6:
                        p_stats(n + 1, 1 - p)
                    if has_o and s == 7:
                        o_xhat(n - 1)
                    if has_p and s == 7:
                        p_mod(n + 1, 1 - p)
                    if has_o and s == 8:
                        o_top(n - 1)
                    if has_o and s == 10:
                        o_base(n - 1)
                    if has_p and s in (12, 13, 14):
                        conv(n + 1, 1 - p, {12: (0,), 13: (1,), 14: (2, 3)}[s])
                    if has_p and s == 15:
                        dt_u(n + 1, 1 - p)
                counted(P_LINKS * has_p, O_LINKS * has_o)

            def epilogue():
                o_skip(NB - 1, 1)
                o_resid(NB - 1, 1)
                o_mod(NB - 1)
                o_xhat(NB - 1)
                o_top(NB - 1)
                o_base(NB - 1)

            sequences(dve, prologue, body, epilogue)


def stage_b(nc, sem, ident, oh, slots, tile_expert, psum, xhat_d, slotx_d,
            w1_sb, w2_sb, b1_sb, b2_sb, gam, bet, W1, W2, b1, b2, gamma, beta, s_wts):
    RING = 8
    with ExitStack() as own:
        def sb(name, shape, dt=F32):
            return own.enter_context(nc.sbuf_tensor(name, shape, dt))

        before = sb("before", [P, P])
        ones = sb("ones", [P, P])
        thr = sb("thr", [P, NT])
        jrow = sb("jrow", [P, NSLOT])
        mask = sb("mask", [P, NT, E])
        tot = sb("tot", [P, E, NT])
        incl = sb("incl", [P, E, NT])
        full = sb("full", [P, E, NT])
        ptiles = sb("ptiles", [P, E])
        tend = sb("tend", [P, E])
        tfirst = sb("tfirst", [P, E])
        slot3 = sb("slot3", [P, NT, E])
        pick = sb("pick", [P, NT, E])
        slotf = sb("slotf", [P, 2, NT])
        ended = sb("ended", [P, NSLOT, E])
        texp = sb("texp", [P, NSLOT])
        xs = sb("xs", [P, RING, D])
        s_k = sem("b_constants")
        s_mask = sem("mask_ready")
        s_cnt = sem("counts_ps")
        s_slots = sem("slots_ready")
        s_xs = [sem(f"xs_loaded{i}") for i in range(RING)]
        s_sc = [sem(f"xs_scattered{i}") for i in range(RING)]
        s_link = sem("b_links")
        block = own.enter_context(nc.Block())

        def load_expert(eng, e):
            eng.dma_start(w1_sb[:, e * DC:(e + 1) * DC, :], W1[e].rearrange("(k p) f -> p k f", p=P)).then_inc(s_wts, 16)
            eng.dma_start(w2_sb[:, e * FC:(e + 1) * FC, :], W2[e].rearrange("(k p) d -> p k d", p=P)).then_inc(s_wts, 16)

        @block.sync
        def _(sp):
            for i in range(NT):
                if i >= RING:
                    sp.wait_ge(s_sc[i % RING], 32 * (i // RING))
                sp.dma_start(xs[:, i % RING, :], xhat_d[i * P:(i + 1) * P, :]).then_inc(s_xs[i % RING], 16)

        @block.scalar
        def _(act):
            act.dma_start(gam[:, :], gamma).then_inc(s_wts, 16)
            act.dma_start(bet[:, :], beta).then_inc(s_wts, 16)
            act.dma_start(b1_sb[:, :, :].rearrange("p e f -> p (e f)"), b1.to_broadcast([P, E * F])).then_inc(s_wts, 16)
            act.dma_start(b2_sb[:, :, :].rearrange("p e d -> p (e d)"), b2.to_broadcast([P, E * D])).then_inc(s_wts, 16)
            for e in range(E):
                load_expert(act, e)
            act.wait_ge(s_wts, 16 * (4 + 2 * E))

        @block.gpsimd
        def _(pool):
            pool.memset(before[:, :], 0.0).then_inc(s_k, 1)
            pool.memset(ones[:, :], 1.0)
            pool.iota(thr[:, :], [[P, NT]], base=0, channel_multiplier=0, allow_small_or_imprecise_dtypes=True)
            pool.iota(jrow[:, :], [[1, NSLOT]], base=0, channel_multiplier=0, allow_small_or_imprecise_dtypes=True)
            pool.wait_ge(s_k, 1)
            pool.affine_select(out=before[:, :], in_=before[:, :], compare_op=ALU.is_ge, fill=1.0, base=0,
                               pattern=[[-1, P]], channel_multiplier=1).then_inc(s_k, 1)
            pool.wait_ge(s_slots, 1)
            for i in range(NT):
                pool.wait_ge(s_xs[i % RING], 16 * (i // RING + 1))
                for k in range(2):
                    pool.indirect_dma_start(slotx_d, bass.IndirectOffsetOnAxis(ap=slots[:, k, i:i + 1], axis=0),
                                            xs[:, i % RING, :], None).then_inc(s_sc[i % RING], 16)
            for r in range(RING):
                pool.wait_ge(s_sc[r], 32 * (NT // RING))

        @block.tensor
        def _(pe):
            pe.wait_ge(s_k, 2)
            pe.wait_ge(s_mask, 1)
            m = mask[:, :, :].rearrange("p i e -> p (i e)")
            nc.tensor.matmul(psum[:, 0, 0:NT * E], before[:, :], m, start=True, stop=True)
            nc.tensor.matmul(psum[:, 1, 0:NT * E], ones[:, :], m, start=True, stop=True).then_inc(s_cnt, 1)

        @block.vector
        def _(dve):
            steps = [0]

            def link(ins):
                steps[0] += 1
                ins.then_inc(s_link, 1)
                dve.wait_ge(s_link, steps[0])

            def over_tiles(v):
                return v.unsqueeze(1).to_broadcast([P, NT, E])

            nc.vector.tensor_tensor(mask[:, :, :], oh[:, 0, :, :], oh[:, 1, :, :], ALU.add).then_inc(s_mask, 1)
            dve.wait_ge(s_k, 2)
            dve.wait_ge(s_cnt, 1)
            link(nc.vector.tensor_copy(tot[:, :, :], psum[:, 1, 0:NT * E].rearrange("p (i e) -> p e i", e=E)))
            for e in range(E):
                last = nc.vector.tensor_tensor_scan(incl[:, e, :], ones[:, 0:NT], tot[:, e, :], 0.0, ALU.mult, ALU.add)
            link(last)
            link(nc.vector.tensor_tensor(full[:, :, :], incl[:, :, NT - 1:NT].to_broadcast([P, E, NT]),
                                         thr[:, :].unsqueeze(1).to_broadcast([P, E, NT]), ALU.is_gt))
            link(nc.vector.tensor_reduce(ptiles[:, :], full[:, :, :], AX.X, ALU.add))
            link(nc.vector.tensor_tensor_scan(tend[:, :], ones[:, 0:E], ptiles[:, :], 0.0, ALU.mult, ALU.add))
            link(nc.vector.tensor_tensor(tfirst[:, :], tend[:, :], ptiles[:, :], ALU.subtract))
            link(nc.vector.tensor_scalar(tfirst[:, :], tfirst[:, :], float(P), None, ALU.mult))
            link(nc.vector.tensor_tensor(incl[:, :, :], incl[:, :, :], tot[:, :, :], ALU.subtract))
            link(nc.vector.tensor_tensor(slot3[:, :, :], psum[:, 0, 0:NT * E].rearrange("p (i e) -> p i e", e=E),
                                         incl[:, :, :].rearrange("p e i -> p i e"), ALU.add))
            link(nc.vector.tensor_tensor(slot3[:, :, :], slot3[:, :, :], over_tiles(tfirst[:, :]), ALU.add))
            for k in range(2):
                link(nc.vector.tensor_tensor(pick[:, :, :], slot3[:, :, :], oh[:, k, :, :], ALU.mult))
                link(nc.vector.tensor_reduce(slotf[:, k, :], pick[:, :, :], AX.X, ALU.add))
            nc.vector.tensor_copy(slots[:, :, :], slotf[:, :, :]).then_inc(s_slots, 1)
            link(nc.vector.tensor_tensor(ended[:, :, :], tend[:, :].unsqueeze(1).to_broadcast([P, NSLOT, E]),
                                         jrow[:, :].unsqueeze(2).to_broadcast([P, NSLOT, E]), ALU.is_le))
            link(nc.vector.tensor_reduce(texp[:, :], ended[:, :, :], AX.X, ALU.add))
            link(nc.vector.tensor_scalar(texp[:, :], texp[:, :], float(E - 1), None, ALU.min))
            link(nc.vector.tensor_copy(tile_expert[:, :], texp[:, :]))


def stage_c(nc, sem, ident, tile_expert, psum, slotx_d, sloty_d, w1_sb, w2_sb, b1_sb, b2_sb, gam, bet):
    XR, YR = 4, 4
    with ExitStack() as own:
        def sb(name, shape, dt=F32):
            return own.enter_context(nc.sbuf_tensor(name, shape, dt))

        xg = sb("xg", [P, XR, D])
        xgT = sb("xgT", [P, 2, DC, P])
        hb = sb("hb", [P, F])
        hT = sb("hT", [P, FC, P])
        ysb = sb("ysb", [P, YR, D])
        X_PS = psum[:, 0, 0:DC * P].rearrange("p (k t) -> p k t", k=DC)
        H_PS = psum[:, 2:4, :]
        HT_PS = psum[:, 4:6, :]
        Y_PS = psum[:, 6:8, 0:D]
        s_x = [sem(f"xg_loaded{i}") for i in range(XR)]
        s_xtp = sem("xgT_ps")
        s_xt = sem("xgT_ready")
        s_hp = sem("h_ps")
        s_hb = sem("hb_ready")
        s_htp = sem("hT_ps")
        s_ht = sem("hT_ready")
        s_yp = sem("y_ps")
        s_ys = sem("ysb_ready")
        s_st = [sem(f"y_stored{i}") for i in range(YR)]
        block = own.enter_context(nc.Block())
        TURN = 4

        def after(eng, s, value):
            if not (isinstance(value, int) and value <= 0):
                eng.wait_ge(s, value)

        def tiles(eng, body):
            for r in range(TURN):
                body(r, r, 0)
            with eng.Fori(1, NSLOT // TURN) as group:
                for r in range(TURN):
                    body(group * TURN + r, r, group)

        @block.sync
        def _(sp):
            def step(j, r, group):
                after(sp, s_xtp, j - XR + 1)
                sp.dma_start(xg[:, r, :], slotx_d[bass.ds(j * P, P), :]).then_inc(s_x[r], 16)

            tiles(sp, step)

        @block.gpsimd
        def _(pool):
            def step(j, r, group):
                pool.wait_ge(s_ys, j + 1)
                pool.dma_start(sloty_d[bass.ds(j * P, P), :], ysb[:, r, :]).then_inc(s_st[r], 16)

            tiles(pool, step)
            for r in range(YR):
                pool.wait_ge(s_st[r], 16 * (NSLOT // YR))

        @block.scalar
        def _(act):
            def step(j, r, group):
                act.wait_ge(s_htp, j + 1)
                for b in range(2):
                    last = nc.scalar.activation(hT[:, 4 * b:4 * b + 4, :],
                                                HT_PS[:, b, :].rearrange("p (k t) -> p k t", k=4), ACT.Relu)
                last.then_inc(s_ht, 1)

            tiles(act, step)

        @block.tensor
        def _(pe):
            def transpose_x(j, r, group):
                pe.wait_ge(s_x[r], (group + 1) * 16)
                after(pe, s_xt, j)
                for k in range(DC):
                    last = nc.tensor.transpose(X_PS[:, k, :], xg[:, r, k * P:(k + 1) * P], ident[:, :])
                last.then_inc(s_xtp, 1)

            def first(j, r, e):
                pe.wait_ge(s_xt, j + 1)
                after(pe, s_hb, j)
                for f in range(2):
                    for k in range(DC):
                        last = nc.tensor.matmul(H_PS[:, f, :], xgT[:, r % 2, k, :],
                                                w1_sb[:, bass.ds(e * DC + k, 1), f * 512:(f + 1) * 512].rearrange("p a f -> p (a f)"),
                                                start=(k == 0), stop=(k == DC - 1))
                last.then_inc(s_hp, 1)

            def second(j, r, e):
                pe.wait_ge(s_ht, j + 1)
                after(pe, s_ys, j - 1)
                for k in range(FC):
                    last = nc.tensor.matmul(Y_PS[:, r % 2, :], hT[:, k, :],
                                            w2_sb[:, bass.ds(e * FC + k, 1), :].rearrange("p a d -> p (a d)"),
                                            start=(k == 0), stop=(k == FC - 1))
                last.then_inc(s_yp, 1)

            def transpose_h(j):
                pe.wait_ge(s_hb, j + 1)
                after(pe, s_ht, j)
                for k in range(FC):
                    last = nc.tensor.transpose(HT_PS[:, k // 4, (k % 4) * P:(k % 4 + 1) * P], hb[:, k * P:(k + 1) * P], ident[:, :])
                last.then_inc(s_htp, 1)

            def expert(j):
                return pe.value_load(tile_expert[0:1, bass.ds(j, 1)], min_val=0, max_val=E - 1)

            transpose_x(0, 0, 0)
            for r in range(TURN):
                first(r, r, expert(r))
                if r > 0:
                    second(r - 1, r - 1, expert(r - 1))
                transpose_h(r)
                if r + 1 < TURN:
                    transpose_x(r + 1, r + 1, 0)
            with pe.Fori(1, NSLOT // TURN) as group:
                for r in range(TURN):
                    j = group * TURN + r
                    if r == 0:
                        transpose_x(j, 0, group)
                    first(j, r, expert(j))
                    second(j - 1, (r - 1) % TURN, expert(j - 1))
                    transpose_h(j)
                    if r + 1 < TURN:
                        transpose_x(j + 1, r + 1, group)
            second(NSLOT - 1, TURN - 1, expert(NSLOT - 1))

        @block.vector
        def _(dve):
            def x_in(j, r, e):
                dve.wait_ge(s_xtp, j + 1)
                after(dve, s_hp, j - 1)
                for k in range(DC):
                    at = bass.ds(e * DC + k, 1)
                    last = nc.vector.tensor_scalar(xgT[:, r % 2, k, :], X_PS[:, k, :], gam[:, at], bet[:, at], ALU.mult, ALU.add)
                last.then_inc(s_xt, 1)

            def h_in(j, e):
                dve.wait_ge(s_hp, j + 1)
                after(dve, s_htp, j)
                nc.vector.tensor_tensor(hb[:, :], H_PS.rearrange("p b f -> p (b f)"),
                                        b1_sb[:, bass.ds(e, 1), :].rearrange("p a f -> p (a f)"), ALU.add).then_inc(s_hb, 1)

            def y_in(j, r, e, group):
                dve.wait_ge(s_yp, j + 1)
                after(dve, s_st[r], 16 * group)
                nc.vector.tensor_tensor(ysb[:, r, :], Y_PS[:, r % 2, :],
                                        b2_sb[:, bass.ds(e, 1), :].rearrange("p a d -> p (a d)"), ALU.add).then_inc(s_ys, 1)

            def expert(j):
                return dve.value_load(tile_expert[0:1, bass.ds(j, 1)], min_val=0, max_val=E - 1)

            x_in(0, 0, expert(0))
            for r in range(TURN):
                h_in(r, expert(r))
                if r > 0:
                    y_in(r - 1, r - 1, expert(r - 1), 0)
                if r + 1 < TURN:
                    x_in(r + 1, r + 1, expert(r + 1))
            def turn(group):
                for r in range(TURN):
                    j = group * TURN + r
                    if r == 0:
                        x_in(j, 0, expert(j))
                    h_in(j, expert(j))
                    y_in(j - 1, (r - 1) % TURN, expert(j - 1), group - 1 if r == 0 else group)
                    if r + 1 < TURN:
                        x_in(j + 1, r + 1, expert(j + 1))

            turn(1)
            with dve.Fori(2, NSLOT // TURN) as group:
                turn(group)
            y_in(NSLOT - 1, TURN - 1, expert(NSLOT - 1), NSLOT // TURN - 1)


def stage_d(nc, sem, slots, wts, mod_d, base_d, sloty_d, out):
    with ExitStack() as own:
        def sb(name, shape, dt=F32):
            return own.enter_context(nc.sbuf_tensor(name, shape, dt))

        BUF = 4
        gb = sb("gb", [P, NB, D])
        base = sb("base", [P, BUF, TI, D])
        y12 = sb("y12", [P, BUF, 2, TI, D])
        res = sb("res", [P, BUF, TI, D])
        s_gb = sem("gb_loaded")
        s_b = [sem(f"base_loaded{i}") for i in range(BUF)]
        s_g = [sem(f"y12_gathered{i}") for i in range(BUF)]
        s_link = sem("d_links")
        s_res = sem("res_ready")
        s_out = [sem(f"out_stored{i}") for i in range(BUF)]
        block = own.enter_context(nc.Block())

        def rows(t, n):
            return t[n * L:(n + 1) * L, :].rearrange("(i p) d -> p i d", p=P)

        @block.sync
        def _(sp):
            for n in range(NB):
                sp.dma_start(gb[:, n, :], mod_d[n:n + 1, 5 * D:6 * D].to_broadcast([P, D])).then_inc(s_gb, 16)
            for n in range(NB):
                if n >= BUF:
                    sp.wait_ge(s_res, n - BUF + 1)
                sp.dma_start(base[:, n % BUF, :, :], rows(base_d, n)).then_inc(s_b[n % BUF], 16)

        @block.gpsimd
        def _(pool):
            for n in range(NB):
                if n >= BUF:
                    pool.wait_ge(s_res, n - BUF + 1)
                for i in range(TI):
                    for k in range(2):
                        t = n * TI + i
                        pool.indirect_dma_start(y12[:, n % BUF, k, i, :], None, sloty_d,
                                                bass.IndirectOffsetOnAxis(ap=slots[:, k, t:t + 1], axis=0)
                                                ).then_inc(s_g[n % BUF], 16)

        @block.vector
        def _(dve):
            steps = [0]

            def link(ins):
                steps[0] += 1
                ins.then_inc(s_link, 1)
                dve.wait_ge(s_link, steps[0])

            dve.wait_ge(s_gb, 16 * NB)
            for n in range(NB):
                b = n % BUF
                dve.wait_ge(s_g[b], 16 * 2 * TI * (n // BUF + 1))
                if n >= BUF:
                    dve.wait_ge(s_out[b], 16 * (n // BUF))
                for i in range(TI):
                    t = n * TI + i
                    last = nc.vector.tensor_scalar(res[:, b, i, :], y12[:, b, 0, i, :], wts[:, 0, t:t + 1], None, ALU.mult)
                link(last)
                for i in range(TI):
                    t = n * TI + i
                    last = nc.vector.scalar_tensor_tensor(res[:, b, i, :], y12[:, b, 1, i, :], wts[:, 1, t:t + 1],
                                                          res[:, b, i, :], ALU.mult, ALU.add)
                link(last)
                link(nc.vector.tensor_tensor(res[:, b, :, :], res[:, b, :, :], gb[:, n, :].unsqueeze(1).to_broadcast([P, TI, D]), ALU.mult))
                dve.wait_ge(s_b[b], 16 * (n // BUF + 1))
                nc.vector.tensor_tensor(res[:, b, :, :], res[:, b, :, :], base[:, b, :, :], ALU.add).then_inc(s_res, 1)

        @block.scalar
        def _(act):
            for n in range(NB):
                act.wait_ge(s_res, n + 1)
                act.dma_start(rows(out, n), res[:, n % BUF, :, :]).then_inc(s_out[n % BUF], 16)
            for b in range(BUF):
                act.wait_ge(s_out[b], 16 * (NB // BUF))


def kernel(**inputs):
    import numpy as np
    import concourse.bacc as bacc
    from concourse.bass_utils import run_bass_kernel_spmd

    a = {k: np.asarray(v) for k, v in inputs.items()}

    def columns(v, chunks):
        return v.reshape(-1, chunks, P).transpose(2, 0, 1).reshape(P, -1)

    arrays = {
        "x": a["L0_attn_x"].reshape(NTOK, D),
        "norm_w": columns(a["L0_attn_norm_w"], DC),
        "W_in": a["L0_attn_W_in"],
        "conv_w": a["L0_attn_conv_w"].reshape(CH, P, K).transpose(1, 0, 2),
        "conv_b": columns(a["L0_attn_conv_b"], CH),
        "W_x": a["L0_attn_W_x"],
        "W_dt": a["L0_attn_W_dt"],
        "b_dt": columns(a["L0_attn_b_dt"], CH),
        "A_log": a["L0_attn_A_log"].reshape(CH, P, NS).transpose(1, 0, 2),
        "D_skip": columns(a["L0_attn_D_skip"], CH),
        "W_out": a["L0_attn_W_out"],
        "Wg": a["L0_ffn_Wg"],
        "gamma": columns(a["L0_ffn_gamma"], DC),
        "beta": columns(a["L0_ffn_beta"], DC),
        "W1": a["L0_ffn_W1"],
        "b1": a["L0_ffn_b1"].reshape(1, E * F),
        "W2": a["L0_ffn_W2"],
        "b2": a["L0_ffn_b2"].reshape(1, E * D),
        "cT": a["L0_c"].T,
        "wmod": a["L0_wmod"],
    }
    arrays = {f"in_{k}": np.ascontiguousarray(v) for k, v in arrays.items()}
    nc = bacc.Bacc("TRN2", target_bir_lowering=False, num_devices=1)
    args = {k[3:]: nc.dram_tensor(k, v.shape, mybir.dt.from_np(v.dtype), kind="ExternalInput").ap()
            for k, v in arrays.items()}
    out = nc.dram_tensor("out", (NTOK, D), F32, kind="ExternalOutput").ap()
    adaln_kernel(nc, **args, out=out)
    r = run_bass_kernel_spmd(nc, [arrays], core_ids=[0])
    return r.results[0]["out"].reshape(NB, L, D)
```

```python
import concourse.bass as bass
from concourse import mybir
from contextlib import ExitStack

F32 = mybir.dt.float32
U32 = mybir.dt.uint32
I32 = mybir.dt.int32
ALU = mybir.AluOpType
ACT = mybir.ActivationFunctionType
AX = mybir.AxisListType

NB, L, D = 8, 512, 256
DIN, NS, R, K = 512, 16, 64, 4
E, F = 8, 1024
P = 128
NTOK = NB * L
CH = DIN // P
TI = L // P
DC = D // P
FC = F // P
XD = R + 2 * NS
NT = NTOK // P
NSLOT = 2 * NTOK // P + E
UNITS = NS * CH
PAD = K - 1
RING = 2 * CH
LN_EPS, FFN_EPS = 1e-5, 1e-6
P_LINKS, O_LINKS = 3, 17


def adaln_kernel(nc, x, norm_w, W_in, conv_w, conv_b, W_x, W_dt, b_dt, A_log, D_skip, W_out,
                 Wg, gamma, beta, W1, b1, W2, b2, cT, wmod, out):
    def dram(name, shape):
        return nc.dram_tensor(name, shape, F32, kind="Internal").ap()

    mod_d = dram("mod_d", (NB, 6 * D))
    b_d = dram("b_d", (NB, NS, L))
    xhat_d = dram("xhat_d", (NTOK, D))
    h_d = dram("h_d", (NTOK, D))
    base_d = dram("base_d", (NTOK, D))
    slotx_d = dram("slotx_d", (NSLOT * P, D))
    sloty_d = dram("sloty_d", (NSLOT * P, D))

    ctx = ExitStack()
    with ctx:
        def sb(name, shape, dt=F32, stack=ctx):
            return stack.enter_context(nc.sbuf_tensor(name, shape, dt))

        def sem(name):
            return ctx.enter_context(nc.semaphore(name))

        ident = sb("ident", [P, P])
        oh = sb("oh", [P, 2, NT, E])
        wts = sb("wts", [P, 2, NT])
        slots = sb("slots", [P, 2, NT], U32)
        tile_expert = sb("tile_expert", [P, NSLOT], I32)
        psum = ctx.enter_context(nc.psum_tensor("psum", [P, 8, 512], F32))
        T = psum[:, 0:4, :]
        Q = psum[:, 4:8, :]

        stage_a(nc, ctx, sem, ident, oh, wts, T, Q, mod_d, b_d, h_d, xhat_d, base_d, slotx_d,
                x, norm_w, W_in, conv_w, conv_b, W_x, W_dt, b_dt, A_log, D_skip, W_out, Wg, cT, wmod)
        with ExitStack() as held:
            w1_sb = sb("w1_sb", [P, E * DC, F], stack=held)
            w2_sb = sb("w2_sb", [P, E * FC, D], stack=held)
            b1_sb = sb("b1_sb", [P, E, F], stack=held)
            b2_sb = sb("b2_sb", [P, E, D], stack=held)
            gam = sb("gam", [P, E * DC], stack=held)
            bet = sb("bet", [P, E * DC], stack=held)
            weights_in = sem("weights_in")
            stage_b(nc, sem, ident, oh, slots, tile_expert, psum, xhat_d, slotx_d,
                    w1_sb, w2_sb, b1_sb, b2_sb, gam, bet, W1, W2, b1, b2, gamma, beta, weights_in)
            stage_c(nc, sem, ident, tile_expert, psum, slotx_d, sloty_d, w1_sb, w2_sb, b1_sb, b2_sb, gam, bet)
        stage_d(nc, sem, slots, wts, mod_d, base_d, sloty_d, out)


def stage_a(nc, ctx, sem, ident, oh, wts, T, Q, mod_d, b_d, h_d, xhat_d, base_d, slotx_d,
            x, norm_w, W_in, conv_w, conv_b, W_x, W_dt, b_dt, A_log, D_skip, W_out, Wg, cT, wmod):
    with ExitStack() as own:
        def sb(name, shape, dt=F32):
            return own.enter_context(nc.sbuf_tensor(name, shape, dt))

        win = sb("win", [P, DC, 2 * DIN])
        wx = sb("wx", [P, CH, XD])
        wdt = sb("wdt", [R, DIN])
        wout = sb("wout", [P, CH, D])
        wg = sb("wg", [P, DC, E])
        nw = sb("nw", [P, DC])
        cw = sb("cw", [P, CH, K])
        cb = sb("cb", [P, CH])
        bdt = sb("bdt", [P, CH])
        dsk = sb("dsk", [P, CH])
        aneg = sb("aneg", [P, CH, NS])
        iota8 = sb("iota8", [P, E])
        mhalf = sb("mhalf", [P, TI])
        xin = sb("xin", [P, TI, D])
        hmod = sb("hmod", [P, TI, D])
        xres = sb("xres", [P, TI, D])
        hres = sb("hres", [P, TI, D])
        modp = sb("modp", [P, 2, D])
        modo = sb("modo", [P, 4, D])
        xn = sb("xn", [P, TI, D])
        xnT = sb("xnT", [P, DC, L])
        xipad = sb("xipad", [P, CH, PAD + L])
        xc = sb("xc", [P, 2, CH, L])
        sz = sb("sz", [P, 2, CH, L])
        xd = sb("xd", [XD, L])
        ct = sb("ct", [P, 2, TI, NS])
        dt = sb("dt", [P, 2, CH, L])
        u = sb("u", [P, 2, CH, L])
        brep = sb("brep", [P, 4, L])
        dA = sb("dA", [P, RING, L])
        dBu = sb("dBu", [P, RING, L])
        hs = sb("hs", [P, 2, CH, L])
        y = sb("y", [P, TI, DIN])
        gT = sb("gT", [P, CH, L])
        xfT = gT
        x1 = sb("x1", [P, TI, D])
        xf = sb("xf", [P, TI, D])
        xh = hres
        bs = sb("bs", [P, 3, TI, 6])
        mv = sb("mv", [P, 3, TI, 2])
        rs = sb("rs", [P, 4, TI])
        tmp = sb("tmp", [P, 4, TI])
        ssq = sb("ssq", [P, TI])
        sc = sb("sc", [P, TI, E])
        top = sb("top", [P, TI, 8])
        tix = sb("tix", [P, TI, 8], U32)
        tif = sb("tif", [P, TI, 2])
        vd = sb("vd", [P, 4, TI])
        spare = sb("spare", [P, 1])
        eps = sb("eps", [P, 2, TI])
        cts = xn[:, 0, 0:DC * NB].rearrange("p (k b) -> p k b", k=DC)
        wmod_sb = hs[:, :, :, :].rearrange("p a c l -> p (a c l)")[:, 0:DC * 6 * D].rearrange("p (k n) -> p k n", k=DC)
        m8 = y[0:NB, :, :].rearrange("p a b -> p (a b)")[:, 0:6 * D]
        m8n = gT[0:NB, 0, 0:2 * D].rearrange("p (a d) -> p a d", a=2)
        zrow = dt[:, 0, :, :].rearrange("p c l -> p (c l)")

        s_w = sem("weights_loaded")
        s_ct = sem("c_loaded")
        s_id = sem("ident_steps")
        s_csilu = sem("c_silu")
        s_modps = sem("mod_ps")
        s_m8 = sem("mod_rows_copied")
        s_modr = sem("mod_rows_ready")
        s_modst = sem("mod_stored")
        s_const = sem("constants_ready")
        s_aexp = sem("a_exp")
        s_zero = sem("slot_rows_zeroed")
        s_pload = sem("x_and_modp_loaded")
        s_hst = sem("h_stored")
        s_oload = sem("modo_xres_hres_loaded")
        s_ln1 = sem("ln1_stats")
        s_ln1r = sem("ln1_rstd")
        s_h = sem("h_ready")
        s_sq = sem("square_sums")
        s_rms = sem("rms_rstd")
        s_xn = sem("xn_ready")
        s_xntp = sem("xnT_ps")
        s_xnt = sem("xnT_ready")
        s_xip = sem("xi_ps")
        s_xi = sem("xi_ready")
        s_zp = sem("z_ps")
        s_z = sem("z_ready")
        s_tap = sem("conv_taps")
        s_xc = sem("xc_ready")
        s_xdp = sem("xd_ps")
        s_xd = sem("xd_ready")
        s_bst = sem("b_stored")
        s_cp = sem("c_ps")
        s_c = sem("c_ready")
        s_dtp = sem("dt_ps")
        s_sp = sem("softplus_parts")
        s_dt = sem("dt_ready")
        s_u = sem("u_ready")
        s_br = [sem(f"brep_loaded{i}") for i in range(4)]
        s_dA = sem("dA_ready")
        s_dBu = sem("dBu_ready")
        s_scan = sem("scanned")
        s_tr = sem("states_transposed")
        s_y = sem("y_added")
        s_yT = sem("yT_ps")
        s_g = sem("skip_added")
        s_gate = sem("gated")
        s_op = sem("out_ps")
        s_x1 = sem("x1_ready")
        s_ln2r = sem("ln2_rstd")
        s_xf = sem("xf_ready")
        s_ln3r = sem("ln3_rstd")
        s_xh = sem("xhat_ready")
        s_xhst = sem("xhat_stored")
        s_xftp = sem("xfT_ps")
        s_xft = sem("xfT_ready")
        s_scp = sem("scores_ps")
        s_vd = sem("top_difference")
        s_ve = sem("top_exp")
        s_base = sem("base_ready")
        s_bast = sem("base_stored")
        s_act = sem("act_links")

        def after(eng, s, value):
            if not (isinstance(value, int) and value <= 0):
                eng.wait_ge(s, value)

        def immediate(eng):
            eng.wait_ge(s_id, 2)

        def sequences(eng, prologue, body, epilogue):
            prologue()
            body(0, 0, False, True, True)
            with eng.Fori(0, (NB - 4) // 2) as turn:
                body(2 * turn + 1, 1, True, True, True)
                body(2 * turn + 2, 0, True, True, True)
            body(NB - 3, 1, True, True, True)
            body(NB - 2, 0, True, True, False)
            body(NB - 1, 1, True, False, False)
            epilogue()

        block = own.enter_context(nc.Block())

        @block.sync
        def _(sp):
            sp.dma_start(cts, cT.rearrange("(k p) b -> p k b", p=P)).then_inc(s_ct, 16)
            sp.dma_start(wmod_sb, wmod.rearrange("(k p) n -> p k n", p=P)).then_inc(s_ct, 16)
            for dst, src in ((win[:, :, :], W_in.rearrange("(k p) n -> p k n", p=P)),
                             (wx[:, :, :], W_x.rearrange("(k p) n -> p k n", p=P)),
                             (wdt[:, :], W_dt), (wout[:, :, :], W_out.rearrange("(k p) n -> p k n", p=P)),
                             (wg[:, :, :], Wg.rearrange("(k p) n -> p k n", p=P)),
                             (nw[:, :], norm_w), (cw[:, :, :], conv_w), (cb[:, :], conv_b),
                             (bdt[:, :], b_dt), (dsk[:, :], D_skip), (aneg[:, :, :], A_log)):
                sp.dma_start(dst, src).then_inc(s_w, 16)
            sp.wait_ge(s_const, 1)
            zsrc = zrow.rearrange("p (a d) -> p a d", d=D)
            per = CH * L // D
            for k in range(NSLOT // per):
                sp.dma_start(slotx_d[k * per * P:(k + 1) * per * P, :].rearrange("(p a) d -> p a d", p=P),
                             zsrc).then_inc(s_zero, 16)
            sp.wait_ge(s_modr, 1)
            sp.dma_start(mod_d, m8).then_inc(s_modst, 16)
            sp.wait_ge(s_modst, 16)
            sp.wait_ge(s_zero, 16 * (NSLOT // per))

            def mod_rows(n, first, count, dst):
                rows = mod_d[bass.ds(n, 1), first * D:(first + count) * D]
                return dict(out=dst.rearrange("p m d -> p (m d)"), in_=rows.to_broadcast([P, count * D]))

            def rows(t, n):
                return t[bass.ds(n * L, L), :].rearrange("(i p) d -> p i d", p=P)

            def load(n):
                immediate(sp)
                after(sp, s_h, n)
                sp.dma_start(xin[:, :, :], rows(x, n)).then_inc(s_pload, 16)
                sp.dma_start(**mod_rows(n, 0, 2, modp[:, :, :])).then_inc(s_pload, 16)

            def store_h(n):
                immediate(sp)
                sp.wait_ge(s_h, n + 1)
                sp.dma_start(rows(h_d, n), hmod[:, :, :]).then_inc(s_hst, 16)

            def load_o(n):
                immediate(sp)
                sp.wait_ge(s_hst, 16 * (n + 1))
                after(sp, s_base, n)
                sp.dma_start(**mod_rows(n, 2, 4, modo[:, :, :])).then_inc(s_oload, 16)
                sp.dma_start(xres[:, :, :], rows(x, n)).then_inc(s_oload, 16)
                sp.dma_start(hres[:, :, :], rows(h_d, n)).then_inc(s_oload, 16)

            def load_brep(n, s):
                immediate(sp)
                if s == 0:
                    sp.wait_ge(s_bst, 16 * (n + 1))
                after(sp, s_dBu, n * UNITS + 4 * (s - 3))
                sp.dma_start(brep[:, s % 4, :], b_d[bass.ds(n, 1), s, :].to_broadcast([P, L])).then_inc(s_br[s % 4], 16)

            def store_xhat(n):
                immediate(sp)
                sp.wait_ge(s_xh, n + 1)
                sp.dma_start(rows(xhat_d, n), xh[:, :, :]).then_inc(s_xhst, 16)

            def store_base(n):
                immediate(sp)
                sp.wait_ge(s_base, n + 1)
                sp.dma_start(rows(base_d, n), x1[:, :, :]).then_inc(s_bast, 16)

            def prologue():
                load(0)
                store_h(0)
                load(1)
                store_h(1)

            def body(n, p, has_o, has_p, has_r):
                for s in range(NS):
                    load_brep(n, s)
                    if not has_o and s == 1:
                        load_o(n)
                    if has_r and s == 0:
                        load(n + 2)
                    if has_r and s == 10:
                        store_h(n + 2)
                    if has_o and s == 13:
                        store_xhat(n - 1)
                    if has_o and s == 15:
                        immediate(sp)
                        sp.wait_ge(s_xhst, 16 * n)
                        store_base(n - 1)
                        load_o(n)

            def epilogue():
                store_xhat(NB - 1)
                store_base(NB - 1)
                sp.wait_ge(s_xhst, 16 * NB)
                sp.wait_ge(s_bast, 16 * NB)

            sequences(sp, prologue, body, epilogue)

        @block.gpsimd
        def _(pool):
            pool.memset(zrow, 0.0)
            pool.memset(mhalf[:, :], -0.5)
            pool.memset(eps[:, 0, :], LN_EPS)
            pool.memset(eps[:, 1, :], FFN_EPS)
            pool.iota(iota8[:, :], [[1, E]], base=0, channel_multiplier=0, allow_small_or_imprecise_dtypes=True)
            pool.memset(xipad[:, :, 0:PAD], 0.0).then_inc(s_const, 1)
            pool.memset(ident[:, :], 0.0).then_inc(s_id, 1)
            pool.wait_ge(s_id, 1)
            pool.affine_select(out=ident[:, :], in_=ident[:, :], compare_op=ALU.not_equal, fill=1.0, base=0,
                               pattern=[[-1, P]], channel_multiplier=1).then_inc(s_id, 1)

            def ln1(n):
                pool.wait_ge(s_ln1, n + 1)
                rstd_p(n, 0, mv[:, 0, :, 1], eps[:, 0, :], s_ln1r)

            def rms(n):
                pool.wait_ge(s_sq, n + 1)
                rstd_p(n, 3, ssq[:, :], eps[:, 0, :], s_rms)

            pl, ol = sem("pool_links_p"), sem("pool_links_o")

            def rstd_on(s, count, which, src, add, ready):
                nc.gpsimd.tensor_tensor(tmp[:, which, :], src, add, ALU.add).then_inc(s, 1)
                pool.wait_ge(s, count)
                nc.gpsimd.tensor_tensor(rs[:, which, :], tmp[:, which, :], mhalf[:, :], ALU.pow).then_inc(ready, 1)

            def rstd_p(n, which, src, add, ready):
                rstd_on(pl, 2 * n + (1 if which == 0 else 2), which, src, add, ready)

            def gate(n, p):
                for c in range(CH):
                    pool.wait_ge(s_g, n * CH + c + 1)
                    nc.gpsimd.tensor_tensor(gT[:, c, :], gT[:, c, :], sz[:, p, c, :], ALU.mult).then_inc(s_gate, 1)

            def ln2(n):
                pool.wait_ge(s_x1, n + 1)
                rstd_on(ol, 2 * n + 1, 1, mv[:, 1, :, 1], eps[:, 0, :], s_ln2r)

            def ln3(n):
                pool.wait_ge(s_xf, n + 1)
                rstd_on(ol, 2 * n + 2, 2, mv[:, 2, :, 1], eps[:, 1, :], s_ln3r)

            def inputs(n, p, s):
                pool.wait_ge(s_br[s % 4], 16 * (n * (NS // 4) + s // 4 + 1))
                for c in range(CH):
                    i = s * CH + c
                    if s == 0:
                        pool.wait_ge(s_u, n * CH + c + 1)
                    after(pool, s_scan, n * UNITS + i - RING + 1)
                    nc.gpsimd.tensor_tensor(dBu[:, i % RING, :], u[:, p, c, :], brep[:, s % 4, :], ALU.mult).then_inc(s_dBu, 1)

            def prologue():
                for n in range(2):
                    ln1(n)
                    rms(n)

            def body(n, p, has_o, has_p, has_r):
                for s in range(NS):
                    inputs(n, p, s)
                    if has_o and s == 2:
                        gate(n - 1, 1 - p)
                    if has_r and s == 4:
                        ln1(n + 2)
                    if has_o and s == 6:
                        ln2(n - 1)
                    if has_o and s == 8:
                        ln3(n - 1)
                    if has_r and s == 10:
                        rms(n + 2)

            def epilogue():
                gate(NB - 1, 1)
                ln2(NB - 1)
                ln3(NB - 1)

            sequences(pool, prologue, body, epilogue)

        @block.scalar
        def _(act):
            act.wait_ge(s_ct, 32)
            nc.scalar.activation(cts, cts, ACT.Silu).then_inc(s_csilu, 1)
            for j in range(3):
                act.wait_ge(s_modps, j + 1)
                nc.scalar.activation(m8[:, j * 512:(j + 1) * 512], Q[0:NB, j, :], ACT.Copy).then_inc(s_m8, 1)
            act.wait_ge(s_w, 16 * 11)
            nc.scalar.activation(aneg[:, :, :], aneg[:, :, :], ACT.Exp).then_inc(s_aexp, 1)
            act.wait_ge(s_aexp, 1)
            nc.scalar.activation(aneg[:, :, :], aneg[:, :, :], ACT.Copy, scale=-1.0).then_inc(s_aexp, 1)
            act.wait_ge(s_aexp, 2)

            def squares(n):
                act.wait_ge(s_h, n + 1)
                after(act, s_xntp, n)
                for i in range(TI):
                    last = nc.scalar.activation(xn[:, i, :], hmod[:, i, :], ACT.Square, scale=float(D) ** -0.5, accum_out=ssq[:, i:i + 1])
                last.then_inc(s_sq, 1)

            def norm(n):
                act.wait_ge(s_rms, n + 1)
                for i in range(TI):
                    last = nc.scalar.activation(xn[:, i, :], hmod[:, i, :], ACT.Copy, scale=rs[:, 3, i:i + 1])
                last.then_inc(s_xn, 1)

            def norm_t(n):
                act.wait_ge(s_xntp, n + 1)
                for c in range(DC):
                    last = nc.scalar.activation(xnT[:, c, :], Q[:, 2 + c, :], ACT.Copy, scale=nw[:, c:c + 1])
                last.then_inc(s_xnt, 1)

            def conv_in(n, chunks):
                for c in chunks:
                    act.wait_ge(s_xip, n * CH + c + 1)
                    nc.scalar.activation(xipad[:, c, PAD:], Q[:, (c + 2) % 4, :], ACT.Copy).then_inc(s_xi, 1)

            def silus(n, p):
                for c in range(CH):
                    act.wait_ge(s_zp, n * CH + c + 1)
                    nc.scalar.activation(sz[:, p, c, :], Q[:, c, :], ACT.Silu).then_inc(s_z, 1)
                for c in range(CH):
                    act.wait_ge(s_tap, n * CH * K + CH * (K - 1) + c + 1)
                    nc.scalar.activation(xc[:, p, c, :], xc[:, p, c, :], ACT.Silu).then_inc(s_xc, 1)

            def xd_copy(n):
                act.wait_ge(s_xdp, n + 1)
                after(act, s_bst, 16 * n)
                nc.scalar.activation(xd[:, :], Q[0:XD, 0, :], ACT.Copy).then_inc(s_xd, 1)
                act.wait_ge(s_xd, n + 1)
                act.dma_start(b_d[bass.ds(n, 1), :, :].rearrange("a s l -> (a s) l"), xd[R:R + NS, :]).then_inc(s_bst, 16)

            def c_copy(n, p):
                act.wait_ge(s_cp, n + 1)
                nc.scalar.activation(ct[:, p, :, :], Q[:, 1, 0:TI * XD].rearrange("p (i n) -> p i n", i=TI)[:, :, R + NS:XD],
                                     ACT.Copy).then_inc(s_c, 1)

            def softplus(n, p):
                for c in range(CH):
                    q = Q[:, (c + 2) % 4, :]
                    act.wait_ge(s_dtp, n * CH + c + 1)
                    nc.scalar.activation(u[:, p, c, :], q, ACT.Abs, bias=bdt[:, c:c + 1]).then_inc(s_act, 1)
                    nc.scalar.activation(dt[:, p, c, :], q, ACT.Relu, bias=bdt[:, c:c + 1])
                for c in range(CH):
                    act.wait_ge(s_act, n * 2 * CH + c + 1)
                    nc.scalar.activation(u[:, p, c, :], u[:, p, c, :], ACT.Exp, scale=-1.0).then_inc(s_act, 1)
                for c in range(CH):
                    act.wait_ge(s_act, n * 2 * CH + CH + c + 1)
                    nc.scalar.activation(u[:, p, c, :], u[:, p, c, :], ACT.Ln, bias=1.0).then_inc(s_sp, 1)

            def decays(n, p, s):
                for c in range(CH):
                    i = s * CH + c
                    if s == 0:
                        act.wait_ge(s_dt, n * CH + c + 1)
                    after(act, s_scan, n * UNITS + i - RING + 1)
                    nc.scalar.activation(dA[:, i % RING, :], dt[:, p, c, :], ACT.Exp,
                                         scale=aneg[:, c, s:s + 1]).then_inc(s_dA, 1)

            def scores_in(n):
                act.wait_ge(s_xftp, n + 1)
                for c in range(DC):
                    last = nc.scalar.activation(xfT[:, c, :], Q[:, 2 + c, :], ACT.Copy)
                last.then_inc(s_xft, 1)

            def top_exp(n):
                act.wait_ge(s_vd, n + 1)
                nc.scalar.activation(vd[:, 1, :], vd[:, 0, :], ACT.Exp).then_inc(s_ve, 1)

            def prologue():
                squares(0)
                norm(0)
                norm_t(0)
                squares(1)
                norm(1)
                conv_in(0, range(CH))
                silus(0, 0)
                xd_copy(0)
                c_copy(0, 0)
                softplus(0, 0)

            def body(n, p, has_o, has_p, has_r):
                for s in range(NS):
                    decays(n, p, s)
                    if has_p and s == 4:
                        norm_t(n + 1)
                    if has_p and s in (6, 7):
                        conv_in(n + 1, (0, 1) if s == 6 else (2, 3))
                    if has_r and s == 8:
                        squares(n + 2)
                    if has_o and s == 9:
                        scores_in(n - 1)
                    if has_r and s == 10:
                        norm(n + 2)
                    if has_p and s == 11:
                        silus(n + 1, 1 - p)
                    if has_o and s == 12:
                        top_exp(n - 1)
                    if has_p and s == 13:
                        xd_copy(n + 1)
                    if has_p and s == 14:
                        c_copy(n + 1, 1 - p)
                        softplus(n + 1, 1 - p)

            def epilogue():
                scores_in(NB - 1)
                top_exp(NB - 1)

            sequences(act, prologue, body, epilogue)

        @block.tensor
        def _(pe):
            pe.wait_ge(s_csilu, 1)
            for j in range(3):
                for k in range(DC):
                    last = nc.tensor.matmul(Q[0:NB, j, :], cts[:, k, :], wmod_sb[:, k, j * 512:(j + 1) * 512],
                                            start=(k == 0), stop=(k == DC - 1))
                last.then_inc(s_modps, 1)
            pe.wait_ge(s_id, 2)
            pe.wait_ge(s_w, 16 * 11)
            pe.wait_ge(s_m8, 3)

            def norm_t(n, skipped):
                pe.wait_ge(s_xn, n + 1)
                after(pe, s_g, skipped * CH)
                for c in range(DC):
                    for i in range(TI):
                        last = nc.tensor.transpose(Q[:, 2 + c, i * P:(i + 1) * P], xn[:, i, c * P:(c + 1) * P], ident[:, :])
                last.then_inc(s_xntp, 1)

            def in_proj_x(n, chunks):
                pe.wait_ge(s_xnt, n + 1)
                for c in chunks:
                    for k in range(DC):
                        last = nc.tensor.matmul(Q[:, (c + 2) % 4, :], win[:, k, c * P:(c + 1) * P], xnT[:, k, :],
                                                start=(k == 0), stop=(k == DC - 1))
                    last.then_inc(s_xip, 1)

            def in_proj_z(n, chunks):
                for c in chunks:
                    pe.wait_ge(s_xi, n * CH + (c + 2) % 4 + 1)
                    for k in range(DC):
                        last = nc.tensor.matmul(Q[:, c, :], win[:, k, DIN + c * P:DIN + (c + 1) * P], xnT[:, k, :],
                                                start=(k == 0), stop=(k == DC - 1))
                    last.then_inc(s_zp, 1)

            def x_proj(n, p):
                pe.wait_ge(s_z, n * CH + CH)
                for c in range(CH):
                    pe.wait_ge(s_xc, n * CH + c + 1)
                    last = nc.tensor.matmul(Q[0:XD, 0, :], wx[:, c, :], xc[:, p, c, :],
                                            start=(c == 0), stop=(c == CH - 1))
                last.then_inc(s_xdp, 1)

            def dt_proj(n):
                pe.wait_ge(s_xd, n + 1)
                for i in range(TI):
                    last = nc.tensor.transpose(Q[:, 1, i * XD:(i + 1) * XD], xd[:, i * P:(i + 1) * P], ident[0:XD, 0:XD])
                last.then_inc(s_cp, 1)
                for c in range(CH):
                    if c == 3:
                        pe.wait_ge(s_c, n + 1)
                    nc.tensor.matmul(Q[:, (c + 2) % 4, :], wdt[:, c * P:(c + 1) * P], xd[0:R, :],
                                     start=True, stop=True).then_inc(s_dtp, 1)

            def states(n, s):
                pe.wait_ge(s_scan, n * UNITS + CH * (s + 1))
                for i in range(TI):
                    after(pe, s_y, n * UNITS + TI * (s - 1) + i + 1)
                    for c in range(CH):
                        last = nc.tensor.transpose(T[:, i, c * P:(c + 1) * P], hs[:, s % 2, c, i * P:(i + 1) * P], ident[:, :])
                    last.then_inc(s_tr, 1)

            def y_t(n, projected):
                pe.wait_ge(s_y, (n + 1) * UNITS)
                pe.wait_ge(s_sp, projected * CH)
                for c in range(CH):
                    for i in range(TI):
                        last = nc.tensor.transpose(Q[:, c, i * P:(i + 1) * P], y[:, i, c * P:(c + 1) * P], ident[:, :])
                    last.then_inc(s_yT, 1)

            def out_proj(n):
                pe.wait_ge(s_gate, (n + 1) * CH)
                for i in range(TI):
                    for c in range(CH):
                        last = nc.tensor.matmul(Q[:, i // 2, (i % 2) * D:(i % 2 + 1) * D], gT[:, c, i * P:(i + 1) * P],
                                                wout[:, c, :], start=(c == 0), stop=(c == CH - 1))
                last.then_inc(s_op, 1)

            def xf_t(n):
                pe.wait_ge(s_xf, n + 1)
                for c in range(DC):
                    for i in range(TI):
                        last = nc.tensor.transpose(Q[:, 2 + c, i * P:(i + 1) * P], xf[:, i, c * P:(c + 1) * P], ident[:, :])
                last.then_inc(s_xftp, 1)

            def scores(n):
                pe.wait_ge(s_xft, n + 1)
                for i in range(TI):
                    for c in range(DC):
                        last = nc.tensor.matmul(Q[:, 2, i * E:(i + 1) * E], xfT[:, c, i * P:(i + 1) * P], wg[:, c, :],
                                                start=(c == 0), stop=(c == DC - 1))
                last.then_inc(s_scp, 1)

            def prologue():
                norm_t(0, 0)
                in_proj_x(0, range(CH))
                in_proj_z(0, range(CH))
                x_proj(0, 0)
                dt_proj(0)

            def body(n, p, has_o, has_p, has_r):
                if has_o:
                    y_t(n - 1, n + 1)
                for s in range(NS):
                    states(n, s)
                    if has_p and s == 1:
                        norm_t(n + 1, n)
                    if has_o and s == 2:
                        out_proj(n - 1)
                    if has_p and s == 3:
                        in_proj_x(n + 1, (0, 1))
                    if has_p and s == 4:
                        after(pe, s_x1, n)
                        in_proj_x(n + 1, (2, 3))
                    if has_o and s == 6:
                        after(pe, s_xi, (n + 1) * CH + 2 if has_p else 0)
                        xf_t(n - 1)
                    if has_p and s == 7:
                        in_proj_z(n + 1, (0, 1))
                    if has_o and s == 7:
                        scores(n - 1)
                    if has_p and s == 9:
                        after(pe, s_vd, n)
                        in_proj_z(n + 1, (2, 3))
                    if has_p and s == 10:
                        x_proj(n + 1, 1 - p)
                    if has_p and s == 11:
                        dt_proj(n + 1)

            def epilogue():
                y_t(NB - 1, NB)
                out_proj(NB - 1)
                xf_t(NB - 1)
                scores(NB - 1)

            sequences(pe, prologue, body, epilogue)

        @block.vector
        def _(dve):
            own_p, own_o = sem("dve_links_p"), sem("dve_links_o")
            count = {"p": 0, "o": 0}

            def link(ins, kind, n):
                s, per = (own_p, P_LINKS) if kind == "p" else (own_o, O_LINKS)
                ins.then_inc(s, 1)
                count[kind] += 1
                dve.wait_ge(s, n * per + count[kind])

            def counted(p_links, o_links):
                assert count == {"p": p_links, "o": o_links}, count
                count["p"] = count["o"] = 0

            dve.wait_ge(s_m8, 3)
            m6 = m8.rearrange("p (m d) -> p m d", m=6)
            setup = sem("dve_setup")
            steps = [0]

            def then(ins):
                steps[0] += 1
                ins.then_inc(setup, 1)
                dve.wait_ge(setup, steps[0])

            for m in (1, 4):
                then(nc.vector.tensor_scalar(m6[:, m, :], m6[:, m, :], 1.0, None, ALU.add))
            for m in (2, 5):
                a, b = m8n[:, 0, :], m8n[:, 1, :]
                then(nc.vector.tensor_scalar(a, m6[:, m, :], -1.0, None, ALU.mult))
                then(nc.vector.tensor_tensor(a, a, m6[:, m, :], ALU.max))
                then(nc.vector.tensor_scalar(b, m6[:, m, :], 0.0, 2.0, ALU.is_ge, ALU.mult))
                then(nc.vector.tensor_scalar(b, b, -1.0, None, ALU.add))
                then(nc.vector.tensor_scalar(a, a, 0.25, None, ALU.max))
                then(nc.vector.tensor_tensor(m6[:, m, :], a, b, ALU.mult))
            nc.vector.tensor_copy(tif[0:1, 0, 0:1], m6[0:1, 0, 0:1]).then_inc(s_modr, 1)
            dve.wait_ge(s_const, 1)
            dve.wait_ge(s_w, 16 * 11)
            dve.wait_ge(s_modst, 16)
            dve.wait_ge(s_zero, 16 * (NSLOT // (CH * L // D)))

            def carrier():
                nc.vector.memset(spare[:, :], 0.0)

            def stats(kind, n, src, which, ready):
                for i in range(TI):
                    last = nc.vector.bn_stats(bs[:, which, i, :], src[:, i, :])
                link(last, kind, n)
                carrier()
                for i in range(TI):
                    last = nc.vector.bn_aggr(mv[:, which, i, :], bs[:, which, i, :])
                if ready is not None:
                    last.then_inc(ready, 1)
                return last

            def normalise(dst, src, which):
                for i in range(TI):
                    last = nc.vector.tensor_scalar(dst[:, i, :], src[:, i, :], mv[:, which, i, 0:1], rs[:, which, i:i + 1],
                                                   ALU.subtract, ALU.mult)
                return last

            def rows(m):
                return m.unsqueeze(1).to_broadcast([P, TI, D])

            def p_stats(n):
                dve.wait_ge(s_pload, 32 * (n + 1))
                stats("p", n, xin, 0, s_ln1)

            def p_mod(n):
                h = hmod[:, :, :]
                dve.wait_ge(s_ln1r, n + 1)
                after(dve, s_hst, 16 * n)
                after(dve, s_xn, n)
                link(normalise(h, xin, 0), "p", n)
                link(nc.vector.tensor_tensor(h, h, rows(modp[:, 1, :]), ALU.mult), "p", n)
                nc.vector.tensor_tensor(h, h, rows(modp[:, 0, :]), ALU.add).then_inc(s_h, 1)

            def conv(n, p, taps):
                for k in taps:
                    for c in range(CH):
                        src = xipad[:, c, k:k + L]
                        dst = xc[:, p, c, :]
                        if k == 0:
                            dve.wait_ge(s_xi, n * CH + c + 1)
                            ins = nc.vector.tensor_scalar(dst, src, cw[:, c, 0:1], cb[:, c:c + 1], ALU.mult, ALU.add)
                        else:
                            dve.wait_ge(s_tap, n * CH * K + CH * (k - 1) + c + 1)
                            ins = nc.vector.scalar_tensor_tensor(dst, src, cw[:, c, k:k + 1], dst, ALU.mult, ALU.add)
                        ins.then_inc(s_tap, 1)

            def dt_u(n, p):
                for c in range(CH):
                    dve.wait_ge(s_sp, n * CH + c + 1)
                    nc.vector.tensor_tensor(dt[:, p, c, :], dt[:, p, c, :], u[:, p, c, :], ALU.add).then_inc(s_dt, 1)
                for c in range(CH):
                    dve.wait_ge(s_dt, n * CH + c + 1)
                    nc.vector.tensor_tensor(u[:, p, c, :], dt[:, p, c, :], xc[:, p, c, :], ALU.mult).then_inc(s_u, 1)

            def scan(n, s, c):
                i = s * CH + c
                if c == 0 and s >= 2:
                    dve.wait_ge(s_tr, n * UNITS + TI * (s - 1))
                elif c == 0:
                    after(dve, s_tr, (n - 1) * UNITS + TI * (NS - 1 + s))
                dve.wait_ge(s_dA, n * UNITS + i + 1)
                dve.wait_ge(s_dBu, n * UNITS + i + 1)
                nc.vector.tensor_tensor_scan(hs[:, s % 2, c, :], dA[:, i % RING, :], dBu[:, i % RING, :], 0.0,
                                             ALU.mult, ALU.add).then_inc(s_scan, 1)

            def add_y(n, p, s, i):
                dve.wait_ge(s_tr, n * UNITS + TI * s + i + 1)
                c_s = ct[:, p, i, s:s + 1]
                if s == 0:
                    after(dve, s_yT, n * CH)
                    ins = nc.vector.tensor_scalar(y[:, i, :], T[:, i, :], c_s, None, ALU.mult)
                else:
                    dve.wait_ge(s_y, n * UNITS + TI * (s - 1) + i + 1)
                    ins = nc.vector.scalar_tensor_tensor(y[:, i, :], T[:, i, :], c_s, y[:, i, :], ALU.mult, ALU.add)
                ins.then_inc(s_y, 1)

            def o_skip(n, p):
                for c in range(CH):
                    dve.wait_ge(s_yT, n * CH + c + 1)
                    nc.vector.scalar_tensor_tensor(gT[:, c, :], xc[:, p, c, :], dsk[:, c:c + 1], Q[:, c, :],
                                                   ALU.mult, ALU.add).then_inc(s_g, 1)

            def o_resid(n):
                dve.wait_ge(s_op, n + 1)
                dve.wait_ge(s_oload, 48 * (n + 1))
                o = Q[:, 0:2, :].rearrange("p b (i d) -> p (b i) d", d=D)
                after(dve, s_bast, 16 * n)
                link(nc.vector.tensor_tensor(x1[:, :, :], hres[:, :, :], o, ALU.add), "o", n)
                link(nc.vector.tensor_tensor(x1[:, :, :], x1[:, :, :], rows(modo[:, 0, :]), ALU.mult), "o", n)
                link(nc.vector.tensor_tensor(x1[:, :, :], x1[:, :, :], xres[:, :, :], ALU.add), "o", n)
                stats("o", n, x1, 1, s_x1)

            def o_mod(n):
                dve.wait_ge(s_ln2r, n + 1)
                link(normalise(xf, x1, 1), "o", n)
                link(nc.vector.tensor_tensor(xf[:, :, :], xf[:, :, :], rows(modo[:, 2, :]), ALU.mult), "o", n)
                link(nc.vector.tensor_tensor(xf[:, :, :], xf[:, :, :], rows(modo[:, 1, :]), ALU.add), "o", n)
                stats("o", n, xf, 2, s_xf)

            def o_xhat(n):
                dve.wait_ge(s_ln3r, n + 1)
                after(dve, s_xhst, 16 * n)
                normalise(xh, xf, 2).then_inc(s_xh, 1)

            def o_top(n):
                dve.wait_ge(s_scp, n + 1)
                link(nc.vector.tensor_copy(sc[:, :, :], Q[:, 2, 0:TI * E].rearrange("p (i e) -> p i e", i=TI)), "o", n)
                carrier()
                for i in range(TI):
                    last = nc.vector.max(top[:, i, :], sc[:, i, :])
                link(last, "o", n)
                carrier()
                for i in range(TI):
                    last = nc.vector.max_index(tix[:, i, :], top[:, i, :], sc[:, i, :])
                nc.vector.tensor_tensor(vd[:, 0, :], top[:, :, 1], top[:, :, 0], ALU.subtract).then_inc(s_vd, 1)
                link(last, "o", n)
                link(nc.vector.tensor_copy(tif[:, :, :], tix[:, :, 0:2]), "o", n)
                for k in range(2):
                    nc.vector.tensor_tensor(oh[:, k, bass.ds(n * TI, TI), :], iota8[:, :].unsqueeze(1).to_broadcast([P, TI, E]),
                                            tif[:, :, k].unsqueeze(2).to_broadcast([P, TI, E]), ALU.is_equal)

            def o_base(n):
                dve.wait_ge(s_ve, n + 1)
                w1, w2 = wts[:, 0, bass.ds(n * TI, TI)], wts[:, 1, bass.ds(n * TI, TI)]
                link(nc.vector.tensor_scalar(vd[:, 2, :], vd[:, 1, :], 1.0, None, ALU.add), "o", n)
                link(nc.vector.reciprocal(vd[:, 2, :], vd[:, 2, :]), "o", n)
                link(nc.vector.tensor_tensor(vd[:, 1, :], vd[:, 1, :], vd[:, 2, :], ALU.mult), "o", n)
                nc.vector.tensor_copy(w1, vd[:, 2, :])
                nc.vector.tensor_copy(w2, vd[:, 1, :])
                link(nc.vector.tensor_tensor(vd[:, 3, :], vd[:, 1, :], vd[:, 2, :], ALU.add), "o", n)
                for i in range(TI):
                    last = nc.vector.scalar_tensor_tensor(xf[:, i, :], xf[:, i, :], vd[:, 3, i:i + 1], modo[:, 3, :],
                                                          ALU.mult, ALU.mult)
                link(last, "o", n)
                nc.vector.tensor_tensor(x1[:, :, :], x1[:, :, :], xf[:, :, :], ALU.add).then_inc(s_base, 1)

            def prologue():
                for n in range(2):
                    p_stats(n)
                    p_mod(n)
                    counted(P_LINKS, 0)
                conv(0, 0, range(K))
                dt_u(0, 0)
            def body(n, p, has_o, has_p, has_r):
                if not has_o:
                    for c in range(CH):
                        scan(n, 0, c)
                for s in range(NS):
                    if has_o and s == 0:
                        o_skip(n - 1, 1 - p)
                    for c in range(CH):
                        if s + 1 < NS:
                            scan(n, s + 1, c)
                        elif has_p:
                            scan(n + 1, 0, c)
                        add_y(n, p, s, c)
                    if has_r and s == 1:
                        p_stats(n + 2)
                    if has_o and s == 3:
                        o_resid(n - 1)
                    if has_r and s == 4:
                        p_mod(n + 2)
                    if has_o and s == 5:
                        o_mod(n - 1)
                    if has_p and s in (5, 6, 7, 8):
                        conv(n + 1, 1 - p, (s - 5,))
                    if has_o and s == 7:
                        o_xhat(n - 1)
                    if has_o and s == 8:
                        o_top(n - 1)
                    if has_o and s == 10:
                        o_base(n - 1)
                    if has_p and s == 13:
                        dt_u(n + 1, 1 - p)
                counted(P_LINKS * has_r, O_LINKS * has_o)

            def epilogue():
                o_skip(NB - 1, 1)
                o_resid(NB - 1)
                o_mod(NB - 1)
                o_xhat(NB - 1)
                o_top(NB - 1)
                o_base(NB - 1)

            sequences(dve, prologue, body, epilogue)


def stage_b(nc, sem, ident, oh, slots, tile_expert, psum, xhat_d, slotx_d,
            w1_sb, w2_sb, b1_sb, b2_sb, gam, bet, W1, W2, b1, b2, gamma, beta, s_wts):
    RING = 16
    with ExitStack() as own:
        def sb(name, shape, dt=F32):
            return own.enter_context(nc.sbuf_tensor(name, shape, dt))

        before = sb("before", [P, P])
        ones = sb("ones", [P, P])
        thr = sb("thr", [P, NT])
        jrow = sb("jrow", [P, NSLOT])
        mask = sb("mask", [P, NT, E])
        tot = sb("tot", [P, E, NT])
        incl = sb("incl", [P, E, NT])
        full = sb("full", [P, E, NT])
        ptiles = sb("ptiles", [P, E])
        tend = sb("tend", [P, E])
        tfirst = sb("tfirst", [P, E])
        slot3 = sb("slot3", [P, NT, E])
        pick = sb("pick", [P, NT, E])
        slotf = sb("slotf", [P, 2, NT])
        ended = sb("ended", [P, NSLOT, E])
        texp = sb("texp", [P, NSLOT])
        xs = sb("xs", [P, RING, D])
        s_k = sem("b_constants")
        s_mask = sem("mask_ready")
        s_cnt = sem("counts_ps")
        s_slots = sem("slots_ready")
        s_xs = [sem(f"xs_loaded{i}") for i in range(RING)]
        s_sc = [sem(f"xs_scattered{i}") for i in range(RING)]
        s_link = sem("b_links")
        block = own.enter_context(nc.Block())

        def load_expert(eng, e):
            eng.dma_start(w1_sb[:, e * DC:(e + 1) * DC, :], W1[e].rearrange("(k p) f -> p k f", p=P)).then_inc(s_wts, 16)
            eng.dma_start(w2_sb[:, e * FC:(e + 1) * FC, :], W2[e].rearrange("(k p) d -> p k d", p=P)).then_inc(s_wts, 16)

        @block.sync
        def _(sp):
            for i in range(NT):
                if i >= RING:
                    sp.wait_ge(s_sc[i % RING], 32 * (i // RING))
                sp.dma_start(xs[:, i % RING, :], xhat_d[i * P:(i + 1) * P, :]).then_inc(s_xs[i % RING], 16)

        @block.scalar
        def _(act):
            act.dma_start(gam[:, :], gamma).then_inc(s_wts, 16)
            act.dma_start(bet[:, :], beta).then_inc(s_wts, 16)
            act.dma_start(b1_sb[:, :, :].rearrange("p e f -> p (e f)"), b1.to_broadcast([P, E * F])).then_inc(s_wts, 16)
            act.dma_start(b2_sb[:, :, :].rearrange("p e d -> p (e d)"), b2.to_broadcast([P, E * D])).then_inc(s_wts, 16)
            for e in range(E):
                load_expert(act, e)
            act.wait_ge(s_wts, 16 * (4 + 2 * E))

        @block.gpsimd
        def _(pool):
            pool.memset(before[:, :], 0.0).then_inc(s_k, 1)
            pool.memset(ones[:, :], 1.0)
            pool.iota(thr[:, :], [[P, NT]], base=0, channel_multiplier=0, allow_small_or_imprecise_dtypes=True)
            pool.iota(jrow[:, :], [[1, NSLOT]], base=0, channel_multiplier=0, allow_small_or_imprecise_dtypes=True)
            pool.wait_ge(s_k, 1)
            pool.affine_select(out=before[:, :], in_=before[:, :], compare_op=ALU.is_ge, fill=1.0, base=0,
                               pattern=[[-1, P]], channel_multiplier=1).then_inc(s_k, 1)
            pool.wait_ge(s_slots, 1)
            for i in range(NT):
                pool.wait_ge(s_xs[i % RING], 16 * (i // RING + 1))
                for k in range(2):
                    pool.indirect_dma_start(slotx_d, bass.IndirectOffsetOnAxis(ap=slots[:, k, i:i + 1], axis=0),
                                            xs[:, i % RING, :], None).then_inc(s_sc[i % RING], 16)
            for r in range(RING):
                pool.wait_ge(s_sc[r], 32 * (NT // RING))

        @block.tensor
        def _(pe):
            pe.wait_ge(s_k, 2)
            pe.wait_ge(s_mask, 1)
            m = mask[:, :, :].rearrange("p i e -> p (i e)")
            nc.tensor.matmul(psum[:, 0, 0:NT * E], before[:, :], m, start=True, stop=True)
            nc.tensor.matmul(psum[:, 1, 0:NT * E], ones[:, :], m, start=True, stop=True).then_inc(s_cnt, 1)

        @block.vector
        def _(dve):
            steps = [0]

            def link(ins):
                steps[0] += 1
                ins.then_inc(s_link, 1)
                dve.wait_ge(s_link, steps[0])

            def over_tiles(v):
                return v.unsqueeze(1).to_broadcast([P, NT, E])

            nc.vector.tensor_tensor(mask[:, :, :], oh[:, 0, :, :], oh[:, 1, :, :], ALU.add).then_inc(s_mask, 1)
            dve.wait_ge(s_k, 2)
            dve.wait_ge(s_cnt, 1)
            link(nc.vector.tensor_copy(tot[:, :, :], psum[:, 1, 0:NT * E].rearrange("p (i e) -> p e i", e=E)))
            for e in range(E):
                last = nc.vector.tensor_tensor_scan(incl[:, e, :], ones[:, 0:NT], tot[:, e, :], 0.0, ALU.mult, ALU.add)
            link(last)
            link(nc.vector.tensor_tensor(full[:, :, :], incl[:, :, NT - 1:NT].to_broadcast([P, E, NT]),
                                         thr[:, :].unsqueeze(1).to_broadcast([P, E, NT]), ALU.is_gt))
            link(nc.vector.tensor_reduce(ptiles[:, :], full[:, :, :], AX.X, ALU.add))
            link(nc.vector.tensor_tensor_scan(tend[:, :], ones[:, 0:E], ptiles[:, :], 0.0, ALU.mult, ALU.add))
            link(nc.vector.tensor_tensor(tfirst[:, :], tend[:, :], ptiles[:, :], ALU.subtract))
            link(nc.vector.tensor_scalar(tfirst[:, :], tfirst[:, :], float(P), None, ALU.mult))
            link(nc.vector.tensor_tensor(incl[:, :, :], incl[:, :, :], tot[:, :, :], ALU.subtract))
            link(nc.vector.tensor_tensor(slot3[:, :, :], psum[:, 0, 0:NT * E].rearrange("p (i e) -> p i e", e=E),
                                         incl[:, :, :].rearrange("p e i -> p i e"), ALU.add))
            link(nc.vector.tensor_tensor(slot3[:, :, :], slot3[:, :, :], over_tiles(tfirst[:, :]), ALU.add))
            for k in range(2):
                link(nc.vector.tensor_tensor(pick[:, :, :], slot3[:, :, :], oh[:, k, :, :], ALU.mult))
                link(nc.vector.tensor_reduce(slotf[:, k, :], pick[:, :, :], AX.X, ALU.add))
            nc.vector.tensor_copy(slots[:, :, :], slotf[:, :, :]).then_inc(s_slots, 1)
            link(nc.vector.tensor_tensor(ended[:, :, :], tend[:, :].unsqueeze(1).to_broadcast([P, NSLOT, E]),
                                         jrow[:, :].unsqueeze(2).to_broadcast([P, NSLOT, E]), ALU.is_le))
            link(nc.vector.tensor_reduce(texp[:, :], ended[:, :, :], AX.X, ALU.add))
            link(nc.vector.tensor_scalar(texp[:, :], texp[:, :], float(E - 1), None, ALU.min))
            link(nc.vector.tensor_copy(tile_expert[:, :], texp[:, :]))


def stage_c(nc, sem, ident, tile_expert, psum, slotx_d, sloty_d, w1_sb, w2_sb, b1_sb, b2_sb, gam, bet):
    XR, YR = 4, 4
    with ExitStack() as own:
        def sb(name, shape, dt=F32):
            return own.enter_context(nc.sbuf_tensor(name, shape, dt))

        xg = sb("xg", [P, XR, D])
        xgT = sb("xgT", [P, 2, DC, P])
        hb = sb("hb", [P, F])
        hT = sb("hT", [P, FC, P])
        ysb = sb("ysb", [P, YR, D])
        X_PS = psum[:, 0, 0:DC * P].rearrange("p (k t) -> p k t", k=DC)
        H_PS = psum[:, 2:4, :]
        HT_PS = psum[:, 4:6, :]
        Y_PS = psum[:, 6:8, 0:D]
        s_x = [sem(f"xg_loaded{i}") for i in range(XR)]
        s_xtp = sem("xgT_ps")
        s_xt = sem("xgT_ready")
        s_hp = sem("h_ps")
        s_hb = sem("hb_ready")
        s_htp = sem("hT_ps")
        s_ht = sem("hT_ready")
        s_yp = sem("y_ps")
        s_ys = sem("ysb_ready")
        s_st = [sem(f"y_stored{i}") for i in range(YR)]
        block = own.enter_context(nc.Block())
        TURN = 4

        def after(eng, s, value):
            if not (isinstance(value, int) and value <= 0):
                eng.wait_ge(s, value)

        def tiles(eng, body):
            for r in range(TURN):
                body(r, r, 0)
            with eng.Fori(1, NSLOT // TURN) as group:
                for r in range(TURN):
                    body(group * TURN + r, r, group)

        @block.sync
        def _(sp):
            def step(j, r, group):
                after(sp, s_xtp, j - XR + 1)
                sp.dma_start(xg[:, r, :], slotx_d[bass.ds(j * P, P), :]).then_inc(s_x[r], 16)

            tiles(sp, step)

        @block.gpsimd
        def _(pool):
            def step(j, r, group):
                pool.wait_ge(s_ys, j + 1)
                pool.dma_start(sloty_d[bass.ds(j * P, P), :], ysb[:, r, :]).then_inc(s_st[r], 16)

            tiles(pool, step)
            for r in range(YR):
                pool.wait_ge(s_st[r], 16 * (NSLOT // YR))

        @block.scalar
        def _(act):
            def step(j, r, group):
                act.wait_ge(s_htp, j + 1)
                for b in range(2):
                    last = nc.scalar.activation(hT[:, 4 * b:4 * b + 4, :],
                                                HT_PS[:, b, :].rearrange("p (k t) -> p k t", k=4), ACT.Relu)
                last.then_inc(s_ht, 1)

            tiles(act, step)

        @block.tensor
        def _(pe):
            def transpose_x(j, r, group):
                pe.wait_ge(s_x[r], (group + 1) * 16)
                after(pe, s_xt, j)
                for k in range(DC):
                    last = nc.tensor.transpose(X_PS[:, k, :], xg[:, r, k * P:(k + 1) * P], ident[:, :])
                last.then_inc(s_xtp, 1)

            def first(j, r, e):
                pe.wait_ge(s_xt, j + 1)
                after(pe, s_hb, j)
                for f in range(2):
                    for k in range(DC):
                        last = nc.tensor.matmul(H_PS[:, f, :], xgT[:, r % 2, k, :],
                                                w1_sb[:, bass.ds(e * DC + k, 1), f * 512:(f + 1) * 512].rearrange("p a f -> p (a f)"),
                                                start=(k == 0), stop=(k == DC - 1))
                last.then_inc(s_hp, 1)

            def second(j, r, e):
                pe.wait_ge(s_ht, j + 1)
                after(pe, s_ys, j - 1)
                for k in range(FC):
                    last = nc.tensor.matmul(Y_PS[:, r % 2, :], hT[:, k, :],
                                            w2_sb[:, bass.ds(e * FC + k, 1), :].rearrange("p a d -> p (a d)"),
                                            start=(k == 0), stop=(k == FC - 1))
                last.then_inc(s_yp, 1)

            def transpose_h(j):
                pe.wait_ge(s_hb, j + 1)
                after(pe, s_ht, j)
                for k in range(FC):
                    last = nc.tensor.transpose(HT_PS[:, k // 4, (k % 4) * P:(k % 4 + 1) * P], hb[:, k * P:(k + 1) * P], ident[:, :])
                last.then_inc(s_htp, 1)

            def expert(j):
                return pe.value_load(tile_expert[0:1, bass.ds(j, 1)], min_val=0, max_val=E - 1)

            def turn(group, begins, ends):
                for r in range(TURN):
                    j = group * TURN + r
                    first(j, r, expert(j))
                    if not (ends and r == TURN - 1):
                        transpose_x(j + 1, (r + 1) % TURN, group if r + 1 < TURN else group + 1)
                    if not (begins and r == 0):
                        second(j - 1, (r - 1) % TURN, expert(j - 1))
                    transpose_h(j)

            transpose_x(0, 0, 0)
            turn(0, True, False)
            with pe.Fori(1, NSLOT // TURN - 1) as group:
                turn(group, False, False)
            turn(NSLOT // TURN - 1, False, True)
            second(NSLOT - 1, TURN - 1, expert(NSLOT - 1))

        @block.vector
        def _(dve):
            def x_in(j, r, e):
                dve.wait_ge(s_xtp, j + 1)
                after(dve, s_hp, j - 1)
                for k in range(DC):
                    at = bass.ds(e * DC + k, 1)
                    last = nc.vector.tensor_scalar(xgT[:, r % 2, k, :], X_PS[:, k, :], gam[:, at], bet[:, at], ALU.mult, ALU.add)
                last.then_inc(s_xt, 1)

            def h_in(j, e):
                dve.wait_ge(s_hp, j + 1)
                after(dve, s_htp, j)
                nc.vector.tensor_tensor(hb[:, :], H_PS.rearrange("p b f -> p (b f)"),
                                        b1_sb[:, bass.ds(e, 1), :].rearrange("p a f -> p (a f)"), ALU.add).then_inc(s_hb, 1)

            def y_in(j, r, e, group):
                dve.wait_ge(s_yp, j + 1)
                after(dve, s_st[r], 16 * group)
                nc.vector.tensor_tensor(ysb[:, r, :], Y_PS[:, r % 2, :],
                                        b2_sb[:, bass.ds(e, 1), :].rearrange("p a d -> p (a d)"), ALU.add).then_inc(s_ys, 1)

            def expert(j):
                return dve.value_load(tile_expert[0:1, bass.ds(j, 1)], min_val=0, max_val=E - 1)

            def turn(group, begins, ends):
                for r in range(TURN):
                    j = group * TURN + r
                    h_in(j, expert(j))
                    if not (ends and r == TURN - 1):
                        x_in(j + 1, (r + 1) % TURN, expert(j + 1))
                    if not (begins and r == 0):
                        y_in(j - 1, (r - 1) % TURN, expert(j - 1), group - 1 if r == 0 else group)

            x_in(0, 0, expert(0))
            turn(0, True, False)
            turn(1, False, False)
            with dve.Fori(2, NSLOT // TURN - 1) as group:
                turn(group, False, False)
            turn(NSLOT // TURN - 1, False, True)
            y_in(NSLOT - 1, TURN - 1, expert(NSLOT - 1), NSLOT // TURN - 1)


def stage_d(nc, sem, slots, wts, mod_d, base_d, sloty_d, out):
    with ExitStack() as own:
        def sb(name, shape, dt=F32):
            return own.enter_context(nc.sbuf_tensor(name, shape, dt))

        BUF = 4
        gb = sb("gb", [P, NB, D])
        base = sb("base", [P, BUF, TI, D])
        y12 = sb("y12", [P, BUF, 2, TI, D])
        res = sb("res", [P, BUF, TI, D])
        s_gb = sem("gb_loaded")
        s_b = [sem(f"base_loaded{i}") for i in range(BUF)]
        s_g = [sem(f"y12_gathered{i}") for i in range(BUF)]
        s_link = sem("d_links")
        s_res = sem("res_ready")
        s_out = [sem(f"out_stored{i}") for i in range(BUF)]
        block = own.enter_context(nc.Block())

        def rows(t, n):
            return t[n * L:(n + 1) * L, :].rearrange("(i p) d -> p i d", p=P)

        @block.sync
        def _(sp):
            for n in range(NB):
                sp.dma_start(gb[:, n, :], mod_d[n:n + 1, 5 * D:6 * D].to_broadcast([P, D])).then_inc(s_gb, 16)
            for n in range(NB):
                if n >= BUF:
                    sp.wait_ge(s_res, n - BUF + 1)
                sp.dma_start(base[:, n % BUF, :, :], rows(base_d, n)).then_inc(s_b[n % BUF], 16)

        @block.gpsimd
        def _(pool):
            for n in range(NB):
                if n >= BUF:
                    pool.wait_ge(s_res, n - BUF + 1)
                for i in range(TI):
                    for k in range(2):
                        t = n * TI + i
                        pool.indirect_dma_start(y12[:, n % BUF, k, i, :], None, sloty_d,
                                                bass.IndirectOffsetOnAxis(ap=slots[:, k, t:t + 1], axis=0)
                                                ).then_inc(s_g[n % BUF], 16)

        @block.vector
        def _(dve):
            steps = [0]

            def link(ins):
                steps[0] += 1
                ins.then_inc(s_link, 1)
                dve.wait_ge(s_link, steps[0])

            dve.wait_ge(s_gb, 16 * NB)
            for n in range(NB):
                b = n % BUF
                dve.wait_ge(s_g[b], 16 * 2 * TI * (n // BUF + 1))
                if n >= BUF:
                    dve.wait_ge(s_out[b], 16 * (n // BUF))
                for i in range(TI):
                    t = n * TI + i
                    last = nc.vector.tensor_scalar(res[:, b, i, :], y12[:, b, 0, i, :], wts[:, 0, t:t + 1], None, ALU.mult)
                link(last)
                for i in range(TI):
                    t = n * TI + i
                    last = nc.vector.scalar_tensor_tensor(res[:, b, i, :], y12[:, b, 1, i, :], wts[:, 1, t:t + 1],
                                                          res[:, b, i, :], ALU.mult, ALU.add)
                link(last)
                link(nc.vector.tensor_tensor(res[:, b, :, :], res[:, b, :, :], gb[:, n, :].unsqueeze(1).to_broadcast([P, TI, D]), ALU.mult))
                dve.wait_ge(s_b[b], 16 * (n // BUF + 1))
                nc.vector.tensor_tensor(res[:, b, :, :], res[:, b, :, :], base[:, b, :, :], ALU.add).then_inc(s_res, 1)

        @block.scalar
        def _(act):
            for n in range(NB):
                act.wait_ge(s_res, n + 1)
                act.dma_start(rows(out, n), res[:, n % BUF, :, :]).then_inc(s_out[n % BUF], 16)
            for b in range(BUF):
                act.wait_ge(s_out[b], 16 * (NB // BUF))


def kernel(**inputs):
    import numpy as np
    import concourse.bacc as bacc
    from concourse.bass_utils import run_bass_kernel_spmd

    a = {k: np.asarray(v) for k, v in inputs.items()}

    def columns(v, chunks):
        return v.reshape(-1, chunks, P).transpose(2, 0, 1).reshape(P, -1)

    arrays = {
        "x": a["L0_attn_x"].reshape(NTOK, D),
        "norm_w": columns(a["L0_attn_norm_w"], DC),
        "W_in": a["L0_attn_W_in"],
        "conv_w": a["L0_attn_conv_w"].reshape(CH, P, K).transpose(1, 0, 2),
        "conv_b": columns(a["L0_attn_conv_b"], CH),
        "W_x": a["L0_attn_W_x"],
        "W_dt": a["L0_attn_W_dt"],
        "b_dt": columns(a["L0_attn_b_dt"], CH),
        "A_log": a["L0_attn_A_log"].reshape(CH, P, NS).transpose(1, 0, 2),
        "D_skip": columns(a["L0_attn_D_skip"], CH),
        "W_out": a["L0_attn_W_out"],
        "Wg": a["L0_ffn_Wg"],
        "gamma": columns(a["L0_ffn_gamma"], DC),
        "beta": columns(a["L0_ffn_beta"], DC),
        "W1": a["L0_ffn_W1"],
        "b1": a["L0_ffn_b1"].reshape(1, E * F),
        "W2": a["L0_ffn_W2"],
        "b2": a["L0_ffn_b2"].reshape(1, E * D),
        "cT": a["L0_c"].T,
        "wmod": a["L0_wmod"],
    }
    arrays = {f"in_{k}": np.ascontiguousarray(v) for k, v in arrays.items()}
    nc = bacc.Bacc("TRN2", target_bir_lowering=False, num_devices=1)
    args = {k[3:]: nc.dram_tensor(k, v.shape, mybir.dt.from_np(v.dtype), kind="ExternalInput").ap()
            for k, v in arrays.items()}
    out = nc.dram_tensor("out", (NTOK, D), F32, kind="ExternalOutput").ap()
    adaln_kernel(nc, **args, out=out)
    r = run_bass_kernel_spmd(nc, [arrays], core_ids=[0])
    return r.results[0]["out"].reshape(NB, L, D)
```

```python
import concourse.bass as bass
from concourse import mybir
from contextlib import ExitStack

F32 = mybir.dt.float32
U32 = mybir.dt.uint32
I32 = mybir.dt.int32
ALU = mybir.AluOpType
ACT = mybir.ActivationFunctionType
AX = mybir.AxisListType

NB, L, D = 8, 512, 256
DIN, NS, R, K = 512, 16, 64, 4
E, F = 8, 1024
P = 128
NTOK = NB * L
CH = DIN // P
TI = L // P
DC = D // P
FC = F // P
XD = R + 2 * NS
NT = NTOK // P
NSLOT = 2 * NTOK // P + E
UNITS = NS * CH
PAD = K - 1
EARLY = 6
BASES = 4
YR = 4
ZROWS = 6
RING = 2 * CH
LN_EPS, FFN_EPS = 1e-5, 1e-6
DT = TI - 1
P_LINKS, O_LINKS = 1, 11


def adaln_kernel(nc, x, norm_w, W_in, conv_w, conv_b, W_x, W_dt, b_dt, A_log, D_skip, W_out,
                 Wg, gamma, beta, W1, b1, W2, b2, cT, wmod, out):
    def dram(name, shape):
        return nc.dram_tensor(name, shape, F32, kind="Internal").ap()

    mod_d = dram("mod_d", (NB, 6 * D))
    b_d = dram("b_d", (NB, NS, L))
    xhat_d = dram("xhat_d", (NTOK, D))
    h_d = dram("h_d", (NTOK, D))
    base_d = dram("base_d", (NTOK, D))
    slotx_d = dram("slotx_d", (NSLOT * P, D + 1))
    y12_d = dram("y12_d", (1 + 2 * NTOK + YR * P, D))

    ctx = ExitStack()
    with ctx:
        def sb(name, shape, dt=F32, stack=ctx):
            return stack.enter_context(nc.sbuf_tensor(name, shape, dt))

        def sem(name):
            return ctx.enter_context(nc.semaphore(name))

        ident = sb("ident", [P, P])
        oh = sb("oh", [P, 2, NT, E])
        wts = sb("wts", [P, 2, NT])
        slots = sb("slots", [P, 2, NT], U32)
        tile_expert = sb("tile_expert", [P, NSLOT], I32)
        psum = ctx.enter_context(nc.psum_tensor("psum", [P, 8, 512], F32))
        T = psum[:, 0:4, :]
        Q = psum[:, 4:7, :]
        YT = psum[:, 4:8, :]

        stage_a(nc, ctx, sem, ident, oh, wts, T, Q, YT, mod_d, b_d, h_d, xhat_d, base_d, slotx_d,
                x, norm_w, W_in, conv_w, conv_b, W_x, W_dt, b_dt, A_log, D_skip, W_out, Wg, cT, wmod)
        gb = sb("gb", [P, NB, D])
        base = sb("base", [P, BASES, TI, D])
        s_gb = sem("gb_loaded")
        s_b = [sem(f"base_loaded{i}") for i in range(BASES)]
        with ExitStack() as held:
            w1_sb = sb("w1_sb", [P, E * DC, F], stack=held)
            w2_sb = sb("w2_sb", [P, E * FC, D], stack=held)
            b1_sb = sb("b1_sb", [P, E * FC], stack=held)
            b2_sb = sb("b2_sb", [P, E, D], stack=held)
            gam = sb("gam", [P, E * DC], stack=held)
            bet = sb("bet", [P, E * DC], stack=held)
            weights_in = sem("small_weights_loaded")
            s_we = sem("expert_weights_loaded")
            stage_b(nc, sem, ident, oh, slots, tile_expert, psum, xhat_d, slotx_d,
                    w1_sb, w2_sb, b1_sb, b2_sb, gam, bet, W1, W2, b1, b2, gamma, beta, weights_in, s_we)
            stage_c(nc, sem, ident, tile_expert, psum, slotx_d, y12_d, w1_sb, w2_sb, b1_sb, b2_sb, gam, bet,
                    mod_d, base_d, gb, base, s_gb, s_b, W1, W2, s_we)
        stage_d(nc, sem, wts, base_d, y12_d, out, gb, base, s_gb, s_b)


def stage_a(nc, ctx, sem, ident, oh, wts, T, Q, YT, mod_d, b_d, h_d, xhat_d, base_d, slotx_d,
            x, norm_w, W_in, conv_w, conv_b, W_x, W_dt, b_dt, A_log, D_skip, W_out, Wg, cT, wmod):
    with ExitStack() as own:
        def sb(name, shape, dt=F32):
            return own.enter_context(nc.sbuf_tensor(name, shape, dt))

        win = sb("win", [P, DC, 2 * DIN])
        wx = sb("wx", [P, CH, XD])
        wdt = sb("wdt", [R, DIN])
        wout = sb("wout", [P, CH, D])
        wg = sb("wg", [P, DC, E])
        nw = sb("nw", [P, DC])
        cw = sb("cw", [P, CH, K])
        cb = sb("cb", [P, CH])
        bdt = sb("bdt", [P, CH])
        dsk = sb("dsk", [P, CH])
        aneg = sb("aneg", [P, CH, NS])
        iota8 = sb("iota8", [P, E])
        mhalf = sb("mhalf", [P, TI])
        xin = sb("xin", [P, TI, D])
        hmod = sb("hmod", [P, TI, D])
        xres = sb("xres", [P, TI, D])
        hres = sb("hres", [P, TI, D])
        modp = sb("modp", [P, 2, D])
        modo = sb("modo", [P, 4, D])
        xn = sb("xn", [P, TI, D])
        xnT = sb("xnT", [P, DC, L])
        xipad = sb("xipad", [P, CH, PAD + L])
        xc = sb("xc", [P, 2, CH, L])
        sz = sb("sz", [P, 2, CH, L])
        xd = sb("xd", [XD, L])
        ct = sb("ct", [P, 2, TI, NS])
        dt = sb("dt", [P, 2, CH, L])
        u = sb("u", [P, 2, CH, L])
        brep = sb("brep", [P, 4, L])
        dA = sb("dA", [P, RING, L])
        dBu = sb("dBu", [P, RING, L])
        hs = sb("hs", [P, 2, CH, L])
        y = sb("y", [P, DT, DIN])
        hc = sb("hc", [P, DIN])
        gT = sb("gT", [P, CH, L])
        xfT = gT
        x1 = sb("x1", [P, TI, D])
        xf = sb("xf", [P, TI, D])
        xh = hres
        bs = sb("bs", [P, 3, TI, 6])
        mv = sb("mv", [P, 3, TI, 2])
        rs = sb("rs", [P, 4, TI])
        tmp = sb("tmp", [P, 4, TI])
        ssq = sb("ssq", [P, TI])
        sc = sb("sc", [P, TI, E])
        top = sb("top", [P, TI, 8])
        tix = sb("tix", [P, TI, 8], U32)
        tif = sb("tif", [P, TI, 2])
        vd = sb("vd", [P, 4, TI])
        spare = sb("spare", [P, 1])
        eps = sb("eps", [P, 2, TI])
        cts = xn[:, 0, 0:DC * NB].rearrange("p (k b) -> p k b", k=DC)
        wmod_sb = hs[:, :, :, :].rearrange("p a c l -> p (a c l)")[:, 0:DC * 6 * D].rearrange("p (k n) -> p k n", k=DC)
        m8 = y[0:NB, :, :].rearrange("p a b -> p (a b)")[:, 0:6 * D]
        m8n = gT[0:NB, 0, 0:2 * D].rearrange("p (a d) -> p a d", a=2)
        zrow = dt[:, 0, :, :].rearrange("p c l -> p (c l)")

        s_w = sem("weights_loaded")
        s_ct = sem("c_loaded")
        s_id = sem("ident_steps")
        s_csilu = sem("c_silu")
        s_modps = sem("mod_ps")
        s_m8 = sem("mod_rows_copied")
        s_modr = sem("mod_rows_ready")
        s_modst = sem("mod_stored")
        s_const = sem("constants_ready")
        s_aexp = sem("a_exp")
        s_zero = sem("slot_rows_zeroed")
        s_pload = sem("x_and_modp_loaded")
        s_hst = sem("h_stored")
        s_oload = sem("modo_xres_hres_loaded")
        s_ln1 = sem("ln1_stats")
        s_ln1r = sem("ln1_rstd")
        s_hn = sem("x_normalised")
        s_h = sem("h_ready")
        s_sq = sem("square_sums")
        s_rms = sem("rms_rstd")
        s_xn = sem("xn_ready")
        s_xntp = sem("xnT_ps")
        s_xnt = sem("xnT_ready")
        s_xip = sem("xi_ps")
        s_xi = sem("xi_ready")
        s_zp = sem("z_ps")
        s_z = sem("z_ready")
        s_zs = sem("z_silu_ready")
        s_tap = sem("conv_taps")
        s_xc = sem("xc_ready")
        s_xdp = sem("xd_ps")
        s_xd = sem("xd_ready")
        s_bst = sem("b_stored")
        s_cp = sem("c_ps")
        s_c = sem("c_ready")
        s_dtp = sem("dt_ps")
        s_sp = sem("softplus_parts")
        s_dtr = sem("dt_ps_read")
        s_dt = sem("dt_ready")
        s_u = sem("u_ready")
        s_br = [sem(f"brep_loaded{i}") for i in range(4)]
        s_dA = sem("dA_ready")
        s_dBu = sem("dBu_ready")
        s_scan = sem("scanned")
        s_tr = sem("states_transposed")
        s_y = sem("y_added")
        s_hc = sem("last_tile_times_c")
        s_acc = sem("last_tile_summed")
        s_yT = sem("yT_ps")
        s_g = sem("skip_added")
        s_gate = sem("gated")
        s_op = sem("out_ps")
        s_opr = sem("out_ps_read")
        s_x1 = sem("x1_ready")
        s_ln2r = sem("ln2_rstd")
        s_x1n = sem("x1_normalised")
        s_xfm = sem("xf_modulated")
        s_xf = sem("xf_stats")
        s_ln3r = sem("ln3_rstd")
        s_xh = sem("xhat_ready")
        s_xhst = sem("xhat_stored")
        s_xftp = sem("xfT_ps")
        s_xft = sem("xfT_ready")
        s_scp = sem("scores_ps")
        s_vd = sem("top_difference")
        s_ve = sem("top_exp")
        s_scaled = sem("skip_scaled")
        s_base = sem("base_ready")
        s_bast = sem("base_stored")
        s_act = sem("act_links")

        Z_BANK = (1, 1, 0, 2)
        O_BANK = (2, 0)
        DT_BANK = (0, 1, 0, 2)
        LAG = 3

        def after(eng, s, value):
            if not (isinstance(value, int) and value <= 0):
                eng.wait_ge(s, value)

        def immediate(eng):
            eng.wait_ge(s_id, 2)

        def sequences(eng, prologue, body, epilogue):
            prologue()
            body(0, 0, False, True, True)
            with eng.Fori(0, (NB - 4) // 2) as turn:
                body(2 * turn + 1, 1, True, True, True)
                body(2 * turn + 2, 0, True, True, True)
            body(NB - 3, 1, True, True, True)
            body(NB - 2, 0, True, True, False)
            body(NB - 1, 1, True, False, False)
            epilogue()

        block = own.enter_context(nc.Block())

        @block.sync
        def _(sp):
            sp.dma_start(cts, cT.rearrange("(k p) b -> p k b", p=P)).then_inc(s_ct, 16)
            sp.dma_start(wmod_sb, wmod.rearrange("(k p) n -> p k n", p=P)).then_inc(s_ct, 16)
            sp.dma_start(xin[:, :, :], x[0:L, :].rearrange("(i p) d -> p i d", p=P)).then_inc(s_pload, 16)
            for dst, src in ((win[:, :, :], W_in.rearrange("(k p) n -> p k n", p=P)),
                             (wx[:, :, :], W_x.rearrange("(k p) n -> p k n", p=P)),
                             (wdt[:, :], W_dt), (wout[:, :, :], W_out.rearrange("(k p) n -> p k n", p=P)),
                             (wg[:, :, :], Wg.rearrange("(k p) n -> p k n", p=P)),
                             (nw[:, :], norm_w), (cw[:, :, :], conv_w), (cb[:, :], conv_b),
                             (bdt[:, :], b_dt), (dsk[:, :], D_skip), (aneg[:, :, :], A_log)):
                sp.dma_start(dst, src).then_inc(s_w, 16)
            sp.wait_ge(s_modr, 1)
            sp.dma_start(mod_d, m8).then_inc(s_modst, 16)
            sp.wait_ge(s_modst, 16)

            def mod_rows(n, first, count, dst):
                rows = mod_d[bass.ds(n, 1), first * D:(first + count) * D]
                return dict(out=dst.rearrange("p m d -> p (m d)"), in_=rows.to_broadcast([P, count * D]))

            def rows(t, n):
                return t[bass.ds(n * L, L), :].rearrange("(i p) d -> p i d", p=P)

            def load(n):
                immediate(sp)
                after(sp, s_h, n)
                if not (isinstance(n, int) and n == 0):
                    sp.dma_start(xin[:, :, :], rows(x, n)).then_inc(s_pload, 16)
                sp.dma_start(**mod_rows(n, 0, 2, modp[:, :, :])).then_inc(s_pload, 16)

            def store_h(n):
                immediate(sp)
                sp.wait_ge(s_h, n + 1)
                sp.dma_start(rows(h_d, n), hmod[:, :, :]).then_inc(s_hst, 16)

            def load_o(n):
                immediate(sp)
                sp.wait_ge(s_hst, 16 * (n + 1))
                after(sp, s_base, n)
                sp.dma_start(**mod_rows(n, 2, 4, modo[:, :, :])).then_inc(s_oload, 16)
                sp.dma_start(xres[:, :, :], rows(x, n)).then_inc(s_oload, 16)
                sp.dma_start(hres[:, :, :], rows(h_d, n)).then_inc(s_oload, 16)

            def load_brep(n, s):
                immediate(sp)
                if s == 0:
                    sp.wait_ge(s_bst, 16 * (n + 1))
                after(sp, s_dBu, n * UNITS + 4 * (s - 3))
                sp.dma_start(brep[:, s % 4, :], b_d[bass.ds(n, 1), s, :].to_broadcast([P, L])).then_inc(s_br[s % 4], 16)

            def store_xhat(n):
                immediate(sp)
                sp.wait_ge(s_xh, n + 1)
                sp.dma_start(rows(xhat_d, n), xh[:, :, :]).then_inc(s_xhst, 16)

            def store_base(n):
                immediate(sp)
                sp.wait_ge(s_base, n + 1)
                sp.dma_start(rows(base_d, n), x1[:, :, :]).then_inc(s_bast, 16)

            def prologue():
                load(0)
                load(1)
                store_h(0)
                sp.wait_ge(s_const, 1)
                zsrc = zrow[:, 0:ZROWS * (D + 1)].rearrange("p (a d) -> p a d", d=D + 1)
                for k in range(NSLOT // ZROWS):
                    sp.dma_start(slotx_d[k * ZROWS * P:(k + 1) * ZROWS * P, :].rearrange("(p a) d -> p a d", p=P),
                                 zsrc).then_inc(s_zero, 16)
                store_h(1)

            def body(n, p, has_o, has_p, has_r):
                for s in range(NS):
                    load_brep(n, s)
                    if not has_o and s == 1:
                        load_o(n)
                    if has_r and s == 0:
                        load(n + 2)
                    if has_r and s == 10:
                        store_h(n + 2)
                    if has_o and s == 13:
                        store_xhat(n - 1)
                    if has_o and s == 15:
                        immediate(sp)
                        sp.wait_ge(s_xhst, 16 * n)
                        store_base(n - 1)
                        load_o(n)

            def epilogue():
                store_xhat(NB - 1)
                store_base(NB - 1)
                sp.wait_ge(s_xhst, 16 * NB)
                sp.wait_ge(s_bast, 16 * NB)

            sequences(sp, prologue, body, epilogue)

        @block.gpsimd
        def _(pool):
            pool.memset(zrow, 0.0)
            pool.memset(mhalf[:, :], -0.5)
            pool.memset(eps[:, 0, :], LN_EPS)
            pool.memset(eps[:, 1, :], FFN_EPS)
            pool.iota(iota8[:, :], [[1, E]], base=0, channel_multiplier=0, allow_small_or_imprecise_dtypes=True)
            pool.memset(xipad[:, :, 0:PAD], 0.0).then_inc(s_const, 1)
            pool.memset(ident[:, :], 0.0).then_inc(s_id, 1)
            pool.wait_ge(s_id, 1)
            pool.affine_select(out=ident[:, :], in_=ident[:, :], compare_op=ALU.not_equal, fill=1.0, base=0,
                               pattern=[[-1, P]], channel_multiplier=1).then_inc(s_id, 1)

            def ln1(n):
                pool.wait_ge(s_ln1, n + 1)
                rstd_p(n, 0, mv[:, 0, :, 1], eps[:, 0, :], s_ln1r)

            def p_mod(n):
                h = hmod[:, :, :]
                pool.wait_ge(s_hn, n + 1)
                nc.gpsimd.tensor_tensor(h, h, modp[:, 1, :].unsqueeze(1).to_broadcast([P, TI, D]), ALU.mult).then_inc(pl, 1)
                pool.wait_ge(pl, 3 * n + 2)
                nc.gpsimd.tensor_tensor(h, h, modp[:, 0, :].unsqueeze(1).to_broadcast([P, TI, D]), ALU.add).then_inc(s_h, 1)

            def rms(n):
                pool.wait_ge(s_sq, n + 1)
                rstd_p(n, 3, ssq[:, :], eps[:, 0, :], s_rms)

            pl, ol = sem("pool_links_p"), sem("pool_links_o")

            def rstd_on(s, count, which, src, add, ready):
                nc.gpsimd.tensor_tensor(tmp[:, which, :], src, add, ALU.add).then_inc(s, 1)
                pool.wait_ge(s, count)
                nc.gpsimd.tensor_tensor(rs[:, which, :], tmp[:, which, :], mhalf[:, :], ALU.pow).then_inc(ready, 1)

            def rstd_p(n, which, src, add, ready):
                rstd_on(pl, 3 * n + (1 if which == 0 else 3), which, src, add, ready)

            def gate(n, p):
                for c in range(CH):
                    pool.wait_ge(s_zs, n * CH + c + 1)
                    pool.wait_ge(s_g, n * CH + c + 1)
                    nc.gpsimd.tensor_tensor(gT[:, c, :], gT[:, c, :], sz[:, p, c, :], ALU.mult).then_inc(s_gate, 1)

            def ln2(n):
                pool.wait_ge(s_x1, n + 1)
                rstd_on(ol, 3 * n + 1, 1, mv[:, 1, :, 1], eps[:, 0, :], s_ln2r)

            def ln3(n):
                pool.wait_ge(s_xf, n + 1)
                rstd_on(ol, 3 * n + 3, 2, mv[:, 2, :, 1], eps[:, 1, :], s_ln3r)

            def o_mod(n):
                pool.wait_ge(s_x1n, n + 1)
                nc.gpsimd.tensor_tensor(xf[:, :, :], xf[:, :, :], modo[:, 2, :].unsqueeze(1).to_broadcast([P, TI, D]), ALU.mult).then_inc(ol, 1)
                pool.wait_ge(ol, 3 * n + 2)
                nc.gpsimd.tensor_tensor(xf[:, :, :], xf[:, :, :], modo[:, 1, :].unsqueeze(1).to_broadcast([P, TI, D]), ALU.add).then_inc(s_xfm, 1)

            def base(n):
                pool.wait_ge(s_scaled, n + 1)
                nc.gpsimd.tensor_tensor(x1[:, :, :], x1[:, :, :], xf[:, :, :], ALU.add).then_inc(s_base, 1)

            def inputs(n, p, s):
                pool.wait_ge(s_br[s % 4], 16 * (n * (NS // 4) + s // 4 + 1))
                for c in range(CH):
                    i = s * CH + c
                    if s == 0:
                        pool.wait_ge(s_u, n * CH + c + 1)
                    after(pool, s_scan, n * UNITS + i - RING + 1)
                    nc.gpsimd.tensor_tensor(dBu[:, i % RING, :], u[:, p, c, :], brep[:, s % 4, :], ALU.mult).then_inc(s_dBu, 1)

            def prologue():
                for n in range(2):
                    ln1(n)
                    p_mod(n)
                    rms(n)

            def body(n, p, has_o, has_p, has_r):
                for s in range(NS):
                    inputs(n, p, s)
                    if has_o and s == 3:
                        gate(n - 1, 1 - p)
                    if has_r and s == 5:
                        ln1(n + 2)
                    if has_r and s == 7:
                        p_mod(n + 2)
                    if has_o and s == 8:
                        ln2(n - 1)
                    if has_o and s == 10:
                        o_mod(n - 1)
                    if has_o and s == 12:
                        ln3(n - 1)
                    if has_r and s == 11:
                        rms(n + 2)
                    if has_o and s == 15:
                        base(n - 1)

            def epilogue():
                ln2(NB - 1)
                o_mod(NB - 1)
                ln3(NB - 1)
                base(NB - 1)

            sequences(pool, prologue, body, epilogue)

        @block.scalar
        def _(act):
            act.wait_ge(s_ct, 32)
            nc.scalar.activation(cts, cts, ACT.Silu).then_inc(s_csilu, 1)
            for j in range(3):
                act.wait_ge(s_modps, j + 1)
                nc.scalar.activation(m8[:, j * 512:(j + 1) * 512], Q[0:NB, j, :], ACT.Copy).then_inc(s_m8, 1)
            act.wait_ge(s_w, 16 * 11)
            nc.scalar.activation(aneg[:, :, :], aneg[:, :, :], ACT.Exp).then_inc(s_aexp, 1)
            act.wait_ge(s_aexp, 1)
            nc.scalar.activation(aneg[:, :, :], aneg[:, :, :], ACT.Copy, scale=-1.0).then_inc(s_aexp, 1)
            act.wait_ge(s_aexp, 2)

            def squares(n):
                act.wait_ge(s_h, n + 1)
                after(act, s_xntp, n)
                for i in range(TI):
                    last = nc.scalar.activation(xn[:, i, :], hmod[:, i, :], ACT.Square, scale=float(D) ** -0.5, accum_out=ssq[:, i:i + 1])
                last.then_inc(s_sq, 1)

            def norm(n):
                act.wait_ge(s_rms, n + 1)
                for i in range(TI):
                    last = nc.scalar.activation(xn[:, i, :], hmod[:, i, :], ACT.Copy, scale=rs[:, 3, i:i + 1])
                last.then_inc(s_xn, 1)

            def norm_t(n):
                act.wait_ge(s_xntp, n + 1)
                for c in range(DC):
                    last = nc.scalar.activation(xnT[:, c, :], Q[:, c, :], ACT.Copy, scale=nw[:, c:c + 1])
                last.then_inc(s_xnt, 1)

            def conv_in(n, p, chunks):
                for c in chunks:
                    act.wait_ge(s_xip, n * CH + c + 1)
                    nc.scalar.activation(xc[:, p, c, :], Q[:, (c + 1) % 3, :], ACT.Identity, bias=cb[:, c:c + 1],
                                         scale=cw[:, c, PAD:K])
                    nc.scalar.activation(xipad[:, c, PAD:], Q[:, (c + 1) % 3, :], ACT.Copy).then_inc(s_xi, 1)

            def z_in(n, p, chunks):
                for c in chunks:
                    act.wait_ge(s_zp, n * CH + c + 1)
                    nc.scalar.activation(sz[:, p, c, :], Q[:, Z_BANK[c], :], ACT.Copy).then_inc(s_z, 1)

            def silu_x(n, p):
                for c in range(CH):
                    act.wait_ge(s_tap, n * CH * PAD + CH * (PAD - 1) + c + 1)
                    nc.scalar.activation(xc[:, p, c, :], xc[:, p, c, :], ACT.Silu).then_inc(s_xc, 1)

            def silu_z(n, p):
                act.wait_ge(s_z, n * CH + CH)
                for c in range(CH):
                    nc.scalar.activation(sz[:, p, c, :], sz[:, p, c, :], ACT.Silu).then_inc(s_zs, 1)

            def xd_copy(n):
                act.wait_ge(s_xdp, n + 1)
                after(act, s_bst, 16 * n)
                nc.scalar.activation(xd[:, :], Q[0:XD, 1, :], ACT.Copy).then_inc(s_xd, 1)
                act.wait_ge(s_xd, n + 1)
                act.dma_start(b_d[bass.ds(n, 1), :, :].rearrange("a s l -> (a s) l"), xd[R:R + NS, :]).then_inc(s_bst, 16)

            def c_copy(n, p):
                act.wait_ge(s_cp, n + 1)
                nc.scalar.activation(ct[:, p, :, :], Q[:, 1, 0:TI * XD].rearrange("p (i n) -> p i n", i=TI)[:, :, R + NS:XD],
                                     ACT.Copy).then_inc(s_c, 1)

            def softplus_in(n, p, chunks):
                for c in chunks:
                    q = Q[:, DT_BANK[c], :]
                    act.wait_ge(s_dtp, n * CH + c + 1)
                    nc.scalar.activation(u[:, p, c, :], q, ACT.Abs, bias=bdt[:, c:c + 1]).then_inc(s_act, 1)
                    nc.scalar.activation(dt[:, p, c, :], q, ACT.Relu, bias=bdt[:, c:c + 1]).then_inc(s_dtr, 1)
                for c in chunks:
                    act.wait_ge(s_act, n * 2 * CH + chunks[0] + c + 1)
                    nc.scalar.activation(u[:, p, c, :], u[:, p, c, :], ACT.Exp, scale=-1.0).then_inc(s_act, 1)

            def softplus_ln(n, p):
                act.wait_ge(s_act, (n + 1) * 2 * CH)
                for c in range(CH):
                    nc.scalar.activation(u[:, p, c, :], u[:, p, c, :], ACT.Ln, bias=1.0).then_inc(s_sp, 1)

            def times_c(n, p, s):
                if s == 0:
                    act.wait_ge(s_c, n + 1)
                act.wait_ge(s_tr, n * UNITS + TI * (s + 1))
                after(act, s_acc, n * NS + s)
                nc.scalar.activation(hc[:, :], T[:, DT, :], ACT.Copy, scale=ct[:, p, DT, s:s + 1]).then_inc(s_hc, 1)

            def decays(n, p, s, has_before):
                for c in range(CH):
                    if c == 2 and s >= LAG:
                        times_c(n, p, s - LAG)
                    elif c == 2 and has_before:
                        times_c(n - 1, 1 - p, NS + s - LAG)
                    i = s * CH + c
                    if s == 0:
                        act.wait_ge(s_dt, n * CH + c + 1)
                    after(act, s_scan, n * UNITS + i - RING + 1)
                    nc.scalar.activation(dA[:, i % RING, :], dt[:, p, c, :], ACT.Exp,
                                         scale=aneg[:, c, s:s + 1]).then_inc(s_dA, 1)

            def scores_in(n):
                act.wait_ge(s_xftp, n + 1)
                for c in range(DC):
                    last = nc.scalar.activation(xfT[:, c, :], Q[:, (2 + c) % 3, :], ACT.Copy)
                last.then_inc(s_xft, 1)

            def top_exp(n):
                act.wait_ge(s_vd, n + 1)
                nc.scalar.activation(vd[:, 1, :], vd[:, 0, :], ACT.Exp).then_inc(s_ve, 1)

            def prologue():
                squares(0)
                norm(0)
                norm_t(0)
                conv_in(0, 0, range(CH))
                squares(1)
                norm(1)
                z_in(0, 0, (0,))
                silu_x(0, 0)
                xd_copy(0)
                c_copy(0, 0)
                after(act, s_zero, 16 * (NSLOT // ZROWS))
                softplus_in(0, 0, (0, 1))
                softplus_in(0, 0, (2, 3))
                softplus_ln(0, 0)
                z_in(0, 0, (1, 2, 3))

            def body(n, p, has_o, has_p, has_r):
                for s in range(NS):
                    decays(n, p, s, has_o)
                    if has_o and s == 0:
                        z_in(n, p, (1, 2, 3))
                    if has_p and s == 4:
                        norm_t(n + 1)
                    if has_p and s in (6, 8, 9):
                        conv_in(n + 1, 1 - p, {6: (0,), 8: (1, 2), 9: (3,)}[s])
                    if has_r and s == 9:
                        squares(n + 2)
                    if has_p and s == 10:
                        z_in(n + 1, 1 - p, (0,))
                    if s == 11:
                        if has_p:
                            silu_x(n + 1, 1 - p)
                        silu_z(n, p)
                    if has_o and s == 12:
                        scores_in(n - 1)
                    if has_r and s == 12:
                        norm(n + 2)
                    if has_o and s == 14:
                        top_exp(n - 1)
                    if has_p and s == 12:
                        xd_copy(n + 1)
                    if has_p and s == 13:
                        c_copy(n + 1, 1 - p)
                        softplus_in(n + 1, 1 - p, (0,))
                    if has_p and s == 14:
                        softplus_in(n + 1, 1 - p, (1, 2))
                    if has_p and s == 15:
                        softplus_in(n + 1, 1 - p, (3,))
                        softplus_ln(n + 1, 1 - p)

            def epilogue():
                for s in range(NS - LAG, NS):
                    times_c(NB - 1, 1, s)
                scores_in(NB - 1)
                top_exp(NB - 1)

            sequences(act, prologue, body, epilogue)

        @block.tensor
        def _(pe):
            pe.wait_ge(s_csilu, 1)
            for j in range(3):
                for k in range(DC):
                    last = nc.tensor.matmul(Q[0:NB, j, :], cts[:, k, :], wmod_sb[:, k, j * 512:(j + 1) * 512],
                                            start=(k == 0), stop=(k == DC - 1))
                last.then_inc(s_modps, 1)
            pe.wait_ge(s_id, 2)
            pe.wait_ge(s_w, 16 * 11)
            pe.wait_ge(s_m8, 3)

            def norm_t(n, skipped):
                pe.wait_ge(s_xn, n + 1)
                after(pe, s_g, skipped * CH)
                for c in range(DC):
                    for i in range(TI):
                        last = nc.tensor.transpose(Q[:, c, i * P:(i + 1) * P], xn[:, i, c * P:(c + 1) * P], ident[:, :])
                last.then_inc(s_xntp, 1)

            def in_proj_x(n, chunks):
                pe.wait_ge(s_xnt, n + 1)
                for c in chunks:
                    if c == 3:
                        pe.wait_ge(s_xi, n * CH + 1)
                    for k in range(DC):
                        last = nc.tensor.matmul(Q[:, (c + 1) % 3, :], win[:, k, c * P:(c + 1) * P], xnT[:, k, :],
                                                start=(k == 0), stop=(k == DC - 1))
                    last.then_inc(s_xip, 1)

            def in_proj_z(n, chunks):
                for c in chunks:
                    if c == 0:
                        pe.wait_ge(s_xi, n * CH + CH)
                    if c >= 1:
                        pe.wait_ge(s_dtr, n * CH + c + 1)
                    for k in range(DC):
                        last = nc.tensor.matmul(Q[:, Z_BANK[c], :], win[:, k, DIN + c * P:DIN + (c + 1) * P], xnT[:, k, :],
                                                start=(k == 0), stop=(k == DC - 1))
                    last.then_inc(s_zp, 1)

            def x_proj(n, p):
                pe.wait_ge(s_z, n * CH + 1)
                for c in range(CH):
                    pe.wait_ge(s_xc, n * CH + c + 1)
                    last = nc.tensor.matmul(Q[0:XD, 1, :], wx[:, c, :], xc[:, p, c, :],
                                            start=(c == 0), stop=(c == CH - 1))
                last.then_inc(s_xdp, 1)

            def c_t(n):
                pe.wait_ge(s_xd, n + 1)
                for i in range(TI):
                    last = nc.tensor.transpose(Q[:, 1, i * XD:(i + 1) * XD], xd[:, i * P:(i + 1) * P], ident[0:XD, 0:XD])
                last.then_inc(s_cp, 1)

            def dt_proj(n, chunks):
                for c in chunks:
                    if c == 1:
                        pe.wait_ge(s_c, n + 1)
                    if c == 2:
                        pe.wait_ge(s_dtr, n * CH + 1)
                    nc.tensor.matmul(Q[:, DT_BANK[c], :], wdt[:, c * P:(c + 1) * P], xd[0:R, :],
                                     start=True, stop=True).then_inc(s_dtp, 1)

            def states(n, s):
                pe.wait_ge(s_scan, n * UNITS + CH * (s + 1))
                for i in range(TI):
                    if i < DT:
                        after(pe, s_y, DT * (n * NS + s - 1) + i + 1)
                    else:
                        after(pe, s_hc, n * NS + s)
                    for c in range(CH):
                        last = nc.tensor.transpose(T[:, i, c * P:(c + 1) * P], hs[:, s % 2, c, i * P:(i + 1) * P], ident[:, :])
                    last.then_inc(s_tr, 1)

            def add_last(n, s):
                pe.wait_ge(s_hc, n * NS + s + 1)
                if s == 0:
                    after(pe, s_g, n * CH)
                for c in range(CH):
                    last = nc.tensor.matmul(YT[:, DT, c * P:(c + 1) * P], hc[:, c * P:(c + 1) * P], ident[:, :],
                                            start=(s == 0 and c == 0), stop=(s == NS - 1), skip_group_check=True)
                last.then_inc(s_acc, 1)

            def y_t(n, projected):
                pe.wait_ge(s_y, DT * NS * (n + 1))
                pe.wait_ge(s_sp, projected * CH)
                pe.wait_ge(s_z, projected * CH)
                for i in range(DT):
                    for c in range(CH):
                        last = nc.tensor.transpose(YT[:, i, c * P:(c + 1) * P], y[:, i, c * P:(c + 1) * P], ident[:, :])
                last.then_inc(s_yT, 1)

            def out_proj(n, projected, tiles):
                pe.wait_ge(s_gate, (n + 1) * CH)
                for i in tiles:
                    if i == 2:
                        after(pe, s_xnt, projected)
                    pe.wait_ge(s_oload, 48 * (n + 1))
                    nc.tensor.matmul(Q[:, O_BANK[i // 2], (i % 2) * D:(i % 2 + 1) * D], ident[:, :], hres[:, i, :],
                                     start=True, stop=False)
                    for c in range(CH):
                        last = nc.tensor.matmul(Q[:, O_BANK[i // 2], (i % 2) * D:(i % 2 + 1) * D], gT[:, c, i * P:(i + 1) * P],
                                                wout[:, c, :], start=False, stop=(c == CH - 1))
                last.then_inc(s_op, 1)

            def xf_t(n):
                pe.wait_ge(s_xfm, n + 1)
                for c in range(DC):
                    for i in range(TI):
                        last = nc.tensor.transpose(Q[:, (2 + c) % 3, i * P:(i + 1) * P], xf[:, i, c * P:(c + 1) * P], ident[:, :])
                last.then_inc(s_xftp, 1)

            def scores(n):
                pe.wait_ge(s_xft, n + 1)
                for i in range(TI):
                    for c in range(DC):
                        last = nc.tensor.matmul(Q[:, 2, i * E:(i + 1) * E], xfT[:, c, i * P:(i + 1) * P], wg[:, c, :],
                                                start=(c == 0), stop=(c == DC - 1))
                last.then_inc(s_scp, 1)

            def prologue():
                norm_t(0, 0)
                in_proj_x(0, range(CH))
                in_proj_z(0, (0,))
                x_proj(0, 0)
                c_t(0)
                dt_proj(0, range(CH))
                in_proj_z(0, (1, 2, 3))

            def body(n, p, has_o, has_p, has_r):
                if has_o:
                    y_t(n - 1, n + 1)
                for s in range(NS):
                    states(n, s)
                    if s > 0:
                        add_last(n, s - 1)
                    elif has_o:
                        add_last(n - 1, NS - 1)
                    if has_p and s == 1:
                        norm_t(n + 1, n)
                    if has_p and s == 2:
                        in_proj_x(n + 1, (0,))
                    if has_o and s in (3, 4, 5):
                        out_proj(n - 1, n + 2 if has_p else n + 1, {3: (0,), 4: (1, 2), 5: (3,)}[s])
                    if has_p and s == 5:
                        after(pe, s_opr, n)
                        in_proj_x(n + 1, (1, 2))
                    if has_p and s == 6:
                        in_proj_x(n + 1, (3,))
                    if has_p and s == 7:
                        in_proj_z(n + 1, (0,))
                    if has_o and s == 9:
                        if has_p:
                            pe.wait_ge(s_xi, (n + 1) * CH + 3)
                        xf_t(n - 1)
                    if has_p and s == 9:
                        x_proj(n + 1, 1 - p)
                    if has_o and s == 11:
                        scores(n - 1)
                    if has_p and s == 11:
                        c_t(n + 1)
                        after(pe, s_xft, n)
                        dt_proj(n + 1, (0, 1))
                    if has_p and s == 12:
                        after(pe, s_vd, n)
                        dt_proj(n + 1, (2, 3))
                    if has_p and s == 13:
                        in_proj_z(n + 1, (1, 2, 3))

            def epilogue():
                y_t(NB - 1, NB)
                add_last(NB - 1, NS - 1)
                for tiles in (0,), (1, 2), (3,):
                    out_proj(NB - 1, NB, tiles)
                xf_t(NB - 1)
                scores(NB - 1)

            sequences(pe, prologue, body, epilogue)

        @block.vector
        def _(dve):
            own_p, own_o = sem("dve_links_p"), sem("dve_links_o")
            count = {"p": 0, "o": 0}

            def link(ins, kind, n):
                s, per = (own_p, P_LINKS) if kind == "p" else (own_o, O_LINKS)
                ins.then_inc(s, 1)
                count[kind] += 1
                dve.wait_ge(s, n * per + count[kind])

            def counted(p_links, o_links):
                assert count == {"p": p_links, "o": o_links}, count
                count["p"] = count["o"] = 0

            dve.wait_ge(s_m8, 3)
            m6 = m8.rearrange("p (m d) -> p m d", m=6)
            setup = sem("dve_setup")
            steps = [0]

            def then(ins):
                steps[0] += 1
                ins.then_inc(setup, 1)
                dve.wait_ge(setup, steps[0])

            for m in (1, 4):
                then(nc.vector.tensor_scalar(m6[:, m, :], m6[:, m, :], 1.0, None, ALU.add))
            for m in (2, 5):
                a, b = m8n[:, 0, :], m8n[:, 1, :]
                then(nc.vector.tensor_scalar(a, m6[:, m, :], -1.0, None, ALU.mult))
                then(nc.vector.tensor_tensor(a, a, m6[:, m, :], ALU.max))
                then(nc.vector.tensor_scalar(b, m6[:, m, :], 0.0, 2.0, ALU.is_ge, ALU.mult))
                then(nc.vector.tensor_scalar(b, b, -1.0, None, ALU.add))
                then(nc.vector.tensor_scalar(a, a, 0.25, None, ALU.max))
                then(nc.vector.tensor_tensor(m6[:, m, :], a, b, ALU.mult))
            nc.vector.tensor_copy(tif[0:1, 0, 0:1], m6[0:1, 0, 0:1]).then_inc(s_modr, 1)
            dve.wait_ge(s_const, 1)
            dve.wait_ge(s_w, 16 * 11)
            dve.wait_ge(s_modst, 16)

            def carrier():
                nc.vector.memset(spare[:, :], 0.0)

            def stats(kind, n, src, which, ready):
                for i in range(TI):
                    last = nc.vector.bn_stats(bs[:, which, i, :], src[:, i, :])
                link(last, kind, n)
                carrier()
                for i in range(TI):
                    last = nc.vector.bn_aggr(mv[:, which, i, :], bs[:, which, i, :])
                if ready is not None:
                    last.then_inc(ready, 1)
                return last

            def normalise(dst, src, which):
                for i in range(TI):
                    last = nc.vector.tensor_scalar(dst[:, i, :], src[:, i, :], mv[:, which, i, 0:1], rs[:, which, i:i + 1],
                                                   ALU.subtract, ALU.mult)
                return last

            def rows(m):
                return m.unsqueeze(1).to_broadcast([P, TI, D])

            def p_stats(n):
                dve.wait_ge(s_pload, 32 * (n + 1))
                stats("p", n, xin, 0, s_ln1)

            def p_norm(n):
                dve.wait_ge(s_ln1r, n + 1)
                after(dve, s_hst, 16 * n)
                after(dve, s_xn, n)
                normalise(hmod[:, :, :], xin, 0).then_inc(s_hn, 1)

            def conv(n, p, taps):
                for k, c in taps:
                    src = xipad[:, c, k:k + L]
                    dst = xc[:, p, c, :]
                    if k == 0:
                        dve.wait_ge(s_xi, n * CH + c + 1)
                    else:
                        dve.wait_ge(s_tap, n * CH * PAD + CH * (k - 1) + c + 1)
                    nc.vector.scalar_tensor_tensor(dst, src, cw[:, c, k:k + 1], dst, ALU.mult, ALU.add).then_inc(s_tap, 1)

            def dt_sum(n, p):
                for c in range(CH):
                    dve.wait_ge(s_sp, n * CH + c + 1)
                    nc.vector.tensor_tensor(dt[:, p, c, :], dt[:, p, c, :], u[:, p, c, :], ALU.add).then_inc(s_dt, 1)

            def dt_x(n, p):
                for c in range(CH):
                    dve.wait_ge(s_dt, n * CH + c + 1)
                    nc.vector.tensor_tensor(u[:, p, c, :], dt[:, p, c, :], xc[:, p, c, :], ALU.mult).then_inc(s_u, 1)

            def scan(n, s, c):
                i = s * CH + c
                if c == 0 and s >= 2:
                    dve.wait_ge(s_tr, n * UNITS + TI * (s - 1))
                elif c == 0:
                    after(dve, s_tr, (n - 1) * UNITS + TI * (NS - 1 + s))
                dve.wait_ge(s_dA, n * UNITS + i + 1)
                dve.wait_ge(s_dBu, n * UNITS + i + 1)
                nc.vector.tensor_tensor_scan(hs[:, s % 2, c, :], dA[:, i % RING, :], dBu[:, i % RING, :], 0.0,
                                             ALU.mult, ALU.add).then_inc(s_scan, 1)

            def add_y(n, p, s, i):
                if i == DT:
                    return
                dve.wait_ge(s_tr, n * UNITS + TI * s + i + 1)
                c_s = ct[:, p, i, s:s + 1]
                if s == 0:
                    after(dve, s_yT, n)
                    ins = nc.vector.tensor_scalar(y[:, i, :], T[:, i, :], c_s, None, ALU.mult)
                else:
                    dve.wait_ge(s_y, DT * (n * NS + s - 1) + i + 1)
                    ins = nc.vector.scalar_tensor_tensor(y[:, i, :], T[:, i, :], c_s, y[:, i, :], ALU.mult, ALU.add)
                ins.then_inc(s_y, 1)

            def o_skip(n, p):
                dve.wait_ge(s_yT, n + 1)
                dve.wait_ge(s_acc, NS * (n + 1))
                for c in range(CH):
                    def by_tile(v):
                        return v.rearrange("p (i t) -> p i t", i=TI)
                    nc.vector.scalar_tensor_tensor(by_tile(gT[:, c, :]), by_tile(xc[:, p, c, :]), dsk[:, c:c + 1],
                                                   YT[:, :, c * P:(c + 1) * P], ALU.mult, ALU.add).then_inc(s_g, 1)

            def o_resid(n):
                dve.wait_ge(s_op, 3 * (n + 1))
                dve.wait_ge(s_oload, 48 * (n + 1))
                after(dve, s_bast, 16 * n)
                for b in range(2):
                    at = slice(2 * b, 2 * b + 2)
                    last = nc.vector.tensor_tensor(x1[:, at, :], modo[:, 0, :].unsqueeze(1).to_broadcast([P, 2, D]),
                                                   Q[:, O_BANK[b], :].rearrange("p (i d) -> p i d", d=D), ALU.mult)
                last.then_inc(s_opr, 1)
                dve.wait_ge(s_opr, n + 1)
                link(nc.vector.tensor_tensor(x1[:, :, :], x1[:, :, :], xres[:, :, :], ALU.add), "o", n)
                stats("o", n, x1, 1, s_x1)

            def o_norm(n):
                dve.wait_ge(s_ln2r, n + 1)
                normalise(xf, x1, 1).then_inc(s_x1n, 1)

            def o_stats(n):
                dve.wait_ge(s_xfm, n + 1)
                stats("o", n, xf, 2, s_xf)

            def o_xhat(n):
                dve.wait_ge(s_ln3r, n + 1)
                after(dve, s_xhst, 16 * n)
                normalise(xh, xf, 2).then_inc(s_xh, 1)

            def o_top(n):
                dve.wait_ge(s_scp, n + 1)
                link(nc.vector.tensor_copy(sc[:, :, :], Q[:, 2, 0:TI * E].rearrange("p (i e) -> p i e", i=TI)), "o", n)
                carrier()
                for i in range(TI):
                    last = nc.vector.max(top[:, i, :], sc[:, i, :])
                link(last, "o", n)
                carrier()
                for i in range(TI):
                    last = nc.vector.max_index(tix[:, i, :], top[:, i, :], sc[:, i, :])
                nc.vector.tensor_tensor(vd[:, 0, :], top[:, :, 1], top[:, :, 0], ALU.subtract).then_inc(s_vd, 1)
                link(last, "o", n)
                link(nc.vector.tensor_copy(tif[:, :, :], tix[:, :, 0:2]), "o", n)
                for k in range(2):
                    nc.vector.tensor_tensor(oh[:, k, bass.ds(n * TI, TI), :], iota8[:, :].unsqueeze(1).to_broadcast([P, TI, E]),
                                            tif[:, :, k].unsqueeze(2).to_broadcast([P, TI, E]), ALU.is_equal)

            def o_base(n):
                dve.wait_ge(s_ve, n + 1)
                w1, w2 = wts[:, 0, bass.ds(n * TI, TI)], wts[:, 1, bass.ds(n * TI, TI)]
                link(nc.vector.tensor_scalar(vd[:, 2, :], vd[:, 1, :], 1.0, None, ALU.add), "o", n)
                link(nc.vector.reciprocal(vd[:, 2, :], vd[:, 2, :]), "o", n)
                link(nc.vector.tensor_tensor(vd[:, 1, :], vd[:, 1, :], vd[:, 2, :], ALU.mult), "o", n)
                nc.vector.tensor_copy(w1, vd[:, 2, :])
                nc.vector.tensor_copy(w2, vd[:, 1, :])
                link(nc.vector.tensor_tensor(vd[:, 3, :], vd[:, 1, :], vd[:, 2, :], ALU.add), "o", n)
                for i in range(TI):
                    last = nc.vector.scalar_tensor_tensor(xf[:, i, :], xf[:, i, :], vd[:, 3, i:i + 1], modo[:, 3, :],
                                                          ALU.mult, ALU.mult)
                last.then_inc(s_scaled, 1)

            def prologue():
                for n in range(2):
                    p_stats(n)
                    p_norm(n)
                    counted(P_LINKS, 0)
                conv(0, 0, [(k, c) for k in range(PAD) for c in range(CH)])
                dt_sum(0, 0)
                dt_x(0, 0)

            def body(n, p, has_o, has_p, has_r):
                if not has_o:
                    for c in range(CH):
                        scan(n, 0, c)
                for s in range(NS):
                    for c in range(CH):
                        if s + 1 < NS:
                            scan(n, s + 1, c)
                        elif has_p:
                            scan(n + 1, 0, c)
                        add_y(n, p, s, c)
                    if has_o and s == 0:
                        o_skip(n - 1, 1 - p)
                    if has_r and s == 2:
                        p_stats(n + 2)
                    if has_r and s == 4:
                        p_norm(n + 2)
                    if has_o and s == 5:
                        o_resid(n - 1)
                    if has_o and s == 7:
                        o_norm(n - 1)
                    if has_p and s in (6, 7, 8):
                        taps = [(k, c) for k in range(PAD) for c in range(CH)]
                        conv(n + 1, 1 - p, {6: taps[:3], 7: taps[3:7], 8: taps[7:]}[s])
                    if has_o and s == 9:
                        o_stats(n - 1)
                    if has_o and s == 10:
                        o_xhat(n - 1)
                    if has_o and s == 11:
                        o_top(n - 1)
                    if has_o and s == 12:
                        o_base(n - 1)
                    if has_p and s == 13:
                        dt_sum(n + 1, 1 - p)
                    if has_p and s == 14:
                        dt_x(n + 1, 1 - p)
                counted(P_LINKS * has_r, O_LINKS * has_o)

            def epilogue():
                o_skip(NB - 1, 1)
                for c in range(CH):
                    dve.wait_ge(s_zs, (NB - 1) * CH + c + 1)
                    dve.wait_ge(s_g, (NB - 1) * CH + c + 1)
                    nc.vector.tensor_tensor(gT[:, c, :], gT[:, c, :], sz[:, 1, c, :], ALU.mult).then_inc(s_gate, 1)
                o_resid(NB - 1)
                o_norm(NB - 1)
                o_stats(NB - 1)
                o_xhat(NB - 1)
                o_top(NB - 1)
                o_base(NB - 1)

            sequences(dve, prologue, body, epilogue)


def load_weights(eng, s_we, k, w1_sb, w2_sb, W1, W2):
    e = k // 2
    if k % 2 == 0:
        eng.dma_start(w1_sb[:, e * DC:(e + 1) * DC, :], W1[e].rearrange("(k p) f -> p k f", p=P)).then_inc(s_we, 16)
    else:
        eng.dma_start(w2_sb[:, e * FC:(e + 1) * FC, :], W2[e].rearrange("(k p) d -> p k d", p=P)).then_inc(s_we, 16)


def stage_b(nc, sem, ident, oh, slots, tile_expert, psum, xhat_d, slotx_d,
            w1_sb, w2_sb, b1_sb, b2_sb, gam, bet, W1, W2, b1, b2, gamma, beta, s_wts, s_we):
    RING = 12
    with ExitStack() as own:
        def sb(name, shape, dt=F32):
            return own.enter_context(nc.sbuf_tensor(name, shape, dt))

        before = sb("before", [P, P])
        ones = sb("ones", [P, P])
        thr = sb("thr", [P, NT])
        jrow = sb("jrow", [P, NSLOT])
        mask = sb("mask", [P, NT, E])
        tot = sb("tot", [P, E, NT])
        incl = sb("incl", [P, E, NT])
        full = sb("full", [P, E, NT])
        ptiles = sb("ptiles", [P, E])
        tend = sb("tend", [P, E])
        tfirst = sb("tfirst", [P, E])
        slot3 = sb("slot3", [P, NT, E])
        pick = sb("pick", [P, NT, E])
        slotf = sb("slotf", [P, 2, NT])
        ended = sb("ended", [P, NSLOT, E])
        texp = sb("texp", [P, NSLOT])
        xs = sb("xs", [P, RING, 2, D + 1])
        place = sb("place", [P, 2, NT])
        s_xp = sem("xs_with_places")
        s_k = sem("b_constants")
        s_mask = sem("mask_ready")
        s_cnt = sem("counts_ps")
        s_slots = sem("slots_ready")
        s_xs = [sem(f"xs_loaded{i}") for i in range(RING)]
        s_sc = [sem(f"xs_scattered{i}") for i in range(RING)]
        s_link = sem("b_links")
        block = own.enter_context(nc.Block())

        @block.sync
        def _(sp):
            for i in range(NT):
                if i >= RING:
                    sp.wait_ge(s_sc[i % RING], 32 * (i // RING))
                sp.dma_start(xs[:, i % RING, 0, 0:D], xhat_d[i * P:(i + 1) * P, :]).then_inc(s_xs[i % RING], 16)

        @block.scalar
        def _(act):
            act.dma_start(b1_sb[:, :], b1).then_inc(s_wts, 16)
            act.dma_start(b2_sb[:, :, :].rearrange("p e d -> p (e d)"), b2.to_broadcast([P, E * D])).then_inc(s_wts, 16)
            act.dma_start(gam[:, :], gamma).then_inc(s_wts, 16)
            act.dma_start(bet[:, :], beta).then_inc(s_wts, 16)
            for k in range(2 * EARLY):
                load_weights(act, s_we, k, w1_sb, w2_sb, W1, W2)
                act.wait_ge(s_we, 16 * (k + 1))
            act.wait_ge(s_wts, 64)

        @block.gpsimd
        def _(pool):
            pool.memset(before[:, :], 0.0).then_inc(s_k, 1)
            pool.memset(ones[:, :], 1.0)
            pool.iota(thr[:, :], [[P, NT]], base=0, channel_multiplier=0, allow_small_or_imprecise_dtypes=True)
            pool.iota(jrow[:, :], [[1, NSLOT]], base=0, channel_multiplier=0, allow_small_or_imprecise_dtypes=True)
            for k in range(2):
                pool.iota(place[:, k, :], [[2 * P, NT]], base=1 + k, channel_multiplier=2, allow_small_or_imprecise_dtypes=True)
            pool.wait_ge(s_k, 1)
            pool.affine_select(out=before[:, :], in_=before[:, :], compare_op=ALU.is_ge, fill=1.0, base=0,
                               pattern=[[-1, P]], channel_multiplier=1).then_inc(s_k, 1)
            pool.wait_ge(s_slots, 1)
            for i in range(NT):
                pool.wait_ge(s_xp, i + 1)
                for k in range(2):
                    pool.indirect_dma_start(slotx_d, bass.IndirectOffsetOnAxis(ap=slots[:, k, i:i + 1], axis=0),
                                            xs[:, i % RING, k, :], None).then_inc(s_sc[i % RING], 16)
            for r in range(RING):
                pool.wait_ge(s_sc[r], 32 * len(range(r, NT, RING)))

        @block.tensor
        def _(pe):
            pe.wait_ge(s_k, 2)
            pe.wait_ge(s_mask, 1)
            m = mask[:, :, :].rearrange("p i e -> p (i e)")
            nc.tensor.matmul(psum[:, 0, 0:NT * E], before[:, :], m, start=True, stop=True)
            nc.tensor.matmul(psum[:, 1, 0:NT * E], ones[:, :], m, start=True, stop=True).then_inc(s_cnt, 1)

        @block.vector
        def _(dve):
            steps = [0]

            def link(ins):
                steps[0] += 1
                ins.then_inc(s_link, 1)
                dve.wait_ge(s_link, steps[0])

            def over_tiles(v):
                return v.unsqueeze(1).to_broadcast([P, NT, E])

            nc.vector.tensor_tensor(mask[:, :, :], oh[:, 0, :, :], oh[:, 1, :, :], ALU.add).then_inc(s_mask, 1)
            dve.wait_ge(s_k, 2)
            dve.wait_ge(s_cnt, 1)
            link(nc.vector.tensor_copy(tot[:, :, :], psum[:, 1, 0:NT * E].rearrange("p (i e) -> p e i", e=E)))
            for e in range(E):
                last = nc.vector.tensor_tensor_scan(incl[:, e, :], ones[:, 0:NT], tot[:, e, :], 0.0, ALU.mult, ALU.add)
            link(last)
            link(nc.vector.tensor_tensor(full[:, :, :], incl[:, :, NT - 1:NT].to_broadcast([P, E, NT]),
                                         thr[:, :].unsqueeze(1).to_broadcast([P, E, NT]), ALU.is_gt))
            link(nc.vector.tensor_reduce(ptiles[:, :], full[:, :, :], AX.X, ALU.add))
            link(nc.vector.tensor_tensor_scan(tend[:, :], ones[:, 0:E], ptiles[:, :], 0.0, ALU.mult, ALU.add))
            link(nc.vector.tensor_tensor(tfirst[:, :], tend[:, :], ptiles[:, :], ALU.subtract))
            link(nc.vector.tensor_scalar(tfirst[:, :], tfirst[:, :], float(P), None, ALU.mult))
            link(nc.vector.tensor_tensor(incl[:, :, :], incl[:, :, :], tot[:, :, :], ALU.subtract))
            link(nc.vector.tensor_tensor(slot3[:, :, :], psum[:, 0, 0:NT * E].rearrange("p (i e) -> p i e", e=E),
                                         incl[:, :, :].rearrange("p e i -> p i e"), ALU.add))
            link(nc.vector.tensor_tensor(slot3[:, :, :], slot3[:, :, :], over_tiles(tfirst[:, :]), ALU.add))
            for k in range(2):
                link(nc.vector.tensor_tensor(pick[:, :, :], slot3[:, :, :], oh[:, k, :, :], ALU.mult))
                link(nc.vector.tensor_reduce(slotf[:, k, :], pick[:, :, :], AX.X, ALU.add))
            nc.vector.tensor_copy(slots[:, :, :], slotf[:, :, :]).then_inc(s_slots, 1)

            for i in range(NT):
                dve.wait_ge(s_xs[i % RING], 16 * (i // RING + 1))
                for k in range(2):
                    nc.vector.tensor_copy(xs[:, i % RING, k, D:D + 1], place[:, k, i:i + 1])
                nc.vector.tensor_copy(xs[:, i % RING, 1, 0:D], xs[:, i % RING, 0, 0:D]).then_inc(s_xp, 1)

            link(nc.vector.tensor_tensor(ended[:, :, :], tend[:, :].unsqueeze(1).to_broadcast([P, NSLOT, E]),
                                         jrow[:, :].unsqueeze(2).to_broadcast([P, NSLOT, E]), ALU.is_le))
            link(nc.vector.tensor_reduce(texp[:, :], ended[:, :, :], AX.X, ALU.add))
            link(nc.vector.tensor_scalar(texp[:, :], texp[:, :], float(E - 1), None, ALU.min))
            link(nc.vector.tensor_copy(tile_expert[:, :], texp[:, :]))


def stage_c(nc, sem, ident, tile_expert, psum, slotx_d, y12_d, w1_sb, w2_sb, b1_sb, b2_sb, gam, bet,
            mod_d, base_d, gb, base, s_gb, s_b, W1, W2, s_we):
    XR = 4
    with ExitStack() as own:
        def sb(name, shape, dt=F32):
            return own.enter_context(nc.sbuf_tensor(name, shape, dt))

        xg = sb("xg", [P, XR, D + 1])
        place = sb("row_of_y12", [P, YR], U32)
        unfilled = sb("unfilled", [P, YR])
        filler = sb("filler", [P, YR])
        spare = sb("spare_c", [P, YR])
        s_car = sem("carried")
        s_un = sem("unfilled_rows")
        s_fil = sem("filler_ready")
        xgT = sb("xgT", [P, 2, DC, P])
        hT = sb("hT", [P, 2, FC, P])
        w1_now = sb("w1_now", [P, 2, DC, F])
        s_w1 = sem("w1_now_ready")
        ysb = sb("ysb", [P, YR, D])
        X_PS = psum[:, 0, 0:DC * P].rearrange("p (k t) -> p k t", k=DC)
        H_PS = psum[:, 2:6, :].rearrange("p (a b) (f t) -> p a (b f) t", a=2, t=P)
        Y_PS = psum[:, 6:8, 0:D]
        s_x = [sem(f"xg_loaded{i}") for i in range(XR)]
        s_xtp = sem("xgT_ps")
        s_xt = sem("xgT_ready")
        s_hp = sem("hT_ps")
        s_ht = sem("hT_ready")
        s_yp = sem("y_ps")
        s_ys = sem("ysb_ready")
        s_st = [sem(f"y_stored{i}") for i in range(YR)]
        block = own.enter_context(nc.Block())
        TURN = 4

        def after(eng, s, value):
            if not (isinstance(value, int) and value <= 0):
                eng.wait_ge(s, value)

        def tiles(eng, body):
            for r in range(TURN):
                body(r, r, 0)
            with eng.Fori(1, NSLOT // TURN) as group:
                for r in range(TURN):
                    body(group * TURN + r, r, group)

        @block.sync
        def _(sp):
            def step(j, r, group):
                after(sp, s_xt, j - XR + 1)
                sp.dma_start(xg[:, r, :], slotx_d[bass.ds(j * P, P), :]).then_inc(s_x[r], 16)

            for r in range(TURN):
                step(r, r, 0)
            for k in range(2 * EARLY, 2 * E):
                load_weights(sp, s_we, k, w1_sb, w2_sb, W1, W2)
                sp.wait_ge(s_we, 16 * (k + 1))
            with sp.Fori(1, NSLOT // TURN) as group:
                for r in range(TURN):
                    step(group * TURN + r, r, group)
            for n in range(NB):
                sp.dma_start(gb[:, n, :], mod_d[n:n + 1, 5 * D:6 * D].to_broadcast([P, D])).then_inc(s_gb, 16)
            for n in range(BASES):
                sp.dma_start(base[:, n, :, :], base_d[n * L:(n + 1) * L, :].rearrange("(i p) d -> p i d", p=P)).then_inc(s_b[n], 16)

        @block.gpsimd
        def _(pool):
            pool.iota(unfilled[:, :], [[P, YR]], base=1 + 2 * NTOK, channel_multiplier=1,
                      allow_small_or_imprecise_dtypes=True).then_inc(s_un, 1)
            pool.wait_ge(s_un, 1)

            def step(j, r, group):
                after(pool, s_car, j + 1 - YR)
                pool.wait_ge(s_ys, j + 1)
                nc.gpsimd.tensor_tensor(spare[:, r:r + 1], unfilled[:, r:r + 1], unfilled[:, r:r + 1], ALU.mult).then_inc(s_car, 1)
                pool.indirect_dma_start(y12_d, bass.IndirectOffsetOnAxis(ap=place[:, r:r + 1], axis=0),
                                        ysb[:, r, :], None).then_inc(s_st[r], 16)

            tiles(pool, step)
            for r in range(YR):
                pool.wait_ge(s_st[r], 16 * (NSLOT // YR))

        @block.scalar
        def _(act):
            def step(j, r, group):
                e = act.value_load(tile_expert[0:1, bass.ds(j, 1)], min_val=0, max_val=E - 1)
                act.wait_ge(s_we, 32 * (e + 1))
                after(act, s_hp, j - 1)
                nc.scalar.activation(w1_now[:, r % 2, :, :], w1_sb[:, bass.ds(e * DC, DC), :], ACT.Copy).then_inc(s_w1, 1)

            tiles(act, step)

        @block.tensor
        def _(pe):
            def transpose_x(j, r, group):
                pe.wait_ge(s_x[r], (group + 1) * 16)
                after(pe, s_xt, j)
                for k in range(DC):
                    last = nc.tensor.transpose(X_PS[:, k, :], xg[:, r, k * P:(k + 1) * P], ident[:, :])
                last.then_inc(s_xtp, 1)

            def first(j, r):
                pe.wait_ge(s_w1, j + 1)
                pe.wait_ge(s_xt, j + 1)
                after(pe, s_ht, j - 1)
                for f in range(FC):
                    for k in range(DC):
                        last = nc.tensor.matmul(H_PS[:, r % 2, f, :],
                                                w1_now[:, r % 2, k, f * P:(f + 1) * P],
                                                xgT[:, r % 2, k, :], start=(k == 0), stop=(k == DC - 1))
                last.then_inc(s_hp, 1)

            def second(j, r, e):
                pe.wait_ge(s_we, 32 * (e + 1))
                pe.wait_ge(s_ht, j + 1)
                after(pe, s_ys, j - 1)
                for k in range(FC):
                    last = nc.tensor.matmul(Y_PS[:, r % 2, :], hT[:, r % 2, k, :],
                                            w2_sb[:, bass.ds(e * FC + k, 1), :].rearrange("p a d -> p (a d)"),
                                            start=(k == 0), stop=(k == FC - 1))
                last.then_inc(s_yp, 1)

            def expert(j):
                return pe.value_load(tile_expert[0:1, bass.ds(j, 1)], min_val=0, max_val=E - 1)

            def turn(group, begins, ends):
                for r in range(TURN):
                    j = group * TURN + r
                    if not (ends and r == TURN - 1):
                        transpose_x(j + 1, (r + 1) % TURN, group if r + 1 < TURN else group + 1)
                    first(j, r)
                    if not (begins and r == 0):
                        second(j - 1, (r - 1) % TURN, expert(j - 1))

            transpose_x(0, 0, 0)
            turn(0, True, False)
            with pe.Fori(1, NSLOT // TURN - 1) as group:
                turn(group, False, False)
            turn(NSLOT // TURN - 1, False, True)
            second(NSLOT - 1, TURN - 1, expert(NSLOT - 1))

        @block.vector
        def _(dve):
            def x_in(j, r, e, group):
                dve.wait_ge(s_xtp, j + 1)
                after(dve, s_st[r], 16 * group)
                nc.vector.scalar_tensor_tensor(filler[:, r:r + 1], xg[:, r, D:D + 1], 0.0, unfilled[:, r:r + 1],
                                               ALU.is_equal, ALU.mult).then_inc(s_fil, 1)
                dve.wait_ge(s_fil, j + 1)
                nc.vector.tensor_tensor(place[:, r:r + 1], filler[:, r:r + 1], xg[:, r, D:D + 1], ALU.add)
                after(dve, s_hp, j - 1)
                for k in range(DC):
                    at = bass.ds(e * DC + k, 1)
                    last = nc.vector.tensor_scalar(xgT[:, r % 2, k, :], X_PS[:, k, :], gam[:, at], bet[:, at], ALU.mult, ALU.add)
                last.then_inc(s_xt, 1)

            def h_in(j, r, e):
                dve.wait_ge(s_hp, j + 1)
                after(dve, s_yp, j - 1)
                for f in range(FC):
                    last = nc.vector.tensor_scalar(hT[:, r % 2, f, :], H_PS[:, r % 2, f, :], b1_sb[:, bass.ds(e * FC + f, 1)], 0.0,
                                                   ALU.add, ALU.max)
                last.then_inc(s_ht, 1)

            def y_in(j, r, e, group):
                dve.wait_ge(s_yp, j + 1)
                nc.vector.tensor_tensor(ysb[:, r, :], Y_PS[:, r % 2, :],
                                        b2_sb[:, bass.ds(e, 1), :].rearrange("p a d -> p (a d)"), ALU.add).then_inc(s_ys, 1)

            def expert(j):
                return dve.value_load(tile_expert[0:1, bass.ds(j, 1)], min_val=0, max_val=E - 1)

            def turn(group, begins, ends):
                for r in range(TURN):
                    j = group * TURN + r
                    if not (ends and r == TURN - 1):
                        x_in(j + 1, (r + 1) % TURN, expert(j + 1), group if r + 1 < TURN else group + 1)
                    h_in(j, r, expert(j))
                    if not (begins and r == 0):
                        y_in(j - 1, (r - 1) % TURN, expert(j - 1), group - 1 if r == 0 else group)

            dve.wait_ge(s_un, 1)
            x_in(0, 0, expert(0), 0)
            turn(0, True, False)
            turn(1, False, False)
            with dve.Fori(2, NSLOT // TURN - 1) as group:
                turn(group, False, False)
            turn(NSLOT // TURN - 1, False, True)
            y_in(NSLOT - 1, TURN - 1, expert(NSLOT - 1), NSLOT // TURN - 1)


def stage_d(nc, sem, wts, base_d, y12_d, out, gb, base, s_gb, s_b):
    with ExitStack() as own:
        def sb(name, shape, dt=F32):
            return own.enter_context(nc.sbuf_tensor(name, shape, dt))

        BUF = BASES
        y12 = sb("y12", [P, BUF, TI, 2, D])
        res = sb("res", [P, BUF, TI, D])
        s_g = [sem(f"y12_loaded{i}") for i in range(BUF)]
        s_link = sem("d_links")
        s_res = sem("res_ready")
        s_out = [sem(f"out_stored{i}") for i in range(BUF)]
        block = own.enter_context(nc.Block())

        def rows(t, n):
            return t[n * L:(n + 1) * L, :].rearrange("(i p) d -> p i d", p=P)

        @block.sync
        def _(sp):
            for n in range(NB):
                if n >= BUF:
                    sp.wait_ge(s_res, n - BUF + 1)
                sp.dma_start(y12[:, n % BUF, :, :, :],
                             y12_d[1 + 2 * L * n:1 + 2 * L * (n + 1), :].rearrange("(i p k) d -> p i k d", p=P, k=2)
                             ).then_inc(s_g[n % BUF], 16)
                if n >= BUF:
                    sp.dma_start(base[:, n % BUF, :, :], rows(base_d, n)).then_inc(s_b[n % BUF], 16)

        @block.vector
        def _(dve):
            steps = [0]

            def link(ins):
                steps[0] += 1
                ins.then_inc(s_link, 1)
                dve.wait_ge(s_link, steps[0])

            dve.wait_ge(s_gb, 16 * NB)
            for n in range(NB):
                b = n % BUF
                dve.wait_ge(s_g[b], 16 * (n // BUF + 1))
                if n >= BUF:
                    dve.wait_ge(s_out[b], 16 * (n // BUF))
                for i in range(TI):
                    t = n * TI + i
                    last = nc.vector.tensor_scalar(res[:, b, i, :], y12[:, b, i, 0, :], wts[:, 0, t:t + 1], None, ALU.mult)
                link(last)
                for i in range(TI):
                    t = n * TI + i
                    last = nc.vector.scalar_tensor_tensor(res[:, b, i, :], y12[:, b, i, 1, :], wts[:, 1, t:t + 1],
                                                          res[:, b, i, :], ALU.mult, ALU.add)
                link(last)
                link(nc.vector.tensor_tensor(res[:, b, :, :], res[:, b, :, :], gb[:, n, :].unsqueeze(1).to_broadcast([P, TI, D]), ALU.mult))
                dve.wait_ge(s_b[b], 16 * (n // BUF + 1))
                nc.vector.tensor_tensor(res[:, b, :, :], res[:, b, :, :], base[:, b, :, :], ALU.add).then_inc(s_res, 1)

        @block.scalar
        def _(act):
            for n in range(NB):
                act.wait_ge(s_res, n + 1)
                act.dma_start(rows(out, n), res[:, n % BUF, :, :]).then_inc(s_out[n % BUF], 16)
            for b in range(BUF):
                act.wait_ge(s_out[b], 16 * (NB // BUF))


def kernel(**inputs):
    import numpy as np
    import concourse.bacc as bacc
    from concourse.bass_utils import run_bass_kernel_spmd

    a = {k: np.asarray(v) for k, v in inputs.items()}

    def columns(v, chunks):
        return v.reshape(-1, chunks, P).transpose(2, 0, 1).reshape(P, -1)

    arrays = {
        "x": a["L0_attn_x"].reshape(NTOK, D),
        "norm_w": columns(a["L0_attn_norm_w"], DC),
        "W_in": a["L0_attn_W_in"],
        "conv_w": a["L0_attn_conv_w"].reshape(CH, P, K).transpose(1, 0, 2),
        "conv_b": columns(a["L0_attn_conv_b"], CH),
        "W_x": a["L0_attn_W_x"],
        "W_dt": a["L0_attn_W_dt"],
        "b_dt": columns(a["L0_attn_b_dt"], CH),
        "A_log": a["L0_attn_A_log"].reshape(CH, P, NS).transpose(1, 0, 2),
        "D_skip": columns(a["L0_attn_D_skip"], CH),
        "W_out": a["L0_attn_W_out"],
        "Wg": a["L0_ffn_Wg"],
        "gamma": columns(a["L0_ffn_gamma"], DC),
        "beta": columns(a["L0_ffn_beta"], DC),
        "W1": a["L0_ffn_W1"],
        "b1": columns(a["L0_ffn_b1"], FC),
        "W2": a["L0_ffn_W2"],
        "b2": a["L0_ffn_b2"].reshape(1, E * D),
        "cT": a["L0_c"].T,
        "wmod": a["L0_wmod"],
    }
    arrays = {f"in_{k}": np.ascontiguousarray(v) for k, v in arrays.items()}
    nc = bacc.Bacc("TRN2", target_bir_lowering=False, num_devices=1)
    args = {k[3:]: nc.dram_tensor(k, v.shape, mybir.dt.from_np(v.dtype), kind="ExternalInput").ap()
            for k, v in arrays.items()}
    out = nc.dram_tensor("out", (NTOK, D), F32, kind="ExternalOutput").ap()
    adaln_kernel(nc, **args, out=out)
    r = run_bass_kernel_spmd(nc, [arrays], core_ids=[0])
    return r.results[0]["out"].reshape(NB, L, D)
```
